# Optimizing a Trainium2 kernel written in Bass

```python
import numpy as np
import jax
import jax.numpy as jnp

def _softmax(x, axis=-1):
    return jax.nn.softmax(x, axis=axis)

def _gelu(x):
    return jax.nn.gelu(x, approximate=True)

def _silu(x):
    return jax.nn.silu(x)

def _sigmoid(x):
    return jax.nn.sigmoid(x)

def _layernorm(x, axis=-1, eps=1e-05):
    m = jnp.mean(x, axis=axis, keepdims=True)
    v = jnp.var(x, axis=axis, keepdims=True)
    return (x - m) / jnp.sqrt(v + eps)

def _scatter_add(tgt, idx, src, axis=0):
    return tgt.at[idx].add(src)

def _segment_sum(src, seg, n):
    return jax.ops.segment_sum(src, seg, n)
kernel_name = 'mk_lm_tower_d1_tok_ids768_r4_e3adf7'

def setup_inputs(seed: int=0):
    np.random.seed(seed)
    _w = jnp.asarray

    def _rec_inputs():
        import jax
        import jax.numpy as jnp
        _rk = jax.random.key(seed)
        x = jax.random.randint(jax.random.fold_in(_rk, 1), (32, 128), 0, 30522, jnp.int32)
        itok_BS_0_4999 = jax.random.randint(jax.random.fold_in(_rk, 21), (32, 128), 0, 1250, jnp.int32)
        mask_BS_i0_1 = jnp.where(jnp.ones((32, 128), dtype=bool), 0, 1).astype(jnp.int32)
        pos_BS = jnp.broadcast_to(jnp.arange(128, dtype=jnp.int32), (32, 128))
        return (x, itok_BS_0_4999, mask_BS_i0_1, pos_BS)
    x, itok_BS_0_4999, mask_BS_i0_1, pos_BS = _rec_inputs()

    def _L0_tok_setup():
        import jax, jax.numpy as jnp
        import numpy as np
        VOCAB = 30522
        HIDDEN = 192
        MAX_POS = 128
        TYPE_VOCAB = 2
        DOMAIN_VOCAB = 1250
        DOMAIN_DIM = 128
        EPS = 1e-12
        B, S = (64, 128)
        key = jax.random.key(seed)
        ks = jax.random.split(key, 10)
        input_ids = jax.random.randint(ks[0], (B, S), 0, VOCAB)
        domain_ids = jax.random.randint(ks[1], (B, S), 0, DOMAIN_VOCAB)
        token_type_ids = jax.random.randint(ks[2], (B, S), 0, TYPE_VOCAB)
        position_ids = jnp.broadcast_to(jnp.arange(S, dtype=jnp.int64 if jax.config.jax_enable_x64 else jnp.int32), (B, S))
        word_table = jax.random.normal(ks[3], (VOCAB, HIDDEN), dtype=jnp.float32) * 0.02
        word_table = word_table.at[0].set(0.0)
        domain_table = jax.random.normal(ks[4], (DOMAIN_VOCAB, DOMAIN_DIM), dtype=jnp.float32) * 0.02
        pos_table = jax.random.normal(ks[5], (MAX_POS, HIDDEN), dtype=jnp.float32) * 0.02
        type_table = jax.random.normal(ks[6], (TYPE_VOCAB, HIDDEN), dtype=jnp.float32) * 0.02
        proj_w = jax.random.normal(ks[7], (HIDDEN, DOMAIN_DIM), dtype=jnp.float32) * (1.0 / np.sqrt(DOMAIN_DIM))
        proj_b = jnp.zeros((HIDDEN,), dtype=jnp.float32)
        ln_gamma = jnp.ones((HIDDEN,), dtype=jnp.float32)
        ln_beta = jnp.zeros((HIDDEN,), dtype=jnp.float32)
        return {'input_ids': input_ids, 'domain_ids': domain_ids, 'token_type_ids': token_type_ids, 'position_ids': position_ids, 'word_table': word_table, 'domain_table': domain_table, 'pos_table': pos_table, 'type_table': type_table, 'proj_w': proj_w, 'proj_b': proj_b, 'ln_gamma': ln_gamma, 'ln_beta': ln_beta}
    _L0_tok_all = _L0_tok_setup()
    _L0_tok_in = {k: v for k, v in _L0_tok_all.items() if k in ('word_table', 'domain_table', 'pos_table', 'type_table', 'proj_w', 'proj_b', 'ln_gamma', 'ln_beta')}
    del _L0_tok_all

    def _L0_attn_setup():
        import jax, jax.numpy as jnp
        import numpy as np
        H = 12

        def _heads(x, B, S):
            return x.reshape(B, S, H, -1).transpose(0, 2, 1, 3)
        key = jax.random.key(seed)
        ks = jax.random.split(key, 6)
        B, S, D = (2, 512, 192)
        sc = 0.02
        return {'hidden_states': jax.random.normal(ks[0], (B, S, D), jnp.float32), 'Wqr': jax.random.normal(ks[1], (D, D), jnp.float32) * sc, 'Wqi': jax.random.normal(ks[2], (D, D), jnp.float32) * sc, 'Wkr': jax.random.normal(ks[3], (D, D), jnp.float32) * sc, 'Wki': jax.random.normal(ks[4], (D, D), jnp.float32) * sc, 'Wv': jax.random.normal(ks[5], (D, D), jnp.float32) * sc}
    _L0_attn_all = _L0_attn_setup()
    _L0_attn_in = {k: v for k, v in _L0_attn_all.items() if k in ('Wqr', 'Wqi', 'Wkr', 'Wki', 'Wv')}
    del _L0_attn_all

    def _L0_ffn_setup():
        import math
        import jax, jax.numpy as jnp
        import numpy as np
        N_HEAD = 12
        N_EXP = 8
        TOP_K = 2
        TRAIN_CAPACITY = 1.25
        MIN_CAPACITY = 4
        LN_EPS = 1e-05
        NEG_INF = -1e+30

        def _layer_norm(x, w, b):
            mu = jnp.mean(x, axis=-1, keepdims=True)
            var = jnp.var(x, axis=-1, keepdims=True)
            return (x - mu) * jax.lax.rsqrt(var + LN_EPS) * w + b

        def _attention(x, qkv_w, qkv_b, proj_w, proj_b):
            B, T, C = x.shape
            H, D = (N_HEAD, C // N_HEAD)
            qkv = x @ qkv_w + qkv_b
            q, k, v = jnp.split(qkv, 3, axis=-1)
            q = q.reshape(B, T, H, D).transpose(0, 2, 1, 3)
            k = k.reshape(B, T, H, D).transpose(0, 2, 1, 3)
            v = v.reshape(B, T, H, D).transpose(0, 2, 1, 3)
            scores = jnp.einsum('bhqd,bhkd->bhqk', q, k) / math.sqrt(D)
            causal = jnp.tril(jnp.ones((T, T), bool))
            scores = jnp.where(causal, scores, NEG_INF)
            attn = jax.nn.softmax(scores, axis=-1)
            y = jnp.einsum('bhqk,bhkd->bhqd', attn, v)
            y = y.transpose(0, 2, 1, 3).reshape(B, T, C)
            return y @ proj_w + proj_b

        def _moe(x, w_g, fc_w, fc_b, pj_w, pj_b):
            B, T, C = x.shape
            N, E, K = (B * T, N_EXP, TOP_K)
            cap = int(math.floor(K * TRAIN_CAPACITY * N / E))
            cap += cap % 2
            cap = max(cap, MIN_CAPACITY)
            logits = (x @ w_g).reshape(N, E)
            _, topk_idx = jax.lax.top_k(logits, K)
            hot = jax.nn.one_hot(topk_idx, E, dtype=jnp.int32)
            sel = hot.sum(axis=1) > 0
            router_probs = jax.nn.softmax(jnp.where(sel, logits, NEG_INF), axis=-1)
            exp_mask = hot.transpose(1, 0, 2)
            exp_rank = jnp.cumsum(exp_mask.reshape(K * N, E), axis=0) - 1
            exp_rank = exp_rank.reshape(K, N, E)
            exp_mask = exp_mask * (exp_rank < cap).astype(jnp.int32)
            exp_rank = jnp.sum(exp_mask * exp_rank, axis=-1)
            exp_weights = exp_mask.astype(x.dtype) * router_probs[None]
            rank_sc = jax.nn.one_hot(exp_rank, cap, dtype=x.dtype)
            cb_weight = jnp.einsum('kne,knc->nec', exp_weights, rank_sc)
            sec_mask = (cb_weight != 0).astype(x.dtype)
            xf = x.reshape(N, C)
            xb = jnp.einsum('nec,nd->ecd', sec_mask, xf)
            h = jax.nn.gelu(jnp.einsum('ecd,edf->ecf', xb, fc_w) + fc_b, approximate=False)
            out = jnp.einsum('ecf,efd->ecd', h, pj_w) + pj_b
            y = jnp.einsum('nec,ecd->nd', cb_weight, out)
            return y.reshape(B, T, C)
        key = jax.random.key(seed)
        ks = jax.random.split(key, 12)
        B, T, C = (4, 256, 192)
        E, F = (N_EXP, 4 * C)
        s = 0.02
        return {'x': jax.random.normal(ks[0], (B, T, C), jnp.float32), 'ln1_w': jnp.ones((C,), jnp.float32), 'ln1_b': jnp.zeros((C,), jnp.float32), 'ln2_w': jnp.ones((C,), jnp.float32), 'ln2_b': jnp.zeros((C,), jnp.float32), 'attn_qkv_w': jax.random.normal(ks[1], (C, 3 * C), jnp.float32) * s, 'attn_qkv_b': jnp.zeros((3 * C,), jnp.float32), 'attn_proj_w': jax.random.normal(ks[2], (C, C), jnp.float32) * s, 'attn_proj_b': jnp.zeros((C,), jnp.float32), 'w_g': jax.random.normal(ks[3], (C, E), jnp.float32) * s, 'exp_fc_w': jax.random.normal(ks[4], (E, C, F), jnp.float32) * s, 'exp_fc_b': jnp.zeros((E, 1, F), jnp.float32), 'exp_proj_w': jax.random.normal(ks[5], (E, F, C), jnp.float32) * s, 'exp_proj_b': jnp.zeros((E, 1, C), jnp.float32)}
    _L0_ffn_all = _L0_ffn_setup()
    _L0_ffn_in = {k: v for k, v in _L0_ffn_all.items() if k in ('ln1_w', 'ln1_b', 'ln2_w', 'ln2_b', 'attn_qkv_w', 'attn_qkv_b', 'attn_proj_w', 'attn_proj_b', 'w_g', 'exp_fc_w', 'exp_fc_b', 'exp_proj_w', 'exp_proj_b')}
    del _L0_ffn_all
    return {'x': x, 'itok_BS_0_4999': itok_BS_0_4999, 'mask_BS_i0_1': mask_BS_i0_1, 'pos_BS': pos_BS, 'L0_tok_word_table': _L0_tok_in['word_table'], 'L0_tok_domain_table': _L0_tok_in['domain_table'], 'L0_tok_pos_table': _L0_tok_in['pos_table'], 'L0_tok_type_table': _L0_tok_in['type_table'], 'L0_tok_proj_w': _L0_tok_in['proj_w'], 'L0_tok_proj_b': _L0_tok_in['proj_b'], 'L0_tok_ln_gamma': _L0_tok_in['ln_gamma'], 'L0_tok_ln_beta': _L0_tok_in['ln_beta'], 'L0_attn_Wqr': _L0_attn_in['Wqr'], 'L0_attn_Wqi': _L0_attn_in['Wqi'], 'L0_attn_Wkr': _L0_attn_in['Wkr'], 'L0_attn_Wki': _L0_attn_in['Wki'], 'L0_attn_Wv': _L0_attn_in['Wv'], 'L0_ffn_ln1_w': _L0_ffn_in['ln1_w'], 'L0_ffn_ln1_b': _L0_ffn_in['ln1_b'], 'L0_ffn_ln2_w': _L0_ffn_in['ln2_w'], 'L0_ffn_ln2_b': _L0_ffn_in['ln2_b'], 'L0_ffn_attn_qkv_w': _L0_ffn_in['attn_qkv_w'], 'L0_ffn_attn_qkv_b': _L0_ffn_in['attn_qkv_b'], 'L0_ffn_attn_proj_w': _L0_ffn_in['attn_proj_w'], 'L0_ffn_attn_proj_b': _L0_ffn_in['attn_proj_b'], 'L0_ffn_w_g': _L0_ffn_in['w_g'], 'L0_ffn_exp_fc_w': _L0_ffn_in['exp_fc_w'], 'L0_ffn_exp_fc_b': _L0_ffn_in['exp_fc_b'], 'L0_ffn_exp_proj_w': _L0_ffn_in['exp_proj_w'], 'L0_ffn_exp_proj_b': _L0_ffn_in['exp_proj_b']}

def reference(x, itok_BS_0_4999, mask_BS_i0_1, pos_BS, L0_tok_word_table, L0_tok_domain_table, L0_tok_pos_table, L0_tok_type_table, L0_tok_proj_w, L0_tok_proj_b, L0_tok_ln_gamma, L0_tok_ln_beta, L0_attn_Wqr, L0_attn_Wqi, L0_attn_Wkr, L0_attn_Wki, L0_attn_Wv, L0_ffn_ln1_w, L0_ffn_ln1_b, L0_ffn_ln2_w, L0_ffn_ln2_b, L0_ffn_attn_qkv_w, L0_ffn_attn_qkv_b, L0_ffn_attn_proj_w, L0_ffn_attn_proj_b, L0_ffn_w_g, L0_ffn_exp_fc_w, L0_ffn_exp_fc_b, L0_ffn_exp_proj_w, L0_ffn_exp_proj_b):
    import jax
    import jax.numpy as jnp

    def _L0_tok_ref(input_ids, domain_ids, token_type_ids, position_ids, word_table, domain_table, pos_table, type_table, proj_w, proj_b, ln_gamma, ln_beta):
        import jax, jax.numpy as jnp
        import numpy as np
        VOCAB = 30522
        HIDDEN = 192
        MAX_POS = 128
        TYPE_VOCAB = 2
        DOMAIN_VOCAB = 1250
        DOMAIN_DIM = 128
        EPS = 1e-12
        B, S = (64, 128)
        words = word_table[input_ids]
        domain = domain_table[domain_ids]
        types = type_table[token_type_ids]
        pos = pos_table[position_ids]
        domain_proj = jnp.einsum('bsd,hd->bsh', domain, proj_w) + proj_b
        emb = words + domain_proj + types + pos
        mean = jnp.mean(emb, axis=-1, keepdims=True)
        var = jnp.mean(jnp.square(emb - mean), axis=-1, keepdims=True)
        out = (emb - mean) / jnp.sqrt(var + EPS) * ln_gamma + ln_beta
        return out

    def _L0_attn_ref(hidden_states, Wqr, Wqi, Wkr, Wki, Wv):
        import jax, jax.numpy as jnp
        import numpy as np
        H = 12

        def _heads(x, B, S):
            return x.reshape(B, S, H, -1).transpose(0, 2, 1, 3)
        B, S, D = hidden_states.shape
        Dh = D // H
        x = hidden_states
        qr = _heads(x @ Wqr.T, B, S)
        qi = _heads(x @ Wqi.T, B, S)
        kr = _heads(x @ Wkr.T, B, S)
        ki = _heads(x @ Wki.T, B, S)
        v = _heads(x @ Wv.T, B, S)
        scale = 1.0 / jnp.sqrt(jnp.float32(Dh))
        sr = (jnp.einsum('bhqd,bhkd->bhqk', qr, kr) + jnp.einsum('bhqd,bhkd->bhqk', qi, ki)) * scale
        si = (jnp.einsum('bhqd,bhkd->bhqk', qi, kr) - jnp.einsum('bhqd,bhkd->bhqk', qr, ki)) * scale
        scores = jnp.sqrt(sr * sr + si * si)
        probs = jax.nn.softmax(scores, axis=-1)
        ctx = jnp.einsum('bhqk,bhkd->bhqd', probs, v)
        return ctx.transpose(0, 2, 1, 3).reshape(B, S, D)

    def _L0_ffn_ref(x, ln1_w, ln1_b, ln2_w, ln2_b, attn_qkv_w, attn_qkv_b, attn_proj_w, attn_proj_b, w_g, exp_fc_w, exp_fc_b, exp_proj_w, exp_proj_b):
        import math
        import jax, jax.numpy as jnp
        import numpy as np
        N_HEAD = 12
        N_EXP = 8
        TOP_K = 2
        TRAIN_CAPACITY = 1.25
        MIN_CAPACITY = 4
        LN_EPS = 1e-05
        NEG_INF = -1e+30

        def _layer_norm(x, w, b):
            mu = jnp.mean(x, axis=-1, keepdims=True)
            var = jnp.var(x, axis=-1, keepdims=True)
            return (x - mu) * jax.lax.rsqrt(var + LN_EPS) * w + b

        def _attention(x, qkv_w, qkv_b, proj_w, proj_b):
            B, T, C = x.shape
            H, D = (N_HEAD, C // N_HEAD)
            qkv = x @ qkv_w + qkv_b
            q, k, v = jnp.split(qkv, 3, axis=-1)
            q = q.reshape(B, T, H, D).transpose(0, 2, 1, 3)
            k = k.reshape(B, T, H, D).transpose(0, 2, 1, 3)
            v = v.reshape(B, T, H, D).transpose(0, 2, 1, 3)
            scores = jnp.einsum('bhqd,bhkd->bhqk', q, k) / math.sqrt(D)
            causal = jnp.tril(jnp.ones((T, T), bool))
            scores = jnp.where(causal, scores, NEG_INF)
            attn = jax.nn.softmax(scores, axis=-1)
            y = jnp.einsum('bhqk,bhkd->bhqd', attn, v)
            y = y.transpose(0, 2, 1, 3).reshape(B, T, C)
            return y @ proj_w + proj_b

        def _moe(x, w_g, fc_w, fc_b, pj_w, pj_b):
            B, T, C = x.shape
            N, E, K = (B * T, N_EXP, TOP_K)
            cap = int(math.floor(K * TRAIN_CAPACITY * N / E))
            cap += cap % 2
            cap = max(cap, MIN_CAPACITY)
            logits = (x @ w_g).reshape(N, E)
            _, topk_idx = jax.lax.top_k(logits, K)
            hot = jax.nn.one_hot(topk_idx, E, dtype=jnp.int32)
            sel = hot.sum(axis=1) > 0
            router_probs = jax.nn.softmax(jnp.where(sel, logits, NEG_INF), axis=-1)
            exp_mask = hot.transpose(1, 0, 2)
            exp_rank = jnp.cumsum(exp_mask.reshape(K * N, E), axis=0) - 1
            exp_rank = exp_rank.reshape(K, N, E)
            exp_mask = exp_mask * (exp_rank < cap).astype(jnp.int32)
            exp_rank = jnp.sum(exp_mask * exp_rank, axis=-1)
            exp_weights = exp_mask.astype(x.dtype) * router_probs[None]
            rank_sc = jax.nn.one_hot(exp_rank, cap, dtype=x.dtype)
            cb_weight = jnp.einsum('kne,knc->nec', exp_weights, rank_sc)
            sec_mask = (cb_weight != 0).astype(x.dtype)
            xf = x.reshape(N, C)
            xb = jnp.einsum('nec,nd->ecd', sec_mask, xf)
            h = jax.nn.gelu(jnp.einsum('ecd,edf->ecf', xb, fc_w) + fc_b, approximate=False)
            out = jnp.einsum('ecf,efd->ecd', h, pj_w) + pj_b
            y = jnp.einsum('nec,ecd->nd', cb_weight, out)
            return y.reshape(B, T, C)
        x = x + _attention(_layer_norm(x, ln1_w, ln1_b), attn_qkv_w, attn_qkv_b, attn_proj_w, attn_proj_b)
        x = x + _moe(_layer_norm(x, ln2_w, ln2_b), w_g, exp_fc_w, exp_fc_b, exp_proj_w, exp_proj_b)
        return x
    h = _L0_tok_ref(x, itok_BS_0_4999, mask_BS_i0_1, pos_BS, L0_tok_word_table, L0_tok_domain_table, L0_tok_pos_table, L0_tok_type_table, L0_tok_proj_w, L0_tok_proj_b, L0_tok_ln_gamma, L0_tok_ln_beta)
    h = h + _L0_attn_ref(_layernorm(h, axis=-1), L0_attn_Wqr, L0_attn_Wqi, L0_attn_Wkr, L0_attn_Wki, L0_attn_Wv)
    h = h + _L0_ffn_ref(_layernorm(h, axis=-1), L0_ffn_ln1_w, L0_ffn_ln1_b, L0_ffn_ln2_w, L0_ffn_ln2_b, L0_ffn_attn_qkv_w, L0_ffn_attn_qkv_b, L0_ffn_attn_proj_w, L0_ffn_attn_proj_b, L0_ffn_w_g, L0_ffn_exp_fc_w, L0_ffn_exp_fc_b, L0_ffn_exp_proj_w, L0_ffn_exp_proj_b)
    return h

_drawn_inputs = setup_inputs


def setup_inputs(seed=0):
    import zlib

    import numpy as np

    out = dict(_drawn_inputs(seed))
    spreads = {'L0_tok_proj_b': (0.0, 0.1),
     'L0_tok_ln_gamma': (1.0, 0.2),
     'L0_tok_ln_beta': (0.0, 0.1),
     'L0_ffn_ln1_w': (1.0, 0.6),
     'L0_ffn_ln1_b': (0.0, 0.8),
     'L0_ffn_ln2_w': (1.0, 0.6),
     'L0_ffn_ln2_b': (0.0, 0.442),
     'L0_ffn_attn_qkv_b': (0.0, 0.561),
     'L0_ffn_attn_proj_b': (0.0, 0.1),
     'L0_ffn_exp_fc_b': (0.0, 0.8),
     'L0_ffn_exp_proj_b': (0.0, 0.374)}
    factors = {'L0_attn_Wqr': 8.0,
     'L0_attn_Wqi': 8.0,
     'L0_attn_Wkr': 8.0,
     'L0_attn_Wki': 8.0,
     'L0_ffn_exp_fc_w': 3.227,
     'L0_ffn_exp_proj_w': 2.929}
    for name, (base, spread) in spreads.items():
        noise = np.random.default_rng([zlib.crc32(name.encode()), seed]).standard_normal(out[name].shape)
        drawn = base * np.exp(spread * noise) if base else spread * noise
        out[name] = jnp.asarray(drawn.astype(out[name].dtype))
    for name, factor in factors.items():
        out[name] = (out[name] * factor).astype(out[name].dtype)
    return out
```

```python
from contextlib import ExitStack

import concourse.bass as bass
from concourse import mybir

F32 = mybir.dt.float32
F32R = mybir.dt.float32r
BF16 = mybir.dt.bfloat16
I32 = mybir.dt.int32
U32 = mybir.dt.uint32
ALU = mybir.AluOpType
ACT = mybir.ActivationFunctionType
AX = mybir.AxisListType

SEQS, SEQ, HID = 32, 128, 192
REST = HID - 128
TOKENS = SEQS * SEQ
HEADS, HEAD_DIM = 12, 16
GROUP = 4
GROUPS = SEQS // GROUP
BLOCKS = 3
JOBS = GROUP * BLOCKS
EXPERTS, TOPK, FF = 8, 2, 768
FF_CHUNKS = FF // 128
CAP = (TOPK * 5 * TOKENS) // (4 * EXPERTS)
CAP += CAP % 2
SLOTS = EXPERTS * CAP
CAP_TILES = CAP // 128
CHUNKS = [(0, 4), (4, 4), (8, 2)]
MASKED = -1.0e30
WORD_EPS, LN_EPS = 1e-12, 1e-5


PASS_SLOTS = 24
RING = 3


def back_turns(slot):
    fills = [("probT", slot)] if slot < JOBS else []
    if slot >= 4 and (slot - 4) % 3 == 0 and (slot - 4) // 3 < GROUP:
        fills += [("ctx", (slot - 4) // 3)]
    return fills


def back_fills_causal(slot):
    fills = back_turns(slot)
    for s in range(GROUP):
        fills += [("ctxT", s)] if slot == 3 * s + 5 else []
        fills += [("out", s)] if slot == 3 * s + 6 else []
        fills += [("zT", s)] if slot == 3 * s + 9 else []
    fills += [("logits", 0)] if slot == 20 else []
    fills += [("logitsT", 0)] if slot == 21 else []
    return fills


def front_fills_magnitude(slot):
    fills = [("xT", 0), ("xT", 1)] if slot == 0 else []
    fills += [("proj", slot - 1)] if 1 <= slot <= 9 else []
    fills += [("value", slot - 14)] if 14 <= slot <= 15 else []
    return fills


def front_fills_causal(slot):
    fills = [("xT", 0), ("xT", 1)] if slot == 0 else []
    fills += [("proj", slot - 1)] if 1 <= slot <= 6 else []
    fills += [("value", slot - 14)] if 14 <= slot <= 17 else []
    return fills


def prep_fills_embedding(slot):
    fills = [("domT", slot - 13)] if 13 <= slot <= 14 else []
    fills += [("embed", slot - 16)] if 16 <= slot <= 17 else []
    return fills


def no_fills(slot):
    return []


class Phase:

    def __init__(self, sem, name, front, back, prep, values_per_fill):
        self.front, self.back, self.prep, self.values_per_fill = front, back, prep, values_per_fill
        self.lead = [f for k in range(PASS_SLOTS) for f in prep(k)]
        n = lambda fills: sum(len(fills(k)) for k in range(PASS_SLOTS))
        self.per_pass = n(front) + n(back) + n(prep)
        assert self.per_pass % RING == 0
        self.before_loop = len(self.lead) + n(front) + n(prep)
        self.before_tail = self.before_loop + self.per_pass * (GROUPS - 1) - n(prep)
        self.total = self.before_tail + n(back)
        self.ring_full = [sem(f"{name}_ring_full{i}") for i in range(RING)]
        self.ring_free = [sem(f"{name}_ring_free{i}") for i in range(RING)]
        self.high_done = sem(f"{name}_high_done")
        self.scores_full = sem(f"{name}_scores_full")
        self.scores_free = sem(f"{name}_scores_free")
        self.max_done = sem(f"{name}_max_done")
        self.root_done = sem(f"{name}_root_done")
        self.neg_max_done = sem(f"{name}_neg_max_done")
        self.exp_done = sem(f"{name}_exp_done")
        self.pv_done = sem(f"{name}_pv_done")
        self.ctx_copied = sem(f"{name}_ctx_copied")
        self.recip_done = sem(f"{name}_recip_done")
        self.ctx_done = sem(f"{name}_ctx_done")
        self.x_ready = sem(f"{name}_x_ready")
        self.step = {}
        self.sem, self.name = sem, name

    def named(self, what):
        if what not in self.step:
            self.step[what] = self.sem(f"{self.name}_{what}")
        return self.step[what]

    def schedule(self, g, front, back, prep):
        by_slot = [(self.back(k) if back else []) + (self.front(k) if front else [])
                   + (self.prep(k) if prep else []) for k in range(PASS_SLOTS)]
        fills = [f for some in by_slot for f in some]
        if isinstance(g, int):
            first = (len(self.lead) if g == 0 else self.before_tail if g == GROUPS
                     else self.before_loop + self.per_pass * (g - 1))
            return by_slot, {f: ((first + k) % RING, (first + k) // RING) for k, f in enumerate(fills)}
        first = self.before_loop
        return by_slot, {f: ((first + k) % RING, (g - 1) * (self.per_pass // RING) + (first + k) // RING)
                         for k, f in enumerate(fills)}

    def lead_places(self):
        return {f: (k % RING, k // RING) for k, f in enumerate(self.lead)}


def tower_kernel(nc, ids, kinds, word_table, domain_table, pos_table, kind_rows, domain_w, mag_qk, mag_v,
                 causal_qk, causal_qk_b, causal_v, ln_cols, rows, out_w, gate_w, fc_w, fc_b, pj_w, pj_b, out):
    ctx = ExitStack()
    with ctx:
        def sb(name, shape, dt=F32):
            return ctx.enter_context(nc.sbuf_tensor(name, shape, dt))

        def pb(name, shape):
            return ctx.enter_context(nc.psum_tensor(name, shape, F32))

        def sem(name):
            return ctx.enter_context(nc.semaphore(name))

        slot_in = nc.dram_tensor("slot_in", [SLOTS, HID], F32, kind="Internal").ap()
        slot_out = nc.dram_tensor("slot_out", [SLOTS, HID], F32, kind="Internal").ap()

        ps_scores = pb("ps_scores", [128, 4, 512])
        ps_ctx = pb("ps_ctx", [128, 512])
        ps_ring = pb("ps_ring", [128, RING, 512])

        resid = sb("resid", [128, SEQS, HID])
        xin = sb("xin", [128, SEQS, HID])
        logits = sb("logits", [128, SEQS, EXPERTS])
        ident = sb("ident", [128, 128])
        causal = sb("causal", [128, 128])
        zeros = sb("zeros", [128, HID])
        row_c = sb("row_c", [128, 4, HID])
        ln_c = sb("ln_c", [128, 8])
        half = sb("half", [128, GROUP])
        w_hi = sb("w_hi", [128, 2, 3, 384], F32R)
        w_lo = sb("w_lo", [128, 2, 3, 384], F32R)
        v_hi = sb("v_hi", [128, 2, HID], F32R)
        v_lo = sb("v_lo", [128, 2, HID], F32R)
        qk_b = sb("qk_b", [128, 6])
        xn = sb("xn", [128, GROUP, 256])
        x_hi = sb("x_hi", [128, 2, GROUP * 128], F32R)
        x_lo = sb("x_lo", [128, GROUP * 128], F32R)
        q_hi = sb("q_hi", [128, BLOCKS, GROUP, 128], F32R)
        q_lo = sb("q_lo", [128, BLOCKS, GROUP, 128], F32R)
        k_hi = sb("k_hi", [128, BLOCKS, GROUP, 2, 128], F32R)
        k_lo = sb("k_lo", [128, BLOCKS, GROUP, 2, 128], F32R)
        vals = sb("vals", [128, GROUP, HEADS, 32])
        square = sb("square", [128, 2, 4, 2, 128])
        probs = sb("probs", [128, JOBS, 4, 128])
        row_max = sb("row_max", [128, GROUP, HEADS])
        row_root = sb("row_root", [128, GROUP, HEADS])
        neg_max = sb("neg_max", [128, GROUP, HEADS])
        prob_t = sb("prob_t", [128, 2, 4, 128])
        ctx_t = sb("ctx_t", [128, BLOCKS, 128])
        recip = sb("recip", [128, HEADS])
        ctx_n = sb("ctx_n", [128, 256])
        id_all = sb("id_all", [128, 3, SEQS], I32)
        id_now = sb("id_now", [128, 3, GROUP], I32)
        work = sb("work", [128, 4096])
        kind_i = work[0:2, 0:TOKENS].bitcast(I32)
        kind_sc = sb("kind_sc", [2, 2])
        kind_w = sb("kind_w", [3, HID])
        dom_w = sb("dom_w", [128, HID])
        got = sb("got", [128, GROUP * (HID + 128 + HID)])
        got_word = got[:, 0:GROUP * HID].rearrange("p (s d) -> p s d", s=GROUP)
        got_pos = got[:, GROUP * HID:2 * GROUP * HID].rearrange("p (s d) -> p s d", s=GROUP)
        got_dom = got[:, 2 * GROUP * HID:].rearrange("p (s d) -> p s d", s=GROUP)
        stats = sb("stats", [128, GROUP, 6])
        moments = sb("moments", [128, GROUP, 2])
        rstd = sb("rstd", [128, 6, GROUP])
        o_w = sb("o_w", [128, 2, HID])
        g_w = sb("g_w", [128, 2, EXPERTS])
        z = sb("z", [128, 2, HID])
        z_t = sb("z_t", [128, 2, GROUP * 128])
        dom_t = z_t[:, 0, :].rearrange("p (s t) -> p s t", s=GROUP)
        kind_hot = z_t[0:3, 1, :]
        gate_t = work[0:EXPERTS, 1536:2048]
        ctxn_t = work[:, 2048:2304].rearrange("p (c t) -> p c t", c=2)
        out_b = work[:, 2304:2304 + HID]
        x_full = sb("x_full", [128, 2, 256])
        z_stats = sb("z_stats", [128, 6])
        z_moments = sb("z_moments", [128, 2])
        number_e = sb("number_e", [128, EXPERTS])
        below = sb("below", [128, 128], BF16)
        ones_b = sb("ones_b", [128, 128], BF16)
        one_f = sb("one_f", [128, TOPK * SEQS])
        scratch = work[:, 0:1536].rearrange("p (a n) -> p a n", n=256)
        best = scratch[:, 0, :].rearrange("p (t e) -> p t e", e=8)
        best_at = scratch[:, 1, :].bitcast(U32).rearrange("p (t e) -> p t e", e=8)
        choice = sb("choice", [128, TOPK, SEQS])
        hot = scratch[:, 2, :].bitcast(BF16).rearrange("p (t e) -> p t e", e=EXPERTS)
        rank_e = work[:, 768:1280].rearrange("p (t e) -> p t e", e=EXPERTS)
        rank = sb("rank", [128, TOPK, SEQS])
        keep = sb("keep", [128, TOPK, SEQS])
        slot_f = work[:, 1280:1472].rearrange("p (a n) -> p a n", a=3)
        put_at = sb("put_at", [128, TOPK * SEQS], I32)
        take_at = sb("take_at", [128, TOPK * SEQS], I32)
        weight = sb("weight", [128, TOPK, SEQS])
        gap = sb("gap", [128, 3, SEQS])
        fc_bias = sb("fc_bias", [128, EXPERTS, FF_CHUNKS])

        mag = Phase(sem, "mag", front_fills_magnitude, back_turns, prep_fills_embedding, 2)
        cau = Phase(sem, "cau", front_fills_causal, back_fills_causal, no_fills, 1)

        const_loaded = sem("const_loaded")
        const_made = sem("const_made")
        ident_ready = sem("ident_ready")
        wait_ended = sem("wait_ended")
        mag_w_loaded = sem("mag_w_loaded")
        mag_w_high = sem("mag_w_high")
        mag_w_split = sem("mag_w_split")
        cau_w_loaded = sem("cau_w_loaded")
        cau_w_high = sem("cau_w_high")
        cau_w_split = sem("cau_w_split")
        zero_filled = sem("zero_filled")
        id_copied = sem("id_copied")
        word_got = sem("word_got")
        dom_got = sem("dom_got")
        pos_got = sem("pos_got")
        gather_used = sem("gather_used")
        logits_ready = sem("logits_ready")
        z_ready = sem("z_ready")
        z_kept = sem("z_kept")
        z_used = sem("z_used")
        raw = probs[:, :, :, :].rearrange("p j h k -> p (j h k)")
        raw_qk = raw[:, 0:2304].rearrange("p (c m n) -> p c m n", c=2, m=3)
        raw_v = raw[:, 2304:2304 + 384].rearrange("p (c n) -> p c n", c=2)
        raw_fc = work[:, 0:2 * FF].rearrange("p (c n) -> p c n", c=2)
        pj_w_sb = work[:, 2 * FF:2 * FF + 2 * FF_CHUNKS * HID].rearrange("p (u c n) -> p u c n", u=2, c=FF_CHUNKS)
        pj_bias = got[:, 0:EXPERTS * HID].rearrange("p (e n) -> p e n", e=EXPERTS)
        slot_x = [square[:, i, :, :, :].rearrange("p h m k -> p h (m k)") for i in range(2)] + [xn[:, 0:2, :]]
        hidden = raw.rearrange("p (u f t) -> p u f t", u=2, f=FF_CHUNKS)
        OUT_RING = 5
        slot_y = z_t[:, :, :].rearrange("p c t -> p (c t)")[:, 0:OUT_RING * HID].rearrange(
            "p (t d) -> p t d", t=OUT_RING)
        TAKE_RING = 16
        taken = raw.rearrange("p (r k d) -> p r k d", r=TAKE_RING, k=TOPK)

        ps_x = [ps_ring[:, 2, :], ps_ctx[:, :]]

        route = sem("route")
        hot_ready = sem("hot_ready")
        ranked = sem("ranked")
        gap_ready = sem("gap_ready")
        gap_exp = sem("gap_exp")
        put_ready = sem("put_ready")
        slots_put = sem("slots_put")
        bias_loaded = sem("bias_loaded")
        raw_loaded = sem("raw_loaded")
        raw_split = sem("raw_split")
        fc_high = sem("fc_high")
        pj_loaded = [sem(f"pj_loaded{u}") for u in range(2)]
        pj_used = [sem(f"pj_used{u}") for u in range(2)]
        x_loaded = [sem(f"x_loaded{c}") for c in range(3)]
        x_turned = [sem(f"x_turned{c}") for c in range(3)]
        fc_used = sem("fc_used")
        ex_turn_full = [sem(f"ex_turn_full{i}") for i in range(2)]
        ex_turn_free = [sem(f"ex_turn_free{i}") for i in range(2)]
        ex_whole = sem("ex_whole")
        ex_high = sem("ex_high")
        FC_RING = 3
        fc_full = [sem(f"fc_full{i}") for i in range(FC_RING)]
        gelu_done = [sem(f"gelu_done{i}") for i in range(FC_RING)]
        y_full = [sem(f"y_full{i}") for i in range(2)]
        y_free = [sem(f"y_free{i}") for i in range(2)]
        y_stored = [sem(f"y_stored{i}") for i in range(OUT_RING)]
        rows_taken = [sem(f"rows_taken{i}") for i in range(TAKE_RING)]
        first_added = sem("first_added")
        token_done = sem("token_done")
        out_stored = sem("out_stored")
        blk = ctx.enter_context(nc.Block())

        def apart(eng):
            eng.sem_inc(wait_ended, 1)

        @blk.sync
        def _(sp):
            n = 0

            def load(dst, src, done=const_loaded):
                sp.dma_start(dst, src).then_inc(done, 16)

            load(id_all[:, :, :], ids)
            load(kind_i, kinds)
            load(kind_w[:, :], kind_rows)
            load(dom_w[:, :], domain_w)
            load(ln_c[:, :], ln_cols)
            for i in range(4):
                load(row_c[:, i, :], rows[i:i + 1, :].to_broadcast([128, HID]))
            load(o_w[:, 0, :], out_w[0:128, :])
            load(o_w[0:REST, 1, :], out_w[128:HID, :])
            load(g_w[:, 0, :], gate_w[0:128, :])
            load(g_w[0:REST, 1, :], gate_w[128:HID, :])
            load(qk_b[:, :], causal_qk_b)
            for w_src, v_src, done, after in ((mag_qk, mag_v, mag_w_loaded, None),
                                              (causal_qk, causal_v, cau_w_loaded, mag)):
                m = w_src.shape[1]
                if after is not None:
                    sp.wait_ge(mag.pv_done, JOBS * GROUPS + 2)
                load(raw_qk[:, 0, 0:m, :], w_src[0:128, :, :], done)
                load(raw_qk[0:REST, 1, 0:m, :], w_src[128:HID, :, :], done)
                load(raw_qk[REST:128, 1, 0:m, :], w_src[128:HID, :, :], done)
                load(raw_v[:, 0, :], v_src[0:128, :], done)
                load(raw_v[0:REST, 1, :], v_src[128:HID, :], done)
                load(raw_v[REST:128, 1, :], v_src[128:HID, :], done)
                if after is None:
                    sp.wait_ge(const_made, 1)
                    for t in range(SLOTS // 1280):
                        sp.dma_start(slot_in[1280 * t:1280 * (t + 1), :].rearrange("(k p) d -> p k d", p=128),
                                     zeros[:, :].unsqueeze(1).to_broadcast([128, 10, HID])
                                     ).then_inc(zero_filled, 16)

            sp.dma_start(fc_bias[:, :, :], fc_b).then_inc(bias_loaded, 16)
            for e in range(EXPERTS):
                sp.dma_start(pj_bias[:, e, :], pj_b[e:e + 1, :].to_broadcast([128, HID])).then_inc(bias_loaded, 16)
            sp.wait_ge(slots_put, 16 * TOPK * SEQS)
            with sp.Fori(0, EXPERTS // 2, 1) as r:
                for u in range(2):
                    e = r * 2 + u
                    sp.wait_ge(raw_split, e + 1)
                    for dst, rows_ in ((raw_fc[:, 0, :], slice(0, 128)), (raw_fc[0:REST, 1, :], slice(128, HID)),
                                       (raw_fc[REST:128, 1, :], slice(128, HID))):
                        sp.dma_start(dst, fc_w[bass.ds(e, 1), rows_, :].rearrange("e p n -> p (e n)")
                                     ).then_inc(raw_loaded, 16)
                    sp.wait_ge(pj_used[u], r + 1)
                    sp.dma_start(pj_w_sb[:, u, :, :], pj_w[bass.ds(e, 1), :, :].rearrange(
                        "e (c p) n -> p (e c) n", p=128)).then_inc(pj_loaded[u], 16)
                    for c, (t0, nt) in enumerate(CHUNKS):
                        sp.wait_ge(x_turned[c], e + 1)
                        src = slot_in[bass.ds(e * CAP + t0 * 128, nt * 128), :].rearrange("(t p) d -> p t d", p=128)
                        sp.dma_start(slot_x[c][:, :, 0:HID], src).then_inc(x_loaded[c], 16)
                        sp.dma_start(slot_x[c][:, :, HID:256], src[:, :, 128:HID]).then_inc(x_loaded[c], 16)
            for t in range(0, SEQS, 4):
                sp.wait_ge(token_done, t + 4)
                sp.dma_start(out[t:t + 4].rearrange("t p d -> p t d"), resid[:, t:t + 4, :]).then_inc(out_stored, 16)
            sp.wait_ge(out_stored, 16 * (SEQS // 4))
            sp.wait_ge(zero_filled, 16 * (SLOTS // 1280))

        CONST = 14 * 16

        @blk.gpsimd
        def _(pool):
            gp = nc.gpsimd
            gp.memset(zeros[:, :], 0.0).then_inc(const_made, 1)
            gp.memset(half[:, :], -0.5)
            gp.memset(kind_hot[:, :], 1.0)
            gp.memset(ident[:, :], 0.0)
            gp.memset(causal[:, :], 0.0)
            gp.iota(kind_sc[:, 0:1], pattern=[[0, 1]], base=-1, channel_multiplier=2,
                    allow_small_or_imprecise_dtypes=True)
            gp.iota(kind_sc[:, 1:2], pattern=[[0, 1]], base=1, channel_multiplier=-1,
                    allow_small_or_imprecise_dtypes=True)
            gp.memset(below[:, :], 1.0)
            gp.memset(ones_b[:, :], 1.0)
            gp.memset(one_f[:, :], 1.0)
            gp.iota(number_e[:, :], pattern=[[1, EXPERTS]], base=0, channel_multiplier=0,
                    allow_small_or_imprecise_dtypes=True)
            gp.memset(vals[:, :, :, :], 0.0).then_inc(const_made, 1)
            pool.wait_ge(const_made, 2)
            gp.affine_select(out=ident[:, :], in_=ident[:, :], compare_op=ALU.not_equal, fill=1.0, base=0,
                             pattern=[[-1, 128]], channel_multiplier=1)
            gp.affine_select(out=below[:, :], in_=below[:, :], compare_op=ALU.is_gt, fill=0.0, base=0,
                             pattern=[[1, 128]], channel_multiplier=-1)
            gp.affine_select(out=causal[:, :], in_=causal[:, :], compare_op=ALU.is_ge, fill=MASKED, base=0,
                             pattern=[[-1, 128]], channel_multiplier=1)
            gp.memset(vals[:, :, :, HEAD_DIM:HEAD_DIM + 1], 1.0).then_inc(ident_ready, 1)
            pool.wait_ge(const_loaded, CONST)

            def power(n, src, dst, eps, p, name, base):
                k = p.named(name + "_eps")
                gp.tensor_scalar(dst, src, eps, None, ALU.add).then_inc(k, 1)
                pool.wait_ge(k, n + 1)
                gp.tensor_tensor(dst, dst, half[:, 0:dst.shape[1]], ALU.pow).then_inc(p.named(name), 1)

            def gathers(g):
                pool.wait_ge(mag.named("emb_affine0"), g + 1)
                gp.tensor_copy(id_now[:, :, :], id_all[:, :, bass.ds(GROUP * g, GROUP)]).then_inc(id_copied, 1)
                pool.wait_ge(id_copied, g + 1)
                apart(pool)
                for table, dst, done, i in ((domain_table, got_dom, dom_got, 1), (word_table, got_word, word_got, 0),
                                            (pos_table, got_pos, pos_got, 2)):
                    for s in range(GROUP):
                        gp.indirect_dma_start(dst[:, s, :], None, table[:, :],
                                              bass.IndirectOffsetOnAxis(id_now[:, i, s:s + 1], 0)
                                              ).then_inc(done, 16)

            def embedding_norms(g):
                pool.wait_ge(mag.named("emb_moments"), g + 1)
                apart(pool)
                power(g, moments[:, :, 1], rstd[:, 0, :], WORD_EPS, mag, "emb_rstd", 0)
                pool.wait_ge(mag.named("x_moments"), g + 1)
                apart(pool)
                power(g, moments[:, :, 1], rstd[:, 1, :], LN_EPS, mag, "x_rstd", 0)

            def negate_max_roots(g):
                for s in range(GROUP):
                    pool.wait_ge(mag.root_done, GROUP * g + s + 1)
                    apart(pool)
                    gp.tensor_scalar(neg_max[:, s, :], row_root[:, s, :], -1.0, None,
                                     ALU.mult).then_inc(mag.neg_max_done, 1)

            def put_tokens():
                pool.wait_ge(put_ready, 1)
                pool.wait_ge(zero_filled, 16 * (SLOTS // 1280))
                pool.wait_ge(z_kept, SEQS + 2)
                for k in range(TOPK):
                    for t in range(SEQS):
                        c = k * SEQS + t
                        gp.indirect_dma_start(slot_in[:, :], bass.IndirectOffsetOnAxis(put_at[:, c:c + 1], 0),
                                              xin[:, t, :], None, bounds_check=SLOTS - 1, oob_is_err=False
                                              ).then_inc(slots_put, 16)

            def store_slots():
                with pool.Fori(0, EXPERTS, 1) as e:
                    for t in range(CAP_TILES):
                        i = t % 2
                        pool.wait_ge(y_free[i], e * (CAP_TILES // 2) + t // 2 + 2)
                        gp.dma_start(slot_out[bass.ds(e * CAP + 128 * t, 128), :], slot_y[:, t % OUT_RING, :]
                                     ).then_inc(y_stored[t % OUT_RING], 16)

            def take_rows():
                for i in range(OUT_RING):
                    pool.wait_ge(y_stored[i], 16 * EXPERTS * CAP_TILES // OUT_RING)
                for t in range(SEQS):
                    if t >= TAKE_RING:
                        pool.wait_ge(token_done, t - TAKE_RING + 1)
                    for k in range(TOPK):
                        c = k * SEQS + t
                        gp.indirect_dma_start(taken[:, t % TAKE_RING, k, :], None, slot_out[:, :],
                                              bass.IndirectOffsetOnAxis(take_at[:, c:c + 1], 0)
                                              ).then_inc(rows_taken[t % TAKE_RING], 16)

            gathers(0)
            embedding_norms(0)

            def magnitude_pass(g, front, back, prep):
                if prep:
                    gathers(g + 1)
                    embedding_norms(g + 1)
                if front:
                    negate_max_roots(g)

            magnitude_pass(0, True, False, True)
            with pool.Fori(1, GROUPS - 1, 1) as g:
                magnitude_pass(g, True, True, True)
            magnitude_pass(GROUPS - 1, True, True, False)

            def layer_norm_scales(g):
                n = g
                pool.wait_ge(cau.named("moments"), n + 1)
                apart(pool)
                power(n, moments[:, :, 1], rstd[:, 0, :], LN_EPS, cau, "first_rstd", 0)
                k = cau.named("second_var")
                pool.wait_ge(cau.named("first_rstd"), n + 1)
                gp.tensor_tensor(rstd[:, 2, :], moments[:, :, 1], rstd[:, 0, :], ALU.mult).then_inc(k, 1)
                pool.wait_ge(k, 2 * n + 1)
                gp.tensor_tensor(rstd[:, 3, :], rstd[:, 2, :], rstd[:, 0, :], ALU.mult).then_inc(k, 1)
                pool.wait_ge(k, 2 * n + 2)
                apart(pool)
                power(n, rstd[:, 3, :], rstd[:, 1, :], LN_EPS, cau, "second_rstd", 0)

            def negate_max(g):
                for s in range(GROUP):
                    pool.wait_ge(cau.scores_free, 2 * (JOBS * g + 3 * s + 3) + 2)
                    apart(pool)
                    gp.tensor_scalar(neg_max[:, s, :], row_max[:, s, :], -0.25, None,
                                     ALU.mult).then_inc(cau.neg_max_done, 1)

            def z_scale(g, s):
                n = GROUP * g + s
                pool.wait_ge(cau.named("z_moments"), n + 1)
                apart(pool)
                power(n, z_moments[:, 1:2], rstd[:, 4, 0:1], LN_EPS, cau, "z_rstd", 0)

            def keep_z(g, s):
                n = GROUP * g + s
                pool.wait_ge(z_ready, n + 1)
                gp.tensor_copy(xin[:, n, :], z[:, s % 2, :]).then_inc(z_kept, 1)

            def causal_pass(g, front, back, prep):
                if back:
                    for s in range(GROUP):
                        z_scale(g - 1, s)
                        keep_z(g - 1, s)
                if prep:
                    layer_norm_scales(g + 1)
                if front:
                    negate_max(g)

            layer_norm_scales(0)
            causal_pass(0, True, False, True)
            with pool.Fori(1, GROUPS - 1, 1) as g:
                causal_pass(g, True, True, True)
            causal_pass(GROUPS - 1, True, True, False)
            causal_pass(GROUPS, False, True, False)
            put_tokens()
            store_slots()
            take_rows()

        @blk.tensor
        def _(pe):
            for p in (mag, cau):
                for i in range(RING):
                    pe.sem_inc(p.ring_free[i], 1)
                pe.sem_inc(p.scores_free, 2)
                pe.sem_inc(p.pv_done, 2)
                pe.sem_inc(p.ctx_copied, 1)

            def transpose(dst, src, n=128):
                return pe.transpose(dst, src, ident[0:n, 0:n])

            def split_product(dst, x, w_cols, v):
                pairs = ((x[0], w_cols[0]), (x[0], w_cols[1]), (x[1], w_cols[0]), (x[2], w_cols[2]),
                         (x[2], w_cols[3]))
                for k, (a, w) in enumerate(pairs):
                    lhs, rhs = (a, w) if v else (w, a)
                    last = pe.matmul(dst, lhs, rhs, start=(k == 0), stop=(k == 4))
                return last

            def taken_out(p, d, f, own):
                i, n = d[f]
                if i != own:
                    pe.wait_ge(p.ring_free[i], n + 2)

            def fill(p, g, f, place, d):
                i, n = place
                kind, s = f
                pe.wait_ge(p.ring_free[i], n + 1)
                dst = ps_ring[:, i, :]
                if kind == "xT":
                    pe.wait_ge(p.x_ready, GROUP * g + 2 * s + 2)
                    for t in range(2):
                        for c in range(2):
                            last = transpose(dst[:, 256 * t + 128 * c:256 * t + 128 * c + 128],
                                             xn[:, 2 * s + t, 128 * c:128 * c + 128])
                elif kind == "proj":
                    m, b = divmod(s, 3)
                    if s == 0:
                        taken_out(p, d, ("xT", 1), i)
                    col = slice(128 * b, 128 * b + 128)
                    last = split_product(dst, (x_hi[:, 0, :], x_lo[:, :], x_hi[:, 1, :]),
                                         (w_hi[:, 0, m, col], w_lo[:, 0, m, col], w_hi[:, 1, m, col],
                                          w_lo[:, 1, m, col]), False)
                elif kind == "value":
                    for t in range(p.values_per_fill):
                        k = 128 * (p.values_per_fill * s + t)
                        tok = slice(k, k + 128)
                        last = split_product(dst[:, HID * t:HID * t + HID],
                                             (x_hi[:, 0, tok], x_lo[:, tok], x_hi[:, 1, tok]),
                                             (v_hi[:, 0, :], v_lo[:, 0, :], v_hi[:, 1, :], v_lo[:, 1, :]), True)
                elif kind == "domT":
                    pe.wait_ge(dom_got, 16 * GROUP * (g + 1) + 16 * GROUP)
                    for t in range(2):
                        last = transpose(dst[:, 128 * t:128 * t + 128], got_dom[:, 2 * s + t, :])
                elif kind == "embed":
                    taken_out(p, d, ("domT", s), i)
                    pe.wait_ge(p.named("kinds_done"), g + 2)
                    for t in (2 * s, 2 * s + 1):
                        o = HID * (t % 2)
                        pe.matmul(dst[:, o:o + HID], dom_t[:, t, :], dom_w[:, :], start=True, stop=False)
                        last = pe.matmul(dst[:, o:o + HID], kind_hot[:, 128 * t:128 * t + 128], kind_w[:, :],
                                         start=False, stop=True)
                elif kind == "ctxT":
                    pe.wait_ge(p.named("ctx_dup"), GROUP * (g - 1) + s + 1)
                    transpose(dst[:, 0:128], ctx_n[:, 0:128])
                    last = transpose(dst[:, 128:256], ctx_n[:, 128:256])
                elif kind == "out":
                    taken_out(p, d, ("ctxT", s), i)
                    pe.matmul(dst[:, 0:HID], ctxn_t[:, 0, :], o_w[:, 0, :], start=True, stop=False)
                    last = pe.matmul(dst[:, 0:HID], ctxn_t[0:REST, 1, :], o_w[0:REST, 1, :],
                                     start=False, stop=True)
                elif kind == "zT":
                    pe.wait_ge(z_ready, GROUP * (g - 1) + s + 1)
                    transpose(dst[:, 0:128], z[:, s % 2, 0:128])
                    last = transpose(dst[0:REST, 128:256], z[:, s % 2, 128:HID])
                elif kind == "logits":
                    taken_out(p, d, ("zT", GROUP - 1), i)
                    pe.matmul(dst[0:EXPERTS, :], g_w[:, 0, :], z_t[:, 0, :], start=True, stop=False)
                    last = pe.matmul(dst[0:EXPERTS, :], g_w[0:REST, 1, :], z_t[0:REST, 1, :],
                                     start=False, stop=True)
                elif kind == "logitsT":
                    taken_out(p, d, ("logits", s), i)
                    apart(pe)
                    for t in range(GROUP):
                        last = transpose(dst[:, 8 * t:8 * t + 8], gate_t[:, 128 * t:128 * t + 128], EXPERTS)
                elif kind == "probT":
                    pe.wait_ge(p.exp_done, JOBS * (g - 1) + s + 1)
                    for h in range(4):
                        last = transpose(dst[:, 128 * h:128 * h + 128], probs[:, s, h, :])
                elif kind == "ctx":
                    pe.wait_ge(p.ctx_copied, GROUP * (g - 1) + s + 2)
                    for b in range(BLOCKS):
                        last = transpose(dst[:, 128 * b:128 * b + 128], ctx_t[:, b, :])
                last.then_inc(p.ring_full[i], 1)

            def scores(p, g, j, d):
                s, b = divmod(j, 3)
                if j == 0:
                    taken_out(p, d, ("proj", 8 if p is mag else 5), None)
                width = 256 if p is mag else 128
                for pair in range(2):
                    pe.wait_ge(p.scores_free, 2 * (JOBS * g + j) + pair + 1)
                    for a in range(3):
                        for h in (2 * pair, 2 * pair + 1):
                            r = slice(32 * h, 32 * h + 32)
                            q = q_lo if a == 1 else q_hi
                            k = k_lo if a == 2 else k_hi
                            keys = k[r, b, s, :, :].rearrange("p m k -> p (m k)")[:, 0:width]
                            last = pe.matmul(ps_scores[:, h, 0:width], q[r, b, s, :], keys,
                                             start=(a == 0), stop=(a == 2))
                    last.then_inc(p.scores_full, 1)

            def values_product(p, gb, j, d):
                s, b = divmod(j, 3)
                i, n = d[("probT", j)]
                pe.wait_ge(p.ring_free[i], n + 2)
                if b == 0:
                    pe.wait_ge(p.ctx_copied, GROUP * gb + s + 1)
                for h in range(4):
                    last = pe.matmul(ps_ctx[32 * h:32 * h + 32, 128 * b:128 * b + 128],
                                     vals[:, s, 4 * b + h, :], prob_t[:, j % 2, h, :],
                                     start=True, stop=True, skip_group_check=True)
                last.then_inc(p.pv_done, 1)

            def one_pass(p, g, front, back, prep):
                by_slot, places = p.schedule(g, front, back, prep)
                for slot in range(PASS_SLOTS):
                    for f in by_slot[slot]:
                        fill(p, g, f, places[f], places)
                    if back and 1 <= slot <= JOBS:
                        values_product(p, g - 1, slot - 1, places)
                    if front and slot >= JOBS:
                        scores(p, g, slot - JOBS, places)

            def phase(p):
                one_pass(p, 0, True, False, True)
                with pe.Fori(1, GROUPS - 1, 1) as g:
                    one_pass(p, g, True, True, True)
                one_pass(p, GROUPS - 1, True, True, False)
                one_pass(p, GROUPS, False, True, False)

            pe.wait_ge(ident_ready, 1)
            pe.wait_ge(const_loaded, CONST)
            lead = mag.lead_places()
            for f in mag.lead:
                fill(mag, -1, f, lead[f], lead)
            pe.wait_ge(mag_w_split, 4)
            phase(mag)
            pe.wait_ge(cau_w_split, 2)
            phase(cau)
            pe.wait_ge(hot_ready, 1)
            hots = hot[:, :, :].rearrange("p t e -> p (t e)")
            pe.matmul(ps_scores[:, 0, :], below[:, :], hots, start=True, stop=True)
            pe.matmul(ps_scores[:, 1, :], ones_b[:, :], hots, start=True, stop=True).then_inc(ranked, 1)

            for i in range(2):
                pe.sem_inc(ex_turn_free[i], 1)
                pe.sem_inc(y_free[i], 1)
                pe.sem_inc(pj_used[i], 1)
            for i in range(FC_RING):
                pe.sem_inc(gelu_done[i], 1)
            for c in range(3):
                pe.sem_inc(x_turned[c], 1)

            def turn_x(e, c):
                t0, nt = CHUNKS[c]
                pe.wait_ge(x_loaded[c], 32 * e + 32)
                for t in range(t0, t0 + nt):
                    i, n = t % 2, e * (CAP_TILES // 2) + t // 2
                    pe.wait_ge(ex_turn_free[i], n + 1)
                    transpose(ps_x[i][:, 0:128], slot_x[c][:, t - t0, 0:128])
                    transpose(ps_x[i][:, 128:256], slot_x[c][:, t - t0, 128:256]).then_inc(ex_turn_full[i], 1)
                pe.transpose(ps_scores[0:32, 3, 0:128], slot_x[c][:, nt - 1, 0:32], ident[:, :]
                             ).then_inc(x_turned[c], 1)

            def first_layer(e, c):
                t0, nt = CHUNKS[c]
                if c == 0:
                    pe.wait_ge(raw_split, e + 2)
                for t in (t0 + nt - 2, t0 + nt - 1):
                    pe.wait_ge(ex_turn_free[t % 2], e * (CAP_TILES // 2) + t // 2 + 2)
                tok = slice(0, 128 * nt)
                for f_ in range(FF_CHUNKS):
                    i = f_ % FC_RING
                    pe.wait_ge(gelu_done[i], e * 6 + 2 * c + f_ // FC_RING + 1)
                    col = slice(128 * f_, 128 * f_ + 128)
                    wh = w_hi[:, :, :, :].rearrange("p c m n -> p c (m n)")
                    wl = w_lo[:, :, :, :].rearrange("p c m n -> p c (m n)")
                    split_product(ps_scores[:, i, tok], (x_hi[:, 0, tok], x_lo[:, tok], x_hi[:, 1, tok]),
                                  (wh[:, 0, col], wl[:, 0, col], wh[:, 1, col], wl[:, 1, col]), False
                                  ).then_inc(fc_full[i], 1)

            def second_layer(r, u, e, c):
                t0, nt = CHUNKS[c]
                if c == 0:
                    pe.wait_ge(pj_loaded[u], 16 * r + 16)
                for i in range(FC_RING):
                    pe.wait_ge(gelu_done[i], e * 6 + 2 * c + 3)
                for t in range(t0, t0 + nt):
                    i, n = t % 2, e * (CAP_TILES // 2) + t // 2
                    pe.wait_ge(y_free[i], n + 1)
                    tok = slice(128 * (t - t0), 128 * (t - t0) + 128)
                    for f_ in range(FF_CHUNKS):
                        last = pe.matmul(ps_ring[:, i, 0:HID], hidden[:, c % 2, f_, tok], pj_w_sb[:, u, f_, :],
                                         start=(f_ == 0), stop=(f_ == FF_CHUNKS - 1))
                    last.then_inc(y_full[i], 1)

            with pe.Fori(0, EXPERTS // 2, 1) as r:
                for u in range(2):
                    e = r * 2 + u
                    turn_x(e, 0)
                    first_layer(e, 0)
                    turn_x(e, 1)
                    second_layer(r, u, e, 0)
                    first_layer(e, 1)
                    turn_x(e, 2)
                    second_layer(r, u, e, 1)
                    first_layer(e, 2)
                    pe.transpose(ps_scores[0:32, 3, 0:128], ident[:, 0:32], ident[:, :]).then_inc(fc_used, 1)
                    second_layer(r, u, e, 2)
                    pe.transpose(ps_scores[0:32, 3, 0:128], ident[:, 0:32], ident[:, :]).then_inc(pj_used[u], 1)

        @blk.scalar
        def _(act):
            sc = nc.scalar

            def split_weights_high(loaded, done, m):
                act.wait_ge(loaded, 6 * 16)
                sc.activation(w_hi[:, :, 0:m, :], raw_qk[:, :, 0:m, :], ACT.Copy).then_inc(done, 1)
                sc.activation(v_hi[:, :, :], raw_v[:, :, :], ACT.Copy).then_inc(done, 1)

            def fill(p, g, f, place, d):
                i, n = place
                kind, s = f
                src = ps_ring[:, i, :]
                if kind in ("embed", "out", "logitsT", "probT", "ctx"):
                    return
                act.wait_ge(p.ring_full[i], n + 1)
                tok = slice(128 * s, 128 * s + 128)
                if kind == "xT":
                    two = slice(256 * s, 256 * s + 256)
                    by_chunk = src.rearrange("p (s c t) -> p c s t", s=2, c=2)
                    if p is mag:
                        sc.activation(x_hi[:, :, two].rearrange("p c (s t) -> p c s t", s=2), by_chunk,
                                      ACT.Copy).then_inc(p.high_done, 1)
                    else:
                        if s > 0:
                            fi, fn = d[("xT", s - 1)]
                            act.wait_ge(p.ring_free[fi], fn + 2)
                        for c in range(2):
                            last = sc.activation(x_full[:, c, :].rearrange("p (s t) -> p s t", s=2),
                                                 by_chunk[:, c, :, :], ACT.Identity, bias=ln_c[:, 2 + c:3 + c],
                                                 scale=ln_c[:, c:c + 1])
                        last.then_inc(p.high_done, 1)
                elif kind == "proj":
                    m, b = divmod(s, 3)
                    dst = q_hi[:, b, :, :] if m == 0 else k_hi[:, b, :, m - 1, :]
                    view = src.rearrange("p (s k) -> p s k", s=GROUP)
                    if p is mag:
                        sc.activation(dst, view, ACT.Copy).then_inc(p.high_done, 1)
                    else:
                        sc.activation(dst, view, ACT.Identity, bias=qk_b[:, s:s + 1]).then_inc(p.high_done, 1)
                elif kind == "value":
                    if p is mag:
                        sc.activation(vals[:, 2 * s:2 * s + 2, :, 0:HEAD_DIM],
                                      src[:, 0:2 * HID].rearrange("p (s h d) -> p s h d", s=2, h=HEADS),
                                      ACT.Copy).then_inc(p.ring_free[i], 1)
                elif kind == "domT":
                    sc.activation(dom_t[:, 2 * s:2 * s + 2, :], src[:, 0:256].rearrange("p (s t) -> p s t", s=2),
                                  ACT.Copy).then_inc(p.ring_free[i], 1)
                elif kind == "ctxT":
                    sc.activation(ctxn_t, src[:, 0:256].rearrange("p (c t) -> p c t", c=2),
                                  ACT.Copy).then_inc(p.ring_free[i], 1)
                elif kind == "zT":
                    sc.activation(z_t[:, 0, tok], src[:, 0:128], ACT.Identity, bias=ln_c[:, 6:7],
                                  scale=ln_c[:, 4:5]).then_inc(z_used, 1)
                    sc.activation(z_t[0:REST, 1, tok], src[0:REST, 128:256], ACT.Identity,
                                  bias=ln_c[0:REST, 7:8], scale=ln_c[0:REST, 5:6]).then_inc(p.ring_free[i], 1)
                elif kind == "logits":
                    sc.activation(gate_t, src[0:EXPERTS, :],
                                  ACT.Copy).then_inc(p.ring_free[i], 1)

            def exps(p, gb, j):
                s, b = divmod(j, 3)
                if b == 0:
                    act.wait_ge(p.neg_max_done, GROUP * gb + s + 1)
                for h in range(4):
                    last = sc.activation(probs[:, j, h, :], probs[:, j, h, :], ACT.Exp,
                                         bias=neg_max[:, s, 4 * b + h:4 * b + h + 1],
                                         scale=1.0 if p is mag else 0.25)
                last.then_inc(p.exp_done, 1)

            def squares(g, j):
                act.wait_ge(mag.max_done, JOBS * g + j + 1)
                for pair in range(2):
                    act.wait_ge(mag.scores_full, 2 * (JOBS * g + j) + pair + 1)
                    h = slice(2 * pair, 2 * pair + 2)
                    sc.activation(square[:, j % 2, h, :, :].rearrange("p h m k -> p h (m k)"),
                                  ps_scores[:, h, 0:256], ACT.Square).then_inc(mag.scores_free, 1)

            def roots(g, s):
                act.wait_ge(mag.max_done, JOBS * g + 3 * s + 3 + 2)
                sc.activation(row_root[:, s, :], row_max[:, s, :], ACT.Sqrt, scale=1.0 / HEAD_DIM)
                sc.activation(probs[:, 3 * s:3 * s + 3, :, :], probs[:, 3 * s:3 * s + 3, :, :],
                              ACT.Sqrt, scale=1.0 / HEAD_DIM).then_inc(mag.root_done, 1)

            def copy_ctx(p, gb, s):
                act.wait_ge(p.pv_done, JOBS * gb + 3 * s + 3 + 2)
                sc.activation(ctx_t[:, :, :], ps_ctx[:, 0:384].rearrange("p (b q) -> p b q", b=3),
                              ACT.Copy).then_inc(p.ctx_copied, 1)

            def one_pass(p, g, front, back, prep):
                by_slot, places = p.schedule(g, front, back, prep)
                for slot in range(PASS_SLOTS):
                    if back and slot == 0:
                        exps(p, g - 1, 0)
                    if back and slot + 1 < JOBS:
                        exps(p, g - 1, slot + 1)
                    for f in by_slot[slot]:
                        fill(p, g, f, places[f], places)
                    if back and slot >= 3 and slot % 3 == 0 and slot // 3 <= GROUP:
                        copy_ctx(p, g - 1, slot // 3 - 1)
                    if p is mag and front and slot >= JOBS:
                        j = slot - JOBS
                        squares(g, j)
                        if j >= 4 and (j - 4) % 3 == 0:
                            roots(g, (j - 4) // 3)
                if p is mag and front:
                    roots(g, 3)

            def phase(p):
                one_pass(p, 0, True, False, True)
                with act.Fori(1, GROUPS - 1, 1) as g:
                    one_pass(p, g, True, True, True)
                one_pass(p, GROUPS - 1, True, True, False)
                one_pass(p, GROUPS, False, True, False)

            act.wait_ge(const_loaded, CONST)
            split_weights_high(mag_w_loaded, mag_w_high, 3)
            lead = mag.lead_places()
            for f in mag.lead:
                fill(mag, -1, f, lead[f], lead)
            phase(mag)
            split_weights_high(cau_w_loaded, cau_w_high, 2)
            phase(cau)
            act.wait_ge(gap_ready, 1)
            sc.activation(gap[:, 1, :], gap[:, 0, :], ACT.Exp).then_inc(gap_exp, 1)

            def expert_weights_high(e):
                act.wait_ge(raw_loaded, 48 * e + 48)
                act.wait_ge(fc_used, e + 1)
                sc.activation(w_hi[:, :, 0:2, :], raw_fc.rearrange("p c (m n) -> p c m n", m=2),
                              ACT.Copy).then_inc(fc_high, 1)

            def whole_x(e, c):
                t0, nt = CHUNKS[c]
                for t in range(t0, t0 + nt):
                    i, n = t % 2, e * (CAP_TILES // 2) + t // 2
                    act.wait_ge(ex_turn_full[i], n + 1)
                    if t > 0:
                        act.wait_ge(ex_turn_free[(t - 1) % 2], e * (CAP_TILES // 2) + (t - 1) // 2 + 2)
                    else:
                        act.wait_ge(ex_turn_free[1], e * (CAP_TILES // 2) + 1)
                    sc.activation(x_full[:, 0, 0:128], ps_x[i][:, 0:128], ACT.Identity, bias=ln_c[:, 6:7],
                                  scale=ln_c[:, 4:5])
                    sc.activation(x_full[:, 1, 0:128], ps_x[i][:, 128:256], ACT.Identity, bias=ln_c[:, 7:8],
                                  scale=ln_c[:, 5:6]).then_inc(ex_whole, 1)

            def gelus(e, c):
                nt = CHUNKS[c][1]
                for f_ in range(FF_CHUNKS):
                    i = f_ % FC_RING
                    act.wait_ge(fc_full[i], e * 6 + 2 * c + f_ // FC_RING + 1)
                    apart(act)
                    sc.activation(hidden[:, c % 2, f_, 0:128 * nt], ps_scores[:, i, 0:128 * nt], ACT.Gelu,
                                  bias=fc_bias[:, e, f_:f_ + 1]).then_inc(gelu_done[i], 1)

            act.sem_inc(fc_used, 1)
            act.wait_ge(bias_loaded, 16 * (1 + EXPERTS))
            with act.Fori(0, EXPERTS, 1) as e:
                expert_weights_high(e)
                whole_x(e, 0)
                gelus(e, 0)
                whole_x(e, 1)
                gelus(e, 1)
                whole_x(e, 2)
                gelus(e, 2)

        @blk.vector
        def _(dve):
            ve = nc.vector
            f = lambda a: a.bitcast(F32)

            def split_weights_low(loaded, high, done, m):
                dve.wait_ge(loaded, 6 * 16)
                dve.wait_ge(high, 2)
                ve.tensor_tensor(w_lo[:, :, 0:m, :], raw_qk[:, :, 0:m, :], f(w_hi[:, :, 0:m, :]),
                                 ALU.subtract).then_inc(done, 1)
                ve.tensor_tensor(v_lo[:, :, :], raw_v[:, :, :], f(v_hi[:, :, :]), ALU.subtract).then_inc(done, 1)

            def negate_imaginary_keys():
                for w in (w_hi, w_lo):
                    v = w[:, :, 2, :].rearrange("p c (h x) -> p c h x", x=32)[:, :, :, 0:HEAD_DIM]
                    ve.tensor_scalar(v, f(v), -1.0, None, ALU.mult).then_inc(mag_w_split, 1)

            def fill(p, g, fl, place):
                i, n = place
                kind, s = fl
                src = ps_ring[:, i, :]
                free = p.ring_free[i]
                two = slice(256 * s, 256 * s + 256)
                hl = slice(REST, 128)
                if kind == "xT":
                    dve.wait_ge(p.high_done, high_count(p, g, fl))
                    if p is mag:
                        by_chunk = src.rearrange("p (s c t) -> p c s t", s=2, c=2)
                        halves = lambda a: a.rearrange("p (s t) -> p s t", s=2)
                        ve.tensor_tensor(halves(x_lo[:, two]), by_chunk[:, 0, :, :], halves(f(x_hi[:, 0, two])),
                                         ALU.subtract)
                        ve.tensor_tensor(halves(x_hi[hl, 1, two]), by_chunk[hl, 1, :, :],
                                         halves(f(x_hi[hl, 1, two])), ALU.subtract).then_inc(free, 1)
                    else:
                        ve.tensor_copy(x_hi[:, :, two], x_full[:, :, :]).then_inc(p.named("x_high"), 1)
                        dve.wait_ge(p.named("x_high"), 2 * g + s + 1)
                        ve.tensor_tensor(x_lo[:, two], x_full[:, 0, :], f(x_hi[:, 0, two]), ALU.subtract)
                        ve.tensor_tensor(x_hi[hl, 1, two], x_full[hl, 1, :], f(x_hi[hl, 1, two]),
                                         ALU.subtract).then_inc(free, 1)
                elif kind == "proj":
                    dve.wait_ge(p.high_done, high_count(p, g, fl))
                    m, b = divmod(s, 3)
                    if m == 0:
                        lo, hi = q_lo[:, b, :, :], q_hi[:, b, :, :]
                    else:
                        lo, hi = k_lo[:, b, :, m - 1, :], k_hi[:, b, :, m - 1, :]
                    view = src.rearrange("p (s k) -> p s k", s=GROUP)
                    if p is mag:
                        ve.tensor_tensor(lo, view, f(hi), ALU.subtract).then_inc(free, 1)
                    else:
                        ve.scalar_tensor_tensor(out=lo, in0=view, scalar=qk_b[:, s:s + 1], in1=f(hi),
                                                op0=ALU.add, op1=ALU.subtract).then_inc(free, 1)
                elif kind == "value" and p is cau:
                    dve.wait_ge(p.ring_full[i], n + 1)
                    ve.tensor_tensor(vals[:, s, :, 0:HEAD_DIM],
                                     src[:, 0:HID].rearrange("p (h d) -> p h d", h=HEADS),
                                     row_c[:, 2, :].rearrange("p (h d) -> p h d", h=HEADS),
                                     ALU.add).then_inc(free, 1)
                elif kind == "embed":
                    dve.wait_ge(p.ring_full[i], n + 1)
                    pair = got_word[:, 2 * s:2 * s + 2, :]
                    ve.tensor_tensor(pair, src[:, 0:2 * HID].rearrange("p (s d) -> p s d", s=2), pair,
                                     ALU.add).then_inc(free, 1)
                elif kind == "probT":
                    dve.wait_ge(p.ring_full[i], n + 1)
                    dve.wait_ge(p.pv_done, JOBS * (g - 1) + s + 1)
                    ve.tensor_copy(prob_t[:, s % 2, :, :], src.rearrange("p (h q) -> p h q", h=4)
                                   ).then_inc(free, 1)
                elif kind == "ctx":
                    t = GROUP * (g - 1) + s
                    dve.wait_ge(p.ring_full[i], n + 1)
                    v = src[:, 0:384].rearrange("p (h x) -> p h x", x=32)
                    ve.reciprocal(recip[:, :], v[:, :, HEAD_DIM]).then_inc(p.recip_done, 1)
                    dve.wait_ge(p.recip_done, t + 1)
                    ve.tensor_tensor(ctx_n[:, 0:HID].rearrange("p (h d) -> p h d", h=HEADS), v[:, :, 0:HEAD_DIM],
                                     recip[:, :].unsqueeze(2).to_broadcast([128, HEADS, HEAD_DIM]),
                                     ALU.mult).then_inc(free, 1)
                    dve.wait_ge(free, n + 2)
                    if p is mag:
                        ve.tensor_tensor(resid[:, t, :], resid[:, t, :], ctx_n[:, 0:HID], ALU.add
                                         ).then_inc(p.ctx_done, 1)
                    else:
                        ve.tensor_copy(ctx_n[:, HID:256], ctx_n[:, 128:HID]).then_inc(p.named("ctx_dup"), 1)
                elif kind == "out":
                    t = GROUP * (g - 1) + s
                    dve.wait_ge(p.ring_full[i], n + 1)
                    ve.tensor_tensor(out_b, src[:, 0:HID], row_c[:, 3, :], ALU.add).then_inc(free, 1)
                    dve.wait_ge(free, n + 2)
                    ve.tensor_tensor(xin[:, t, :], xin[:, t, :], out_b, ALU.add
                                     ).then_inc(p.named("layer_sum"), 1)
                    ve.tensor_tensor(resid[:, t, :], resid[:, t, :], out_b, ALU.add)
                    dve.wait_ge(p.named("layer_sum"), t + 1)
                    apart(dve)
                    ve.bn_stats(z_stats[:, :], xin[:, t, :]).then_inc(p.named("z_stats"), 1)
                    dve.wait_ge(p.named("z_stats"), t + 1)
                    apart(dve)
                    ve.bn_aggr(z_moments[:, :], z_stats[:, :]).then_inc(p.named("z_moments"), 1)
                elif kind == "logitsT":
                    dve.wait_ge(p.ring_full[i], n + 1)
                    ve.tensor_copy(logits[:, bass.ds(GROUP * (g - 1), GROUP), :],
                                   src[:, 0:GROUP * EXPERTS].rearrange("p (t e) -> p t e", t=GROUP)
                                   ).then_inc(free, 1)

            def high_count(p, g, fl):
                kind, s = fl
                per = 2 + (9 if p is mag else 6)
                return per * g + (s if kind == "xT" else 2 + s) + 1

            def normalise_z(p, gb, s):
                t = GROUP * gb + s
                dve.wait_ge(p.named("z_rstd"), t + 1)
                dve.wait_ge(p.named("z_moments"), t + 1)
                dve.wait_ge(z_used, t + 1)
                dve.wait_ge(z_kept, t + 1)
                ve.tensor_scalar(z[:, s % 2, :], xin[:, t, :], z_moments[:, 0:1], rstd[:, 4, 0:1],
                                 ALU.subtract, ALU.mult).then_inc(z_ready, 1)

            def maxima(p, g, j):
                s, b = divmod(j, 3)
                for pair in range(2):
                    if p is mag:
                        dve.wait_ge(mag.scores_free, 2 * (JOBS * g + j) + pair + 1 + 2)
                    else:
                        dve.wait_ge(cau.scores_full, 2 * (JOBS * g + j) + pair + 1)
                    apart(dve)
                    for h in (2 * pair, 2 * pair + 1):
                        if p is mag:
                            a, c = square[:, j % 2, h, 0, :], square[:, j % 2, h, 1, :]
                        else:
                            a, c = ps_scores[:, h, 0:128], causal[:, :]
                        last = ve.tensor_tensor_reduce(out=probs[:, j, h, :], in0=a, in1=c, scale=1.0,
                                                       scalar=-3.0e38, op0=ALU.add, op1=ALU.max,
                                                       accum_out=row_max[:, s, 4 * b + h:4 * b + h + 1])
                    if p is cau:
                        last.then_inc(cau.scores_free, 1)
                if p is mag:
                    last.then_inc(p.max_done, 1)

            def lay_kinds(g):
                ve.tensor_scalar(kind_hot[0:2, :], kind_i[:, bass.ds(512 * g, 512)], kind_sc[:, 0:1],
                                 kind_sc[:, 1:2], ALU.mult, ALU.add).then_inc(mag.named("kinds_done"), 1)

            def add_positions(g):
                dve.wait_ge(word_got, 16 * GROUP * (g + 1))
                dve.wait_ge(pos_got, 16 * GROUP * (g + 1))
                ve.tensor_tensor(got_word[:, :, :], got_word[:, :, :], got_pos[:, :, :], ALU.add
                                 ).then_inc(mag.named("pos_added"), 1)
                dve.wait_ge(mag.named("pos_added"), g + 1)

            def group_moments(p, src, g, name):
                for s in range(GROUP):
                    last = ve.bn_stats(stats[:, s, :], src(s))
                last.then_inc(p.named(name + "_stats"), 1)
                dve.wait_ge(p.named(name + "_stats"), g + 1)
                apart(dve)
                for s in range(GROUP):
                    last = ve.bn_aggr(moments[:, s, :], stats[:, s, :])
                last.then_inc(p.named(name), 1)

            def scale_tile(dst, src, s, r):
                return ve.tensor_scalar(dst, src, moments[:, s, 0:1], rstd[:, r, s:s + 1], ALU.subtract, ALU.mult)

            def dup_view(a):
                return a.unsqueeze(1).to_broadcast([128, 2, REST])

            def embedding_tail(g, places):
                i, n = places[("embed", 1)]
                dve.wait_ge(mag.ring_free[i], n + 2)
                apart(dve)
                group_moments(mag, lambda s: got_word[:, s, :], g, "emb_moments")
                dve.wait_ge(mag.named("emb_moments"), g + 1)
                dve.wait_ge(mag.named("emb_rstd"), g + 1)
                for s in range(GROUP):
                    last = scale_tile(got_word[:, s, :], got_word[:, s, :], s, 0)
                last.then_inc(mag.named("emb_scaled"), 1)
                dve.wait_ge(mag.named("emb_scaled"), g + 1)
                tiles = resid[:, bass.ds(GROUP * g, GROUP), :]
                for i_row, op, src in ((0, ALU.mult, got_word[:, :, :]), (1, ALU.add, tiles)):
                    last = ve.tensor_tensor(tiles, src, row_c[:, i_row, :].unsqueeze(1)
                                            .to_broadcast([128, GROUP, HID]), op)
                    last.then_inc(mag.named(f"emb_affine{i_row}"), 1)
                    dve.wait_ge(mag.named(f"emb_affine{i_row}"), g + 1 + (i_row == 0))
                    apart(dve)
                group_moments(mag, lambda s: resid[:, GROUP * g + s, :], g, "x_moments")
                dve.wait_ge(mag.named("x_moments"), g + 1)
                dve.wait_ge(mag.named("x_rstd"), g + 1)
                for s in range(GROUP):
                    t = GROUP * g + s
                    scale_tile(xn[:, s, 0:128], resid[:, t, 0:128], s, 1)
                    scale_tile(xn[:, s, 128:256].rearrange("p (c d) -> p c d", c=2),
                               dup_view(resid[:, t, 128:HID]), s, 1).then_inc(mag.x_ready, 1)

            def causal_prep(g):
                group_moments(cau, lambda s: resid[:, GROUP * g + s, :], g, "moments")
                dve.wait_ge(cau.named("moments"), g + 1)
                dve.wait_ge(cau.named("first_rstd"), g + 1)
                k = cau.named("x_in")
                for s in range(GROUP):
                    t = GROUP * g + s
                    last = scale_tile(xin[:, t, :], resid[:, t, :], s, 0)
                last.then_inc(k, 1)
                dve.wait_ge(k, g + 1)
                tiles = bass.ds(GROUP * g, GROUP)
                ve.tensor_tensor(resid[:, tiles, :], resid[:, tiles, :], xin[:, tiles, :], ALU.add)
                dve.wait_ge(cau.named("second_rstd"), g + 1)
                for s in range(GROUP):
                    t = GROUP * g + s
                    r = rstd[:, 1, s:s + 1]
                    ve.tensor_scalar(xn[:, s, 0:128], xin[:, t, 0:128], r, None, ALU.mult)
                    ve.tensor_scalar(xn[:, s, 128:256].rearrange("p (c d) -> p c d", c=2),
                                     dup_view(xin[:, t, 128:HID]), r, None, ALU.mult).then_inc(cau.x_ready, 1)

            def one_pass(p, g, front, back, prep):
                by_slot, places = p.schedule(g, front, back, prep)
                for slot in range(PASS_SLOTS):
                    for fl in by_slot[slot]:
                        fill(p, g, fl, places[fl])
                    if p is cau and back and slot >= 7 and (slot - 7) % 3 == 0 and (slot - 7) // 3 < GROUP:
                        normalise_z(p, g - 1, (slot - 7) // 3)
                    if front and slot >= JOBS:
                        maxima(p, g, slot - JOBS)
                    if p is mag and prep and slot == 12:
                        lay_kinds(g + 1)
                    if p is mag and prep and slot == 13:
                        add_positions(g + 1)
                    if p is mag and prep and slot == 19:
                        embedding_tail(g + 1, places)
                    if p is cau and prep and slot == 21:
                        causal_prep(g + 1)

            def phase(p):
                one_pass(p, 0, True, False, True)
                with dve.Fori(1, GROUPS - 1, 1) as g:
                    one_pass(p, g, True, True, True)
                one_pass(p, GROUPS - 1, True, True, False)
                one_pass(p, GROUPS, False, True, False)

            count = [0]

            def step(ins):
                count[0] += 1
                ins.then_inc(route, 1)
                dve.wait_ge(route, count[0])

            def route_tokens():
                for i in range(RING):
                    dve.wait_ge(cau.ring_free[i], (cau.total - i - 1) // RING + 1 + 1)
                for t in range(SEQS):
                    last = ve.max(best[:, t, :], logits[:, t, :])
                step(last)
                for t in range(SEQS):
                    last = ve.max_index(best_at[:, t, :], best[:, t, :], logits[:, t, :])
                step(last)
                ve.tensor_tensor(gap[:, 0, :], best[:, :, 1], best[:, :, 0], ALU.subtract).then_inc(gap_ready, 1)
                step(ve.tensor_copy(choice[:, :, :], best_at[:, :, 0:TOPK].rearrange("p t k -> p k t")))
                chosen = choice[:, :, :].rearrange("p k t -> p (k t)")
                pairs = TOPK * SEQS
                ve.tensor_tensor(hot[:, :, :], number_e[:, :].unsqueeze(1).to_broadcast([128, pairs, EXPERTS]),
                                 chosen.unsqueeze(2).to_broadcast([128, pairs, EXPERTS]),
                                 ALU.is_equal).then_inc(hot_ready, 1)
                dve.wait_ge(ranked, 1)
                dve.wait_ge(hot_ready, 1)
                total = ps_scores[:, 1, :].rearrange("p (t e) -> p t e", e=EXPERTS)
                for e in range(EXPERTS):
                    last = ve.tensor_tensor_scan(rank_e[:, :, e], one_f[:, :], total[:, :, e], 0.0,
                                                 ALU.mult, ALU.add)
                step(last)
                step(ve.tensor_tensor(rank_e[:, :, :], rank_e[:, :, :], total, ALU.subtract))
                step(ve.tensor_tensor(rank_e[:, :, :], rank_e[:, :, :],
                                      ps_scores[:, 0, :].rearrange("p (t e) -> p t e", e=EXPERTS), ALU.add))
                step(ve.tensor_tensor(rank_e[:, :, :], rank_e[:, :, :], hot[:, :, :], ALU.mult))
                ranks = rank[:, :, :].rearrange("p k t -> p (k t)")
                keeps = keep[:, :, :].rearrange("p k t -> p (k t)")
                step(ve.tensor_reduce(ranks, rank_e[:, :, :], AX.X, ALU.add))
                step(ve.tensor_scalar(keeps, ranks, float(CAP), None, ALU.is_lt))
                step(ve.tensor_scalar(slot_f[:, 0, :], keeps, -float(SLOTS), float(SLOTS), ALU.mult, ALU.add))
                step(ve.tensor_tensor(slot_f[:, 0, :], slot_f[:, 0, :], ranks, ALU.add))
                step(ve.scalar_tensor_tensor(out=slot_f[:, 0, :], in0=chosen, scalar=float(CAP),
                                             in1=slot_f[:, 0, :], op0=ALU.mult, op1=ALU.add))
                ve.tensor_copy(put_at[:, :], slot_f[:, 0, :]).then_inc(put_ready, 1)
                step(ve.tensor_scalar(slot_f[:, 1, :], ranks, float(CAP - 1), None, ALU.min))
                step(ve.scalar_tensor_tensor(out=slot_f[:, 2, :], in0=chosen, scalar=float(CAP),
                                             in1=slot_f[:, 1, :], op0=ALU.mult, op1=ALU.add))
                ve.tensor_copy(take_at[:, :], slot_f[:, 2, :]).then_inc(put_ready, 1)
                dve.wait_ge(gap_exp, 1)
                step(ve.tensor_scalar(gap[:, 2, :], gap[:, 1, :], 1.0, None, ALU.add))
                step(ve.reciprocal(weight[:, 0, :], gap[:, 2, :]))
                step(ve.tensor_tensor(weight[:, 1, :], gap[:, 1, :], weight[:, 0, :], ALU.mult))
                step(ve.tensor_tensor(weight[:, :, :], weight[:, :, :], keep[:, :, :], ALU.mult))

            def experts():
                dve.wait_ge(bias_loaded, 16 * (1 + EXPERTS))
                dve.sem_inc(raw_split, 1)

                def split_weights(e):
                    dve.wait_ge(raw_loaded, 48 * e + 48)
                    dve.wait_ge(fc_high, e + 1)
                    ve.tensor_tensor(w_lo[:, :, 0:2, :], raw_fc.rearrange("p c (m n) -> p c m n", m=2),
                                     f(w_hi[:, :, 0:2, :]), ALU.subtract).then_inc(raw_split, 1)

                def split_x(e, c):
                    t0, nt = CHUNKS[c]
                    hl = slice(REST, 128)
                    for t in range(t0, t0 + nt):
                        tok = slice(128 * (t - t0), 128 * (t - t0) + 128)
                        dve.wait_ge(ex_whole, e * CAP_TILES + t + 1)
                        ve.tensor_copy(x_hi[:, :, tok], x_full[:, :, 0:128]).then_inc(ex_high, 1)
                        dve.wait_ge(ex_high, e * CAP_TILES + t + 1)
                        ve.tensor_tensor(x_lo[:, tok], x_full[:, 0, 0:128], f(x_hi[:, 0, tok]), ALU.subtract)
                        ve.tensor_tensor(x_hi[hl, 1, tok], x_full[hl, 1, 0:128], f(x_hi[hl, 1, tok]),
                                         ALU.subtract).then_inc(ex_turn_free[t % 2], 1)

                def add_bias(e, c):
                    t0, nt = CHUNKS[c]
                    for t in range(t0, t0 + nt):
                        i, n = t % 2, e * (CAP_TILES // 2) + t // 2
                        dve.wait_ge(y_full[i], n + 1)
                        o = t % OUT_RING
                        if not (isinstance(e, int) and t < OUT_RING):
                            dve.wait_ge(y_stored[o], e * (16 * CAP_TILES // OUT_RING) + 16 * (t // OUT_RING))
                        ve.tensor_tensor(slot_y[:, o, :], ps_ring[:, i, 0:HID], pj_bias[:, e, :], ALU.add
                                         ).then_inc(y_free[i], 1)

                def expert(e):
                    split_weights(e)
                    split_x(e, 0)
                    split_x(e, 1)
                    add_bias(e, 0)
                    split_x(e, 2)
                    add_bias(e, 1)
                    add_bias(e, 2)

                expert(0)
                with dve.Fori(1, EXPERTS, 1) as e:
                    expert(e)

            def combine():
                for t in range(SEQS + 1):
                    if t < SEQS:
                        o = t % TAKE_RING
                        dve.wait_ge(rows_taken[o], 16 * TOPK * (t // TAKE_RING + 1))
                        ve.scalar_tensor_tensor(out=resid[:, t, :], in0=taken[:, o, 0, :],
                                                scalar=weight[:, 0, t:t + 1], in1=resid[:, t, :],
                                                op0=ALU.mult, op1=ALU.add).then_inc(first_added, 1)
                    if t > 0:
                        b = t - 1
                        dve.wait_ge(first_added, b + 1)
                        ve.scalar_tensor_tensor(out=resid[:, b, :], in0=taken[:, b % TAKE_RING, 1, :],
                                                scalar=weight[:, 1, b:b + 1], in1=resid[:, b, :],
                                                op0=ALU.mult, op1=ALU.add).then_inc(token_done, 1)

            dve.sem_inc(mag.max_done, 2)
            dve.sem_inc(mag.named("emb_affine0"), 1)
            dve.sem_inc(z_used, 2)
            dve.sem_inc(z_kept, 2)
            dve.wait_ge(ident_ready, 1)
            dve.wait_ge(const_loaded, CONST)
            split_weights_low(mag_w_loaded, mag_w_high, mag_w_split, 3)
            dve.wait_ge(mag_w_split, 2)
            negate_imaginary_keys()
            lead = mag.lead_places()
            lay_kinds(0)
            add_positions(0)
            for fl in mag.lead:
                fill(mag, -1, fl, lead[fl])
            embedding_tail(0, lead)
            phase(mag)
            dve.wait_ge(mag.ctx_done, SEQS)
            split_weights_low(cau_w_loaded, cau_w_high, cau_w_split, 2)
            causal_prep(0)
            phase(cau)
            route_tokens()
            experts()
            combine()

        return nc


def kernel(**inputs):
    import numpy as np
    import concourse.bacc as bacc
    from concourse.bass_utils import run_bass_kernel_spmd

    g = lambda name: np.asarray(inputs[name])
    tok, attn, ffn = "L0_tok_", "L0_attn_", "L0_ffn_"

    def by_head(a):
        return a.reshape(HID, HEADS, HEAD_DIM)

    wqr, wqi, wkr, wki, wv = (g(attn + n).T for n in ("Wqr", "Wqi", "Wkr", "Wki", "Wv"))
    pair = lambda a, b: np.concatenate([by_head(a), by_head(b)], axis=2).reshape(HID, 384)
    mag_qk = np.stack([pair(wqr, wqi), pair(wkr, wki), pair(wki, wkr)], axis=1)
    qkv_w, qkv_b = g(ffn + "attn_qkv_w"), g(ffn + "attn_qkv_b")
    pad = lambda a: np.concatenate(
        [a.reshape(-1, HEADS, HEAD_DIM), np.zeros((a.size // HID, HEADS, HEAD_DIM), a.dtype)], axis=2).reshape(-1, 384)
    causal_qk = np.stack([pad(qkv_w[:, 0:HID]), pad(qkv_w[:, HID:2 * HID])], axis=1)
    causal_qk_b = np.concatenate([pad(qkv_b[0:HID]), pad(qkv_b[HID:2 * HID])]).reshape(6, 128).T
    chunks = lambda a: np.stack([a[0:128], np.concatenate([a[128:], a[128:]])], axis=1)
    ln_cols = np.concatenate([chunks(g(ffn + n)) for n in ("ln1_w", "ln1_b", "ln2_w", "ln2_b")], axis=1)
    arrays = {
        "ids": np.stack([g("x"), g("itok_BS_0_4999"), g("pos_BS")]).transpose(2, 0, 1),
        "kinds": np.stack([g("mask_BS_i0_1").reshape(-1)] * 2),
        "word_table": g(tok + "word_table"),
        "domain_table": g(tok + "domain_table"),
        "pos_table": g(tok + "pos_table"),
        "kind_rows": np.concatenate([g(tok + "type_table"), g(tok + "proj_b")[None]]),
        "domain_w": g(tok + "proj_w").T,
        "mag_qk": mag_qk,
        "mag_v": wv,
        "causal_qk": causal_qk,
        "causal_qk_b": causal_qk_b,
        "causal_v": qkv_w[:, 2 * HID:],
        "ln_cols": ln_cols,
        "rows": np.stack([g(tok + "ln_gamma"), g(tok + "ln_beta"), qkv_b[2 * HID:], g(ffn + "attn_proj_b")]),
        "out_w": g(ffn + "attn_proj_w"),
        "gate_w": g(ffn + "w_g"),
        "fc_w": g(ffn + "exp_fc_w"),
        "fc_b": g(ffn + "exp_fc_b").reshape(EXPERTS, FF_CHUNKS, 128).transpose(2, 0, 1),
        "pj_w": g(ffn + "exp_proj_w"),
        "pj_b": g(ffn + "exp_proj_b").reshape(EXPERTS, HID),
    }
    arrays = {name: np.ascontiguousarray(a) for name, a in arrays.items()}
    nc = bacc.Bacc("TRN2", target_bir_lowering=False, num_devices=1)
    args = [nc.dram_tensor(name, list(a.shape), mybir.dt.from_np(a.dtype), kind="ExternalInput").ap()
            for name, a in arrays.items()]
    out = nc.dram_tensor("out", [SEQS, SEQ, HID], F32, kind="ExternalOutput").ap()
    tower_kernel(nc, *args, out)
    r = run_bass_kernel_spmd(nc, [arrays], core_ids=[0])
    return r.results[0]["out"]
```

```python
from contextlib import ExitStack

import concourse.bass as bass
from concourse import mybir

F32 = mybir.dt.float32
F32R = mybir.dt.float32r
BF16 = mybir.dt.bfloat16
I32 = mybir.dt.int32
U32 = mybir.dt.uint32
ALU = mybir.AluOpType
ACT = mybir.ActivationFunctionType
AX = mybir.AxisListType

SEQS, SEQ, HID = 32, 128, 192
REST = HID - 128
TOKENS = SEQS * SEQ
HEADS, HEAD_DIM = 12, 16
GROUP = 4
GROUPS = SEQS // GROUP
BLOCKS = 3
JOBS = GROUP * BLOCKS
EXPERTS, TOPK, FF = 8, 2, 768
FF_CHUNKS = FF // 128
CAP = (TOPK * 5 * TOKENS) // (4 * EXPERTS)
CAP += CAP % 2
SLOTS = EXPERTS * CAP
CAP_TILES = CAP // 128
CHUNKS = [(0, 4), (4, 4), (8, 2)]
MASKED = -1.0e30
WORD_EPS, LN_EPS = 1e-12, 1e-5


PASS_SLOTS = 24
RING = 3


def back_turns(slot):
    fills = [("probT", slot)] if slot < JOBS else []
    if slot >= 4 and (slot - 4) % 3 == 0 and (slot - 4) // 3 < GROUP:
        fills += [("ctx", (slot - 4) // 3)]
    return fills


def back_fills_causal(slot):
    fills = back_turns(slot)
    for s in range(GROUP):
        fills += [("ctxT", s)] if slot == 3 * s + 5 else []
        fills += [("out", s)] if slot == 3 * s + 6 else []
        fills += [("zT", s)] if slot == 3 * s + 9 else []
    fills += [("logits", 0)] if slot == 19 else []
    fills += [("logitsT", 0)] if slot == 20 else []
    return fills


def projections(slot, count):
    return [("proj", k) for k in range(count) if max(0, k - 1) == slot]


def front_fills_magnitude(slot):
    return projections(slot, 9) + ([("value", slot - 14)] if 14 <= slot <= 15 else [])


def front_fills_causal(slot):
    return projections(slot, 6) + ([("value", slot - 14)] if 14 <= slot <= 17 else [])


def prep_fills_embedding(slot):
    fills = [("domT", 0), ("domT", 1)] if slot == 12 else []
    fills += [("embed", 0), ("embed", 1)] if slot == 13 else []
    return fills + prep_fills(slot)


def prep_fills(slot):
    return [("xT", slot - 21)] if 21 <= slot <= 22 else []


class Phase:

    def __init__(self, sem, name, front, back, prep, values_per_fill):
        self.front, self.back, self.prep, self.values_per_fill = front, back, prep, values_per_fill
        self.high_done = sem(f"{name}_high_done")
        self.scores_full = sem(f"{name}_scores_full")
        self.scores_free = sem(f"{name}_scores_free")
        self.max_done = sem(f"{name}_max_done")
        self.neg_max_done = sem(f"{name}_neg_max_done")
        self.exp_done = sem(f"{name}_exp_done")
        self.pv_done = sem(f"{name}_pv_done")
        self.ctx_copied = sem(f"{name}_ctx_copied")
        self.recip_done = sem(f"{name}_recip_done")
        self.ctx_done = sem(f"{name}_ctx_done")
        self.x_ready = sem(f"{name}_x_ready")
        self.step = {}
        self.sem, self.name = sem, name

    def named(self, what):
        if what not in self.step:
            self.step[what] = self.sem(f"{self.name}_{what}")
        return self.step[what]


class Turn:

    def __init__(self, first, front=None, back=None, prep=None, loops=1):
        self.front, self.back, self.prep, self.first = front, back, prep, first
        self.by_slot = [[(role, f) for role, some in (("front", front), ("back", back), ("prep", prep)) if some
                         for f in {"front": some[0].front, "back": some[0].back,
                                   "prep": some[0].prep}[role](slot)]
                        for slot in range(PASS_SLOTS)]
        self.fills = sum(len(fills) for fills in self.by_slot)
        self.loops = loops
        assert loops == 1 or self.fills % RING == 0
        self.end = first + self.fills * loops

    def place(self, k, g):
        n = self.first + k
        return n % RING, n // RING + ((g - 1) * (self.fills // RING) if self.loops > 1 else 0)

    def groups(self, g):
        return [some and (some[0], g + some[1]) for some in (self.front, self.back, self.prep)]

    def schedule(self, g):
        shift = {"front": 0, "back": 1, "prep": -1}
        roles = {"front": self.front, "back": self.back, "prep": self.prep}
        by_slot = [[(roles[role][0], g + roles[role][1] + shift[role], f) for role, f in fills]
                   for fills in self.by_slot]
        flat = [f for fills in self.by_slot for _, f in fills]
        places = {f: self.place(k, g) for k, f in enumerate(flat)}
        places["input"] = self.place(-1, g)
        return by_slot, places


def tower_kernel(nc, ids, kinds, word_table, domain_table, pos_table, kind_rows, domain_w, mag_qk, mag_v,
                 causal_qk, causal_qk_b, causal_v, ln_cols, rows, out_w, gate_w, fc_w, fc_b, pj_w, pj_b, out):
    ctx = ExitStack()
    with ctx:
        def sb(name, shape, dt=F32):
            return ctx.enter_context(nc.sbuf_tensor(name, shape, dt))

        def pb(name, shape):
            return ctx.enter_context(nc.psum_tensor(name, shape, F32))

        def sem(name):
            return ctx.enter_context(nc.semaphore(name))

        slot_in = nc.dram_tensor("slot_in", [SLOTS, HID], F32, kind="Internal").ap()
        slot_out = nc.dram_tensor("slot_out", [SLOTS, HID], F32, kind="Internal").ap()

        ps_scores = pb("ps_scores", [128, 4, 512])
        ps_ctx = pb("ps_ctx", [128, 512])
        ps_ring = pb("ps_ring", [128, RING, 512])

        resid = sb("resid", [128, SEQS, HID])
        xin = sb("xin", [128, SEQS, HID])
        logits = sb("logits", [128, SEQS, EXPERTS])
        ident = sb("ident", [128, 128])
        causal = sb("causal", [128, 128])
        zeros = sb("zeros", [128, HID])
        row_c = sb("row_c", [128, 4, HID])
        ln_c = sb("ln_c", [128, 8])
        half = sb("half", [128, GROUP])
        w_hi = sb("w_hi", [128, 2, 3, 384], F32R)
        w_lo = sb("w_lo", [128, 2, 3, 384], F32R)
        v_hi = sb("v_hi", [128, 2, HID], F32R)
        v_lo = sb("v_lo", [128, 2, HID], F32R)
        qk_b = sb("qk_b", [128, 7])
        xn = sb("xn", [128, GROUP, 256])
        x_hi = sb("x_hi", [128, 2, GROUP * 128], F32R)
        x_lo = sb("x_lo", [128, GROUP * 128], F32R)
        q_hi = sb("q_hi", [128, BLOCKS, GROUP, 128], F32R)
        q_lo = sb("q_lo", [128, BLOCKS, GROUP, 128], F32R)
        k_hi = sb("k_hi", [128, BLOCKS, GROUP, 2, 128], F32R)
        k_lo = sb("k_lo", [128, BLOCKS, GROUP, 2, 128], F32R)
        square = sb("square", [128, 2, 4, 2, 128])
        q_whole = square[:, :, :, :, :].rearrange("p i h m k -> p (i h) m k").rearrange(
            "p (b x) m k -> p b (x m) k", b=4)
        vals = sb("vals", [128, GROUP, HEADS, 32])
        probs = sb("probs", [128, JOBS, 4, 128])
        row_max = sb("row_max", [128, GROUP, HEADS])
        row_root = sb("row_root", [128, GROUP, HEADS])
        neg_max = sb("neg_max", [128, GROUP, HEADS])
        prob_t = sb("prob_t", [128, 2, 4, 128])
        ctx_t = sb("ctx_t", [128, BLOCKS, 128])
        recip = sb("recip", [128, HEADS])
        ctx_n = sb("ctx_n", [128, 256])
        id_all = sb("id_all", [128, 3, SEQS], I32)
        id_now = sb("id_now", [128, 3, GROUP], I32)
        work = sb("work", [128, 4096])
        kind_i = work[0:2, 0:TOKENS].bitcast(I32)
        kind_sc = sb("kind_sc", [2, 2])
        kind_w = sb("kind_w", [3, HID])
        dom_w = sb("dom_w", [128, HID])
        got = sb("got", [128, GROUP * (HID + 128 + HID)])
        got_word = got[:, 0:GROUP * HID].rearrange("p (s d) -> p s d", s=GROUP)
        got_pos = got[:, GROUP * HID:2 * GROUP * HID].rearrange("p (s d) -> p s d", s=GROUP)
        got_dom = got[:, 2 * GROUP * HID:].rearrange("p (s d) -> p s d", s=GROUP)
        stats = sb("stats", [128, GROUP, 6])
        moments = sb("moments", [128, GROUP, 2])
        rstd = sb("rstd", [128, 6, GROUP])
        o_w = sb("o_w", [128, 2, HID])
        g_w = sb("g_w", [128, 2, EXPERTS])
        z = sb("z", [128, 2, HID])
        z_t = sb("z_t", [128, 2, GROUP * 128])
        dom_t = z_t[:, 0, :].rearrange("p (s t) -> p s t", s=GROUP)
        kind_hot = z_t[0:3, 1, :]
        gate_t = work[0:EXPERTS, 1536:2048]
        ctxn_t = work[:, 2048:2304].rearrange("p (c t) -> p c t", c=2)
        out_b = work[:, 2304:2304 + HID]
        x_full = sb("x_full", [128, 2, 256])
        z_stats = sb("z_stats", [128, 6])
        z_moments = sb("z_moments", [128, 2])
        number_e = sb("number_e", [128, EXPERTS])
        below = sb("below", [128, 128], BF16)
        ones_b = sb("ones_b", [128, 128], BF16)
        one_f = sb("one_f", [128, TOPK * SEQS])
        scratch = work[:, 0:1536].rearrange("p (a n) -> p a n", n=256)
        best = scratch[:, 0, :].rearrange("p (t e) -> p t e", e=8)
        best_at = scratch[:, 1, :].bitcast(U32).rearrange("p (t e) -> p t e", e=8)
        choice = sb("choice", [128, TOPK, SEQS])
        hot = scratch[:, 2, :].bitcast(BF16).rearrange("p (t e) -> p t e", e=EXPERTS)
        rank_e = work[:, 768:1280].rearrange("p (t e) -> p t e", e=EXPERTS)
        rank = sb("rank", [128, TOPK, SEQS])
        keep = sb("keep", [128, TOPK, SEQS])
        slot_f = work[:, 1280:1472].rearrange("p (a n) -> p a n", a=3)
        put_at = sb("put_at", [128, TOPK * SEQS], I32)
        take_at = sb("take_at", [128, TOPK * SEQS], I32)
        weight = sb("weight", [128, TOPK, SEQS])
        gap = sb("gap", [128, 3, SEQS])
        fc_bias = sb("fc_bias", [128, EXPERTS, FF_CHUNKS])

        mag = Phase(sem, "mag", front_fills_magnitude, back_turns, prep_fills_embedding, 2)
        cau = Phase(sem, "cau", front_fills_causal, back_fills_causal, prep_fills, 1)
        ring_full = [sem(f"ring_full{i}") for i in range(RING)]
        ring_free = [sem(f"ring_free{i}") for i in range(RING)]
        last = GROUPS - 1
        lead = Turn(0, prep=(mag, 1))
        mag_first = Turn(lead.end, front=(mag, 0), prep=(mag, 1))
        mag_loop = Turn(mag_first.end, front=(mag, 0), back=(mag, -1), prep=(mag, 1), loops=GROUPS - 2)
        mag_last = Turn(mag_loop.end, front=(mag, 0), back=(mag, -1), prep=(cau, -last))
        bridge = Turn(mag_last.end, front=(cau, 0), back=(mag, last), prep=(cau, 1))
        cau_loop = Turn(bridge.end, front=(cau, 0), back=(cau, -1), prep=(cau, 1), loops=GROUPS - 2)
        cau_last = Turn(cau_loop.end, front=(cau, 0), back=(cau, -1))
        tail = Turn(cau_last.end, back=(cau, -1))

        const_loaded = sem("const_loaded")
        const_made = sem("const_made")
        ident_ready = sem("ident_ready")
        wait_ended = sem("wait_ended")
        mag_w_loaded = sem("mag_w_loaded")
        mag_w_high = sem("mag_w_high")
        mag_w_split = sem("mag_w_split")
        cau_w_loaded = sem("cau_w_loaded")
        cau_w_high = sem("cau_w_high")
        cau_w_split = sem("cau_w_split")
        zero_filled = sem("zero_filled")
        id_copied = sem("id_copied")
        word_got = sem("word_got")
        dom_got = sem("dom_got")
        pos_got = sem("pos_got")
        gather_used = sem("gather_used")
        logits_ready = sem("logits_ready")
        z_ready = sem("z_ready")
        z_kept = sem("z_kept")
        z_used = sem("z_used")
        raw = probs[:, :, :, :].rearrange("p j h k -> p (j h k)")

        def raw_weights(m):
            place, n = (raw, 3 * 768) if m == 3 else (work, 2 * 768)
            return (place[:, 0:n].rearrange("p (c m n) -> p c m n", c=2, m=m),
                    place[:, n:n + 2 * HID].rearrange("p (c n) -> p c n", c=2))

        raw_fc = work[:, 0:2 * FF].rearrange("p (c n) -> p c n", c=2)
        pj_w_sb = work[:, 2 * FF:2 * FF + 2 * FF_CHUNKS * HID].rearrange("p (u c n) -> p u c n", u=2, c=FF_CHUNKS)
        pj_bias = got[:, 0:EXPERTS * HID].rearrange("p (e n) -> p e n", e=EXPERTS)
        slot_x = [square[:, i, :, :, :].rearrange("p h m k -> p h (m k)") for i in range(2)] + [xn[:, 0:2, :]]
        hidden = raw.rearrange("p (u f t) -> p u f t", u=2, f=FF_CHUNKS)
        OUT_RING = 5
        slot_y = z_t[:, :, :].rearrange("p c t -> p (c t)")[:, 0:OUT_RING * HID].rearrange(
            "p (t d) -> p t d", t=OUT_RING)
        TAKE_RING = 16
        taken = raw.rearrange("p (r k d) -> p r k d", r=TAKE_RING, k=TOPK)

        ps_x = [ps_ring[:, 2, :], ps_ctx[:, :]]

        route = sem("route")
        hot_ready = sem("hot_ready")
        ranked = sem("ranked")
        gap_ready = sem("gap_ready")
        gap_exp = sem("gap_exp")
        put_ready = sem("put_ready")
        slots_put = sem("slots_put")
        bias_loaded = sem("bias_loaded")
        raw_loaded = sem("raw_loaded")
        raw_split = sem("raw_split")
        fc_high = sem("fc_high")
        pj_loaded = [sem(f"pj_loaded{u}") for u in range(2)]
        pj_used = [sem(f"pj_used{u}") for u in range(2)]
        x_loaded = [sem(f"x_loaded{c}") for c in range(3)]
        x_turned = [sem(f"x_turned{c}") for c in range(3)]
        fc_used = sem("fc_used")
        ex_turn_full = [sem(f"ex_turn_full{i}") for i in range(2)]
        ex_turn_free = [sem(f"ex_turn_free{i}") for i in range(2)]
        ex_whole = sem("ex_whole")
        ex_high = sem("ex_high")
        FC_RING = 3
        fc_full = [sem(f"fc_full{i}") for i in range(FC_RING)]
        gelu_done = [sem(f"gelu_done{i}") for i in range(FC_RING)]
        y_full = [sem(f"y_full{i}") for i in range(2)]
        y_free = [sem(f"y_free{i}") for i in range(2)]
        y_stored = [sem(f"y_stored{i}") for i in range(OUT_RING)]
        rows_taken = [sem(f"rows_taken{i}") for i in range(TAKE_RING)]
        first_added = sem("first_added")
        token_done = sem("token_done")
        out_stored = sem("out_stored")
        blk = ctx.enter_context(nc.Block())

        def apart(eng):
            eng.sem_inc(wait_ended, 1)

        @blk.sync
        def _(sp):
            n = 0

            def load(dst, src, done=const_loaded):
                sp.dma_start(dst, src).then_inc(done, 16)

            load(id_all[:, :, :], ids)
            load(kind_i, kinds)
            load(kind_w[:, :], kind_rows)
            load(dom_w[:, :], domain_w)
            load(ln_c[:, :], ln_cols)
            for i in range(4):
                load(row_c[:, i, :], rows[i:i + 1, :].to_broadcast([128, HID]))
            load(o_w[:, 0, :], out_w[0:128, :])
            load(o_w[0:REST, 1, :], out_w[128:HID, :])
            load(g_w[:, 0, :], gate_w[0:128, :])
            load(g_w[0:REST, 1, :], gate_w[128:HID, :])
            load(qk_b[:, :], causal_qk_b)
            for w_src, v_src, done, after in ((mag_qk, mag_v, mag_w_loaded, None),
                                              (causal_qk, causal_v, cau_w_loaded, mag)):
                m = w_src.shape[1]
                raw_qk, raw_v = raw_weights(m)
                if after is not None:
                    sp.wait_ge(mag.named("kinds_done"), GROUPS)
                load(raw_qk[:, 0, :, :], w_src[0:128, :, :], done)
                load(raw_qk[0:REST, 1, :, :], w_src[128:HID, :, :], done)
                load(raw_qk[REST:128, 1, :, :], w_src[128:HID, :, :], done)
                load(raw_v[:, 0, :], v_src[0:128, :], done)
                load(raw_v[0:REST, 1, :], v_src[128:HID, :], done)
                load(raw_v[REST:128, 1, :], v_src[128:HID, :], done)
                if after is None:
                    sp.wait_ge(const_made, 1)
                    for t in range(SLOTS // 1280):
                        sp.dma_start(slot_in[1280 * t:1280 * (t + 1), :].rearrange("(k p) d -> p k d", p=128),
                                     zeros[:, :].unsqueeze(1).to_broadcast([128, 10, HID])
                                     ).then_inc(zero_filled, 16)

            sp.dma_start(fc_bias[:, :, :], fc_b).then_inc(bias_loaded, 16)
            sp.wait_ge(mag.named("emb_affine0"), GROUPS + 1)
            for e in range(EXPERTS):
                sp.dma_start(pj_bias[:, e, :], pj_b[e:e + 1, :].to_broadcast([128, HID])).then_inc(bias_loaded, 16)
            sp.wait_ge(slots_put, 16 * TOPK * SEQS)
            with sp.Fori(0, EXPERTS // 2, 1) as r:
                for u in range(2):
                    e = r * 2 + u
                    sp.wait_ge(raw_split, e + 1)
                    for dst, rows_ in ((raw_fc[:, 0, :], slice(0, 128)), (raw_fc[0:REST, 1, :], slice(128, HID)),
                                       (raw_fc[REST:128, 1, :], slice(128, HID))):
                        sp.dma_start(dst, fc_w[bass.ds(e, 1), rows_, :].rearrange("e p n -> p (e n)")
                                     ).then_inc(raw_loaded, 16)
                    sp.wait_ge(pj_used[u], r + 1)
                    sp.dma_start(pj_w_sb[:, u, :, :], pj_w[bass.ds(e, 1), :, :].rearrange(
                        "e (c p) n -> p (e c) n", p=128)).then_inc(pj_loaded[u], 16)
                    for c, (t0, nt) in enumerate(CHUNKS):
                        sp.wait_ge(x_turned[c], e + 1)
                        src = slot_in[bass.ds(e * CAP + t0 * 128, nt * 128), :].rearrange("(t p) d -> p t d", p=128)
                        sp.dma_start(slot_x[c][:, :, 0:HID], src).then_inc(x_loaded[c], 16)
                        sp.dma_start(slot_x[c][:, :, HID:256], src[:, :, 128:HID]).then_inc(x_loaded[c], 16)
            for t in range(0, SEQS, 4):
                sp.wait_ge(token_done, t + 4)
                sp.dma_start(out[t:t + 4].rearrange("t p d -> p t d"), resid[:, t:t + 4, :]).then_inc(out_stored, 16)
            sp.wait_ge(out_stored, 16 * (SEQS // 4))
            sp.wait_ge(zero_filled, 16 * (SLOTS // 1280))

        CONST = 14 * 16

        @blk.gpsimd
        def _(pool):
            gp = nc.gpsimd
            gp.memset(zeros[:, :], 0.0).then_inc(const_made, 1)
            gp.memset(half[:, :], -0.5)
            gp.memset(kind_hot[:, :], 1.0)
            gp.memset(ident[:, :], 0.0)
            gp.memset(causal[:, :], 0.0)
            gp.iota(kind_sc[:, 0:1], pattern=[[0, 1]], base=-1, channel_multiplier=2,
                    allow_small_or_imprecise_dtypes=True)
            gp.iota(kind_sc[:, 1:2], pattern=[[0, 1]], base=1, channel_multiplier=-1,
                    allow_small_or_imprecise_dtypes=True)
            gp.memset(below[:, :], 1.0)
            gp.memset(ones_b[:, :], 1.0)
            gp.memset(one_f[:, :], 1.0)
            gp.iota(number_e[:, :], pattern=[[1, EXPERTS]], base=0, channel_multiplier=0,
                    allow_small_or_imprecise_dtypes=True)
            gp.memset(vals[:, :, :, :], 0.0).then_inc(const_made, 1)
            pool.wait_ge(const_made, 2)
            gp.affine_select(out=ident[:, :], in_=ident[:, :], compare_op=ALU.not_equal, fill=1.0, base=0,
                             pattern=[[-1, 128]], channel_multiplier=1)
            gp.affine_select(out=below[:, :], in_=below[:, :], compare_op=ALU.is_gt, fill=0.0, base=0,
                             pattern=[[1, 128]], channel_multiplier=-1)
            gp.affine_select(out=causal[:, :], in_=causal[:, :], compare_op=ALU.is_ge, fill=MASKED, base=0,
                             pattern=[[-1, 128]], channel_multiplier=1)
            gp.memset(vals[:, :, :, HEAD_DIM:HEAD_DIM + 1], 1.0).then_inc(ident_ready, 1)
            pool.wait_ge(const_loaded, CONST)

            def power(n, src, dst, eps, p, name, base):
                k = p.named(name + "_eps")
                gp.tensor_scalar(dst, src, eps, None, ALU.add).then_inc(k, 1)
                pool.wait_ge(k, n + 1)
                gp.tensor_tensor(dst, dst, half[:, 0:dst.shape[1]], ALU.pow).then_inc(p.named(name), 1)

            def gathers(g):
                pool.wait_ge(mag.named("emb_affine0"), g + 1)
                gp.tensor_copy(id_now[:, :, :], id_all[:, :, bass.ds(GROUP * g, GROUP)]).then_inc(id_copied, 1)
                pool.wait_ge(id_copied, g + 1)
                apart(pool)
                for table, dst, done, i in ((domain_table, got_dom, dom_got, 1), (word_table, got_word, word_got, 0),
                                            (pos_table, got_pos, pos_got, 2)):
                    for s in range(GROUP):
                        gp.indirect_dma_start(dst[:, s, :], None, table[:, :],
                                              bass.IndirectOffsetOnAxis(id_now[:, i, s:s + 1], 0)
                                              ).then_inc(done, 16)

            def embedding_norms(g):
                pool.wait_ge(mag.named("emb_moments"), g + 1)
                apart(pool)
                power(g, moments[:, :, 1], rstd[:, 0, :], WORD_EPS, mag, "emb_rstd", 0)
                pool.wait_ge(mag.named("x_moments"), g + 1)
                apart(pool)
                power(g, moments[:, :, 1], rstd[:, 1, :], LN_EPS, mag, "x_rstd", 0)

            def negate_max_roots(g):
                for s in range(GROUP):
                    pool.wait_ge(mag.named("max_root_done"), GROUP * g + s + 1)
                    apart(pool)
                    gp.tensor_scalar(neg_max[:, s, :], row_root[:, s, :], -1.0, None,
                                     ALU.mult).then_inc(mag.neg_max_done, 1)

            def put_tokens():
                pool.wait_ge(put_ready, 1)
                pool.wait_ge(zero_filled, 16 * (SLOTS // 1280))
                pool.wait_ge(z_kept, SEQS + 2)
                for k in range(TOPK):
                    for t in range(SEQS):
                        c = k * SEQS + t
                        gp.indirect_dma_start(slot_in[:, :], bass.IndirectOffsetOnAxis(put_at[:, c:c + 1], 0),
                                              xin[:, t, :], None, bounds_check=SLOTS - 1, oob_is_err=False
                                              ).then_inc(slots_put, 16)

            def store_slots():
                with pool.Fori(0, EXPERTS, 1) as e:
                    for t in range(CAP_TILES):
                        i = t % 2
                        pool.wait_ge(y_free[i], e * (CAP_TILES // 2) + t // 2 + 2)
                        gp.dma_start(slot_out[bass.ds(e * CAP + 128 * t, 128), :], slot_y[:, t % OUT_RING, :]
                                     ).then_inc(y_stored[t % OUT_RING], 16)

            def take_rows():
                for i in range(OUT_RING):
                    pool.wait_ge(y_stored[i], 16 * EXPERTS * CAP_TILES // OUT_RING)
                for t in range(SEQS):
                    if t >= TAKE_RING:
                        pool.wait_ge(token_done, t - TAKE_RING + 1)
                    for k in range(TOPK):
                        c = k * SEQS + t
                        gp.indirect_dma_start(taken[:, t % TAKE_RING, k, :], None, slot_out[:, :],
                                              bass.IndirectOffsetOnAxis(take_at[:, c:c + 1], 0)
                                              ).then_inc(rows_taken[t % TAKE_RING], 16)

            def layer_norm_scales(g):
                n = g
                pool.wait_ge(cau.named("moments"), n + 1)
                apart(pool)
                power(n, moments[:, :, 1], rstd[:, 0, :], LN_EPS, cau, "first_rstd", 0)
                k = cau.named("second_var")
                pool.wait_ge(cau.named("first_rstd"), n + 1)
                gp.tensor_tensor(rstd[:, 2, :], moments[:, :, 1], rstd[:, 0, :], ALU.mult).then_inc(k, 1)
                pool.wait_ge(k, 2 * n + 1)
                gp.tensor_tensor(rstd[:, 3, :], rstd[:, 2, :], rstd[:, 0, :], ALU.mult).then_inc(k, 1)
                pool.wait_ge(k, 2 * n + 2)
                apart(pool)
                power(n, rstd[:, 3, :], rstd[:, 1, :], LN_EPS, cau, "second_rstd", 0)

            def negate_max(g):
                for s in range(GROUP):
                    pool.wait_ge(cau.scores_free, 2 * (JOBS * g + 3 * s + 3) + 2)
                    apart(pool)
                    gp.tensor_scalar(neg_max[:, s, :], row_max[:, s, :], -0.25, None,
                                     ALU.mult).then_inc(cau.neg_max_done, 1)

            def z_scale(g, s):
                n = GROUP * g + s
                pool.wait_ge(cau.named("z_moments"), n + 1)
                apart(pool)
                power(n, z_moments[:, 1:2], rstd[:, 4, 0:1], LN_EPS, cau, "z_rstd", 0)

            def keep_z(g, s):
                n = GROUP * g + s
                pool.wait_ge(z_ready, n + 1)
                gp.tensor_copy(xin[:, n, :], z[:, s % 2, :]).then_inc(z_kept, 1)

            def one_pass(turn, number):
                front, back, prep = turn.groups(number)
                if back and back[0] is cau:
                    for s in range(GROUP):
                        z_scale(back[1], s)
                        keep_z(back[1], s)
                if prep and prep[0] is mag:
                    gathers(prep[1])
                    embedding_norms(prep[1])
                elif prep:
                    layer_norm_scales(prep[1])
                if front:
                    (negate_max_roots if front[0] is mag else negate_max)(front[1])

            one_pass(lead, -1)
            one_pass(mag_first, 0)
            with pool.Fori(1, GROUPS - 1, 1) as g:
                one_pass(mag_loop, g)
            one_pass(mag_last, GROUPS - 1)
            one_pass(bridge, 0)
            with pool.Fori(1, GROUPS - 1, 1) as g:
                one_pass(cau_loop, g)
            one_pass(cau_last, GROUPS - 1)
            one_pass(tail, GROUPS)
            put_tokens()
            store_slots()
            take_rows()

        @blk.tensor
        def _(pe):
            for i in range(RING):
                pe.sem_inc(ring_free[i], 1)
            for p in (mag, cau):
                pe.sem_inc(p.scores_free, 2)
                pe.sem_inc(p.pv_done, 2)
                pe.sem_inc(p.ctx_copied, 1)

            def transpose(dst, src, n=128):
                return pe.transpose(dst, src, ident[0:n, 0:n])

            def split_product(dst, x, w_cols, v):
                pairs = ((x[0], w_cols[0]), (x[0], w_cols[1]), (x[1], w_cols[0]), (x[2], w_cols[2]),
                         (x[2], w_cols[3]))
                for k, (a, w) in enumerate(pairs):
                    lhs, rhs = (a, w) if v else (w, a)
                    last = pe.matmul(dst, lhs, rhs, start=(k == 0), stop=(k == 4))
                return last

            def taken_out(p, d, f, own):
                i, n = d[f]
                if i != own:
                    pe.wait_ge(ring_free[i], n + 2)

            def fill(p, g, f, place, d):
                i, n = place
                kind, s = f
                pe.wait_ge(ring_free[i], n + 1)
                dst = ps_ring[:, i, :]
                if kind == "xT":
                    pe.wait_ge(p.x_ready, GROUP * (g + 1) + 2 * s + 2)
                    for t in range(2):
                        for c in range(2):
                            last = transpose(dst[:, 256 * t + 128 * c:256 * t + 128 * c + 128],
                                             xn[:, 2 * s + t, 128 * c:128 * c + 128])
                elif kind == "proj":
                    m, b = divmod(s, 3)
                    if s == 0:
                        taken_out(p, d, "input", i)
                    col = slice(128 * b, 128 * b + 128)
                    last = split_product(dst, (x_hi[:, 0, :], x_lo[:, :], x_hi[:, 1, :]),
                                         (w_hi[:, 0, m, col], w_lo[:, 0, m, col], w_hi[:, 1, m, col],
                                          w_lo[:, 1, m, col]), False)
                elif kind == "value":
                    for t in range(p.values_per_fill):
                        k = 128 * (p.values_per_fill * s + t)
                        tok = slice(k, k + 128)
                        last = split_product(dst[:, HID * t:HID * t + HID],
                                             (x_hi[:, 0, tok], x_lo[:, tok], x_hi[:, 1, tok]),
                                             (v_hi[:, 0, :], v_lo[:, 0, :], v_hi[:, 1, :], v_lo[:, 1, :]), True)
                elif kind == "domT":
                    pe.wait_ge(dom_got, 16 * GROUP * (g + 1) + 16 * GROUP)
                    for t in range(2):
                        last = transpose(dst[:, 128 * t:128 * t + 128], got_dom[:, 2 * s + t, :])
                elif kind == "embed":
                    taken_out(p, d, ("domT", s), i)
                    pe.wait_ge(p.named("kinds_done"), g + 2)
                    for t in (2 * s, 2 * s + 1):
                        o = HID * (t % 2)
                        pe.matmul(dst[:, o:o + HID], dom_t[:, t, :], dom_w[:, :], start=True, stop=False)
                        last = pe.matmul(dst[:, o:o + HID], kind_hot[:, 128 * t:128 * t + 128], kind_w[:, :],
                                         start=False, stop=True)
                elif kind == "ctxT":
                    pe.wait_ge(p.named("ctx_dup"), GROUP * (g - 1) + s + 1)
                    transpose(dst[:, 0:128], ctx_n[:, 0:128])
                    last = transpose(dst[:, 128:256], ctx_n[:, 128:256])
                elif kind == "out":
                    taken_out(p, d, ("ctxT", s), i)
                    pe.matmul(dst[:, 0:HID], ctxn_t[:, 0, :], o_w[:, 0, :], start=True, stop=False)
                    last = pe.matmul(dst[:, 0:HID], ctxn_t[0:REST, 1, :], o_w[0:REST, 1, :],
                                     start=False, stop=True)
                elif kind == "zT":
                    pe.wait_ge(z_ready, GROUP * (g - 1) + s + 1)
                    transpose(dst[:, 0:128], z[:, s % 2, 0:128])
                    last = transpose(dst[0:REST, 128:256], z[:, s % 2, 128:HID])
                elif kind == "logits":
                    taken_out(p, d, ("zT", GROUP - 1), i)
                    pe.matmul(dst[0:EXPERTS, :], g_w[:, 0, :], z_t[:, 0, :], start=True, stop=False)
                    last = pe.matmul(dst[0:EXPERTS, :], g_w[0:REST, 1, :], z_t[0:REST, 1, :],
                                     start=False, stop=True)
                elif kind == "logitsT":
                    taken_out(p, d, ("logits", s), i)
                    apart(pe)
                    for t in range(GROUP):
                        last = transpose(dst[:, 8 * t:8 * t + 8], gate_t[:, 128 * t:128 * t + 128], EXPERTS)
                elif kind == "probT":
                    pe.wait_ge(p.exp_done, JOBS * (g - 1) + s + 1)
                    for h in range(4):
                        last = transpose(dst[:, 128 * h:128 * h + 128], probs[:, s, h, :])
                elif kind == "ctx":
                    pe.wait_ge(p.ctx_copied, GROUP * (g - 1) + s + 2)
                    for b in range(BLOCKS):
                        last = transpose(dst[:, 128 * b:128 * b + 128], ctx_t[:, b, :])
                last.then_inc(ring_full[i], 1)

            def scores(p, g, j, d):
                s, b = divmod(j, 3)
                if j == 0:
                    taken_out(p, d, ("proj", 8 if p is mag else 5), None)
                width = 256 if p is mag else 128
                for pair in range(2):
                    pe.wait_ge(p.scores_free, 2 * (JOBS * g + j) + pair + 1)
                    products = ((q_hi, k_hi), (q_lo, k_hi), (q_hi, k_lo))[::1 if p is mag else 2]
                    for a, (q, k) in enumerate(products):
                        for h in (2 * pair, 2 * pair + 1):
                            r = slice(32 * h, 32 * h + 32)
                            keys = k[r, b, s, :, :].rearrange("p m k -> p (m k)")[:, 0:width]
                            last = pe.matmul(ps_scores[:, h, 0:width], q[r, b, s, :], keys,
                                             start=(a == 0), stop=(a == len(products) - 1))
                    last.then_inc(p.scores_full, 1)

            def values_product(p, gb, j, d):
                s, b = divmod(j, 3)
                i, n = d[("probT", j)]
                pe.wait_ge(ring_free[i], n + 2)
                if b == 0:
                    pe.wait_ge(p.ctx_copied, GROUP * gb + s + 1)
                for h in range(4):
                    last = pe.matmul(ps_ctx[32 * h:32 * h + 32, 128 * b:128 * b + 128],
                                     vals[:, s, 4 * b + h, :], prob_t[:, j % 2, h, :],
                                     start=True, stop=True, skip_group_check=True)
                last.then_inc(p.pv_done, 1)

            def one_pass(turn, number):
                front, back, prep = turn.groups(number)
                by_slot, places = turn.schedule(number)
                for slot in range(PASS_SLOTS):
                    for p, g, f in by_slot[slot]:
                        fill(p, g, f, places[f], places)
                    if back and 1 <= slot <= JOBS:
                        values_product(*back, slot - 1, places)
                    if front and slot >= JOBS:
                        scores(*front, slot - JOBS, places)


            pe.wait_ge(ident_ready, 1)
            pe.wait_ge(const_loaded, CONST)
            one_pass(lead, -1)
            pe.wait_ge(mag_w_split, 4)
            one_pass(mag_first, 0)
            with pe.Fori(1, GROUPS - 1, 1) as g:
                one_pass(mag_loop, g)
            one_pass(mag_last, GROUPS - 1)
            pe.wait_ge(cau_w_split, 2)
            one_pass(bridge, 0)
            with pe.Fori(1, GROUPS - 1, 1) as g:
                one_pass(cau_loop, g)
            one_pass(cau_last, GROUPS - 1)
            one_pass(tail, GROUPS)
            pe.wait_ge(hot_ready, 1)
            hots = hot[:, :, :].rearrange("p t e -> p (t e)")
            pe.matmul(ps_scores[:, 0, :], below[:, :], hots, start=True, stop=True)
            pe.matmul(ps_scores[:, 1, :], ones_b[:, :], hots, start=True, stop=True).then_inc(ranked, 1)

            for i in range(2):
                pe.sem_inc(ex_turn_free[i], 1)
                pe.sem_inc(y_free[i], 1)
                pe.sem_inc(pj_used[i], 1)
            for i in range(FC_RING):
                pe.sem_inc(gelu_done[i], 1)
            for c in range(3):
                pe.sem_inc(x_turned[c], 1)

            def turn_x(e, c):
                t0, nt = CHUNKS[c]
                pe.wait_ge(x_loaded[c], 32 * e + 32)
                for t in range(t0, t0 + nt):
                    i, n = t % 2, e * (CAP_TILES // 2) + t // 2
                    pe.wait_ge(ex_turn_free[i], n + 1)
                    transpose(ps_x[i][:, 0:128], slot_x[c][:, t - t0, 0:128])
                    transpose(ps_x[i][:, 128:256], slot_x[c][:, t - t0, 128:256]).then_inc(ex_turn_full[i], 1)
                pe.transpose(ps_scores[0:32, 3, 0:128], slot_x[c][:, nt - 1, 0:32], ident[:, :]
                             ).then_inc(x_turned[c], 1)

            def first_layer(e, c):
                t0, nt = CHUNKS[c]
                if c == 0:
                    pe.wait_ge(raw_split, e + 2)
                for t in (t0 + nt - 2, t0 + nt - 1):
                    pe.wait_ge(ex_turn_free[t % 2], e * (CAP_TILES // 2) + t // 2 + 2)
                tok = slice(0, 128 * nt)
                for f_ in range(FF_CHUNKS):
                    i = f_ % FC_RING
                    pe.wait_ge(gelu_done[i], e * 6 + 2 * c + f_ // FC_RING + 1)
                    col = slice(128 * f_, 128 * f_ + 128)
                    wh = w_hi[:, :, :, :].rearrange("p c m n -> p c (m n)")
                    wl = w_lo[:, :, :, :].rearrange("p c m n -> p c (m n)")
                    split_product(ps_scores[:, i, tok], (x_hi[:, 0, tok], x_lo[:, tok], x_hi[:, 1, tok]),
                                  (wh[:, 0, col], wl[:, 0, col], wh[:, 1, col], wl[:, 1, col]), False
                                  ).then_inc(fc_full[i], 1)

            def second_layer(r, u, e, c):
                t0, nt = CHUNKS[c]
                if c == 0:
                    pe.wait_ge(pj_loaded[u], 16 * r + 16)
                for i in range(FC_RING):
                    pe.wait_ge(gelu_done[i], e * 6 + 2 * c + 3)
                for t in range(t0, t0 + nt):
                    i, n = t % 2, e * (CAP_TILES // 2) + t // 2
                    pe.wait_ge(y_free[i], n + 1)
                    tok = slice(128 * (t - t0), 128 * (t - t0) + 128)
                    for f_ in range(FF_CHUNKS):
                        last = pe.matmul(ps_ring[:, i, 0:HID], hidden[:, c % 2, f_, tok], pj_w_sb[:, u, f_, :],
                                         start=(f_ == 0), stop=(f_ == FF_CHUNKS - 1))
                    last.then_inc(y_full[i], 1)

            with pe.Fori(0, EXPERTS // 2, 1) as r:
                for u in range(2):
                    e = r * 2 + u
                    turn_x(e, 0)
                    first_layer(e, 0)
                    turn_x(e, 1)
                    second_layer(r, u, e, 0)
                    first_layer(e, 1)
                    turn_x(e, 2)
                    second_layer(r, u, e, 1)
                    first_layer(e, 2)
                    pe.transpose(ps_scores[0:32, 3, 0:128], ident[:, 0:32], ident[:, :]).then_inc(fc_used, 1)
                    second_layer(r, u, e, 2)
                    pe.transpose(ps_scores[0:32, 3, 0:128], ident[:, 0:32], ident[:, :]).then_inc(pj_used[u], 1)

        @blk.scalar
        def _(act):
            sc = nc.scalar

            def split_weights_high(loaded, done, m):
                act.wait_ge(loaded, 6 * 16)
                raw_qk, raw_v = raw_weights(m)
                sc.activation(w_hi[:, :, 0:m, :], raw_qk, ACT.Copy).then_inc(done, 1)
                sc.activation(v_hi[:, :, :], raw_v, ACT.Copy).then_inc(done, 1)

            def fill(p, f, place, d):
                i, n = place
                kind, s = f
                src = ps_ring[:, i, :]
                if kind in ("embed", "out", "logitsT", "probT", "ctx"):
                    return
                act.wait_ge(ring_full[i], n + 1)
                tok = slice(128 * s, 128 * s + 128)
                if kind == "xT":
                    two = slice(256 * s, 256 * s + 256)
                    by_chunk = src.rearrange("p (s c t) -> p c s t", s=2, c=2)
                    if p is mag:
                        sc.activation(x_hi[:, :, two].rearrange("p c (s t) -> p c s t", s=2), by_chunk,
                                      ACT.Copy).then_inc(p.high_done, 1)
                    else:
                        if s > 0:
                            fi, fn = d[("xT", s - 1)]
                            act.wait_ge(ring_free[fi], fn + 2)
                        for c in range(2):
                            last = sc.activation(x_full[:, c, :].rearrange("p (s t) -> p s t", s=2),
                                                 by_chunk[:, c, :, :], ACT.Identity, bias=ln_c[:, 2 + c:3 + c],
                                                 scale=ln_c[:, c:c + 1])
                        last.then_inc(p.high_done, 1)
                elif kind == "proj":
                    m, b = divmod(s, 3)
                    dst = q_hi[:, b, :, :] if m == 0 else k_hi[:, b, :, m - 1, :]
                    if m == 0 and p is cau:
                        dst = q_whole[:, b, :, :]
                    view = src.rearrange("p (s k) -> p s k", s=GROUP)
                    if p is mag:
                        sc.activation(dst, view, ACT.Copy).then_inc(p.high_done, 1)
                    else:
                        sc.activation(dst, view, ACT.Identity, bias=qk_b[:, s:s + 1]).then_inc(p.high_done, 1)
                elif kind == "value":
                    if p is mag:
                        sc.activation(vals[:, 2 * s:2 * s + 2, :, 0:HEAD_DIM],
                                      src[:, 0:2 * HID].rearrange("p (s h d) -> p s h d", s=2, h=HEADS),
                                      ACT.Copy).then_inc(ring_free[i], 1)
                elif kind == "domT":
                    sc.activation(dom_t[:, 2 * s:2 * s + 2, :], src[:, 0:256].rearrange("p (s t) -> p s t", s=2),
                                  ACT.Copy).then_inc(ring_free[i], 1)
                elif kind == "ctxT":
                    sc.activation(ctxn_t, src[:, 0:256].rearrange("p (c t) -> p c t", c=2),
                                  ACT.Copy).then_inc(ring_free[i], 1)
                elif kind == "zT":
                    sc.activation(z_t[:, 0, tok], src[:, 0:128], ACT.Identity, bias=ln_c[:, 6:7],
                                  scale=ln_c[:, 4:5]).then_inc(z_used, 1)
                    sc.activation(z_t[0:REST, 1, tok], src[0:REST, 128:256], ACT.Identity,
                                  bias=ln_c[0:REST, 7:8], scale=ln_c[0:REST, 5:6]).then_inc(ring_free[i], 1)
                elif kind == "logits":
                    sc.activation(gate_t, src[0:EXPERTS, :],
                                  ACT.Copy).then_inc(ring_free[i], 1)

            def exps(p, gb, j):
                s, b = divmod(j, 3)
                if b == 0:
                    act.wait_ge(p.neg_max_done, GROUP * gb + s + 1)
                    if p is mag:
                        act.wait_ge(mag.named("root_done"), GROUP * gb + s + 1)
                for h in range(4):
                    last = sc.activation(probs[:, j, h, :], probs[:, j, h, :], ACT.Exp,
                                         bias=neg_max[:, s, 4 * b + h:4 * b + h + 1],
                                         scale=1.0 if p is mag else 0.25)
                last.then_inc(p.exp_done, 1)

            def squares(g, j):
                act.wait_ge(mag.max_done, JOBS * g + j + 1)
                for pair in range(2):
                    act.wait_ge(mag.scores_full, 2 * (JOBS * g + j) + pair + 1)
                    h = slice(2 * pair, 2 * pair + 2)
                    sc.activation(square[:, j % 2, h, :, :].rearrange("p h m k -> p h (m k)"),
                                  ps_scores[:, h, 0:256], ACT.Square).then_inc(mag.scores_free, 1)

            def roots(g, s):
                act.wait_ge(mag.max_done, JOBS * g + 3 * s + 3 + 2)
                sc.activation(row_root[:, s, :], row_max[:, s, :], ACT.Sqrt, scale=1.0 / HEAD_DIM
                              ).then_inc(mag.named("max_root_done"), 1)
                sc.activation(probs[:, 3 * s:3 * s + 3, :, :], probs[:, 3 * s:3 * s + 3, :, :],
                              ACT.Sqrt, scale=1.0 / HEAD_DIM).then_inc(mag.named("root_done"), 1)

            def copy_ctx(p, gb, s):
                act.wait_ge(p.pv_done, JOBS * gb + 3 * s + 3 + 2)
                sc.activation(ctx_t[:, :, :], ps_ctx[:, 0:384].rearrange("p (b q) -> p b q", b=3),
                              ACT.Copy).then_inc(p.ctx_copied, 1)

            def one_pass(turn, number):
                front, back, prep = turn.groups(number)
                by_slot, places = turn.schedule(number)
                for slot in range(PASS_SLOTS):
                    fills = list(by_slot[slot])
                    if slot == 0 and back:
                        if front:
                            p, _, f = fills.pop(0)
                            fill(p, f, places[f], places)
                        exps(*back, 0)
                    if back and slot + 1 < JOBS:
                        exps(*back, slot + 1)
                    for p, _, f in fills:
                        fill(p, f, places[f], places)
                    if back and slot >= 3 and slot % 3 == 0 and slot // 3 <= GROUP:
                        copy_ctx(*back, slot // 3 - 1)
                    if front and front[0] is mag and slot >= JOBS:
                        j = slot - JOBS
                        squares(front[1], j)
                        if j >= 4 and (j - 4) % 3 == 0:
                            roots(front[1], (j - 4) // 3)
                    if turn is mag_last and slot == 18:
                        split_weights_high(cau_w_loaded, cau_w_high, 2)
                if front and front[0] is mag:
                    roots(front[1], 3)

            act.wait_ge(const_loaded, CONST)
            split_weights_high(mag_w_loaded, mag_w_high, 3)
            one_pass(lead, -1)
            one_pass(mag_first, 0)
            with act.Fori(1, GROUPS - 1, 1) as g:
                one_pass(mag_loop, g)
            one_pass(mag_last, GROUPS - 1)
            one_pass(bridge, 0)
            with act.Fori(1, GROUPS - 1, 1) as g:
                one_pass(cau_loop, g)
            one_pass(cau_last, GROUPS - 1)
            one_pass(tail, GROUPS)
            act.wait_ge(gap_ready, 1)
            sc.activation(gap[:, 1, :], gap[:, 0, :], ACT.Exp).then_inc(gap_exp, 1)

            def expert_weights_high(e):
                act.wait_ge(raw_loaded, 48 * e + 48)
                act.wait_ge(fc_used, e + 1)
                sc.activation(w_hi[:, :, 0:2, :], raw_fc.rearrange("p c (m n) -> p c m n", m=2),
                              ACT.Copy).then_inc(fc_high, 1)

            def whole_x(e, c):
                t0, nt = CHUNKS[c]
                for t in range(t0, t0 + nt):
                    i, n = t % 2, e * (CAP_TILES // 2) + t // 2
                    act.wait_ge(ex_turn_full[i], n + 1)
                    if t > 0:
                        act.wait_ge(ex_turn_free[(t - 1) % 2], e * (CAP_TILES // 2) + (t - 1) // 2 + 2)
                    else:
                        act.wait_ge(ex_turn_free[1], e * (CAP_TILES // 2) + 1)
                    sc.activation(x_full[:, 0, 0:128], ps_x[i][:, 0:128], ACT.Identity, bias=ln_c[:, 6:7],
                                  scale=ln_c[:, 4:5])
                    sc.activation(x_full[:, 1, 0:128], ps_x[i][:, 128:256], ACT.Identity, bias=ln_c[:, 7:8],
                                  scale=ln_c[:, 5:6]).then_inc(ex_whole, 1)

            def gelus(e, c):
                nt = CHUNKS[c][1]
                for f_ in range(FF_CHUNKS):
                    i = f_ % FC_RING
                    act.wait_ge(fc_full[i], e * 6 + 2 * c + f_ // FC_RING + 1)
                    apart(act)
                    sc.activation(hidden[:, c % 2, f_, 0:128 * nt], ps_scores[:, i, 0:128 * nt], ACT.Gelu,
                                  bias=fc_bias[:, e, f_:f_ + 1]).then_inc(gelu_done[i], 1)

            act.sem_inc(fc_used, 1)
            act.wait_ge(bias_loaded, 16 * (1 + EXPERTS))
            with act.Fori(0, EXPERTS, 1) as e:
                expert_weights_high(e)
                whole_x(e, 0)
                gelus(e, 0)
                whole_x(e, 1)
                gelus(e, 1)
                whole_x(e, 2)
                gelus(e, 2)

        @blk.vector
        def _(dve):
            ve = nc.vector
            f = lambda a: a.bitcast(F32)

            def split_weights_low(loaded, high, done, m):
                dve.wait_ge(loaded, 6 * 16)
                dve.wait_ge(high, 2)
                raw_qk, raw_v = raw_weights(m)
                ve.tensor_tensor(w_lo[:, :, 0:m, :], raw_qk, f(w_hi[:, :, 0:m, :]),
                                 ALU.subtract).then_inc(done, 1)
                ve.tensor_tensor(v_lo[:, :, :], raw_v, f(v_hi[:, :, :]), ALU.subtract).then_inc(done, 1)

            def negate_imaginary_keys():
                for w in (w_hi, w_lo):
                    v = w[:, :, 2, :].rearrange("p c (h x) -> p c h x", x=32)[:, :, :, 0:HEAD_DIM]
                    ve.tensor_scalar(v, f(v), -1.0, None, ALU.mult).then_inc(mag_w_split, 1)

            def fill(p, g, fl, place):
                i, n = place
                kind, s = fl
                src = ps_ring[:, i, :]
                free = ring_free[i]
                two = slice(256 * s, 256 * s + 256)
                hl = slice(REST, 128)
                if kind == "xT":
                    dve.wait_ge(p.high_done, high_count(p, g + 1 if kind == "xT" else g, fl))
                    if p is mag:
                        by_chunk = src.rearrange("p (s c t) -> p c s t", s=2, c=2)
                        halves = lambda a: a.rearrange("p (s t) -> p s t", s=2)
                        ve.tensor_tensor(halves(x_lo[:, two]), by_chunk[:, 0, :, :], halves(f(x_hi[:, 0, two])),
                                         ALU.subtract)
                        ve.tensor_tensor(halves(x_hi[hl, 1, two]), by_chunk[hl, 1, :, :],
                                         halves(f(x_hi[hl, 1, two])), ALU.subtract).then_inc(free, 1)
                    else:
                        ve.tensor_copy(x_hi[:, :, two], x_full[:, :, :]).then_inc(p.named("x_high"), 1)
                        dve.wait_ge(p.named("x_high"), 2 * (g + 1) + s + 1)
                        ve.tensor_tensor(x_lo[:, two], x_full[:, 0, :], f(x_hi[:, 0, two]), ALU.subtract)
                        ve.tensor_tensor(x_hi[hl, 1, two], x_full[hl, 1, :], f(x_hi[hl, 1, two]),
                                         ALU.subtract).then_inc(free, 1)
                elif kind == "proj":
                    dve.wait_ge(p.high_done, high_count(p, g + 1 if kind == "xT" else g, fl))
                    m, b = divmod(s, 3)
                    if m == 0:
                        lo, hi = q_lo[:, b, :, :], q_hi[:, b, :, :]
                    else:
                        lo, hi = k_lo[:, b, :, m - 1, :], k_hi[:, b, :, m - 1, :]
                    view = src.rearrange("p (s k) -> p s k", s=GROUP)
                    if p is mag:
                        ve.tensor_tensor(lo, view, f(hi), ALU.subtract).then_inc(free, 1)
                    elif m == 0:
                        whole = q_whole[:, b, :, :]
                        ve.tensor_copy(lo, whole).then_inc(p.named("q_high"), 1)
                        dve.wait_ge(p.named("q_high"), 3 * g + b + 1)
                        ve.scalar_tensor_tensor(out=hi, in0=f(lo), scalar=qk_b[:, 6:7], in1=whole,
                                                op0=ALU.mult, op1=ALU.add).then_inc(free, 1)
                    else:
                        ve.scalar_tensor_tensor(out=lo, in0=view, scalar=qk_b[:, s:s + 1], in1=f(hi),
                                                op0=ALU.add, op1=ALU.subtract).then_inc(free, 1)
                elif kind == "value" and p is cau:
                    dve.wait_ge(ring_full[i], n + 1)
                    ve.tensor_tensor(vals[:, s, :, 0:HEAD_DIM],
                                     src[:, 0:HID].rearrange("p (h d) -> p h d", h=HEADS),
                                     row_c[:, 2, :].rearrange("p (h d) -> p h d", h=HEADS),
                                     ALU.add).then_inc(free, 1)
                elif kind == "embed":
                    dve.wait_ge(ring_full[i], n + 1)
                    pair = got_word[:, 2 * s:2 * s + 2, :]
                    ve.tensor_tensor(pair, src[:, 0:2 * HID].rearrange("p (s d) -> p s d", s=2), pair,
                                     ALU.add).then_inc(free, 1)
                elif kind == "probT":
                    dve.wait_ge(ring_full[i], n + 1)
                    dve.wait_ge(p.pv_done, JOBS * (g - 1) + s + 1)
                    ve.tensor_copy(prob_t[:, s % 2, :, :], src.rearrange("p (h q) -> p h q", h=4)
                                   ).then_inc(free, 1)
                elif kind == "ctx":
                    t = GROUP * (g - 1) + s
                    dve.wait_ge(ring_full[i], n + 1)
                    v = src[:, 0:384].rearrange("p (h x) -> p h x", x=32)
                    ve.reciprocal(recip[:, :], v[:, :, HEAD_DIM]).then_inc(p.recip_done, 1)
                    dve.wait_ge(p.recip_done, t + 1)
                    ve.tensor_tensor(ctx_n[:, 0:HID].rearrange("p (h d) -> p h d", h=HEADS), v[:, :, 0:HEAD_DIM],
                                     recip[:, :].unsqueeze(2).to_broadcast([128, HEADS, HEAD_DIM]),
                                     ALU.mult).then_inc(free, 1)
                    dve.wait_ge(free, n + 2)
                    if p is mag:
                        ve.tensor_tensor(resid[:, t, :], resid[:, t, :], ctx_n[:, 0:HID], ALU.add
                                         ).then_inc(p.ctx_done, 1)
                    else:
                        ve.tensor_copy(ctx_n[:, HID:256], ctx_n[:, 128:HID]).then_inc(p.named("ctx_dup"), 1)
                elif kind == "out":
                    t = GROUP * (g - 1) + s
                    dve.wait_ge(ring_full[i], n + 1)
                    ve.tensor_tensor(out_b, src[:, 0:HID], row_c[:, 3, :], ALU.add).then_inc(free, 1)
                    dve.wait_ge(free, n + 2)
                    ve.tensor_tensor(xin[:, t, :], xin[:, t, :], out_b, ALU.add
                                     ).then_inc(p.named("layer_sum"), 1)
                    ve.tensor_tensor(resid[:, t, :], resid[:, t, :], out_b, ALU.add)
                    dve.wait_ge(p.named("layer_sum"), t + 1)
                    apart(dve)
                    ve.bn_stats(z_stats[:, :], xin[:, t, :]).then_inc(p.named("z_stats"), 1)
                    dve.wait_ge(p.named("z_stats"), t + 1)
                    apart(dve)
                    ve.bn_aggr(z_moments[:, :], z_stats[:, :]).then_inc(p.named("z_moments"), 1)
                elif kind == "logitsT":
                    dve.wait_ge(ring_full[i], n + 1)
                    ve.tensor_copy(logits[:, bass.ds(GROUP * (g - 1), GROUP), :],
                                   src[:, 0:GROUP * EXPERTS].rearrange("p (t e) -> p t e", t=GROUP)
                                   ).then_inc(free, 1)

            def high_count(p, g, fl):
                kind, s = fl
                per = 2 + (9 if p is mag else 6)
                return per * g + (s if kind == "xT" else 2 + s) + 1

            def normalise_z(p, gb, s):
                t = GROUP * gb + s
                dve.wait_ge(p.named("z_rstd"), t + 1)
                dve.wait_ge(p.named("z_moments"), t + 1)
                dve.wait_ge(z_used, t + 1)
                dve.wait_ge(z_kept, t + 1)
                ve.tensor_scalar(z[:, s % 2, :], xin[:, t, :], z_moments[:, 0:1], rstd[:, 4, 0:1],
                                 ALU.subtract, ALU.mult).then_inc(z_ready, 1)

            def maxima(p, g, j):
                s, b = divmod(j, 3)
                for pair in range(2):
                    if p is mag:
                        dve.wait_ge(mag.scores_free, 2 * (JOBS * g + j) + pair + 1 + 2)
                    else:
                        dve.wait_ge(cau.scores_full, 2 * (JOBS * g + j) + pair + 1)
                    apart(dve)
                    for h in (2 * pair, 2 * pair + 1):
                        if p is mag:
                            a, c = square[:, j % 2, h, 0, :], square[:, j % 2, h, 1, :]
                        else:
                            a, c = ps_scores[:, h, 0:128], causal[:, :]
                        last = ve.tensor_tensor_reduce(out=probs[:, j, h, :], in0=a, in1=c, scale=1.0,
                                                       scalar=-3.0e38, op0=ALU.add, op1=ALU.max,
                                                       accum_out=row_max[:, s, 4 * b + h:4 * b + h + 1])
                    if p is cau:
                        last.then_inc(cau.scores_free, 1)
                if p is mag:
                    last.then_inc(p.max_done, 1)

            def lay_kinds(g):
                ve.tensor_scalar(kind_hot[0:2, :], kind_i[:, bass.ds(512 * g, 512)], kind_sc[:, 0:1],
                                 kind_sc[:, 1:2], ALU.mult, ALU.add).then_inc(mag.named("kinds_done"), 1)

            def add_positions(g):
                dve.wait_ge(word_got, 16 * GROUP * (g + 1))
                dve.wait_ge(pos_got, 16 * GROUP * (g + 1))
                ve.tensor_tensor(got_word[:, :, :], got_word[:, :, :], got_pos[:, :, :], ALU.add
                                 ).then_inc(mag.named("pos_added"), 1)
                dve.wait_ge(mag.named("pos_added"), g + 1)

            def group_moments(p, src, g, name):
                for s in range(GROUP):
                    last = ve.bn_stats(stats[:, s, :], src(s))
                last.then_inc(p.named(name + "_stats"), 1)
                dve.wait_ge(p.named(name + "_stats"), g + 1)
                apart(dve)
                for s in range(GROUP):
                    last = ve.bn_aggr(moments[:, s, :], stats[:, s, :])
                last.then_inc(p.named(name), 1)

            def scale_tile(dst, src, s, r):
                return ve.tensor_scalar(dst, src, moments[:, s, 0:1], rstd[:, r, s:s + 1], ALU.subtract, ALU.mult)

            def dup_view(a):
                return a.unsqueeze(1).to_broadcast([128, 2, REST])

            def embedding_step(g, slot, places):
                tiles = resid[:, bass.ds(GROUP * g, GROUP), :]
                if slot == 11:
                    lay_kinds(g)
                elif slot == 12:
                    add_positions(g)
                elif slot == 14:
                    i, n = places[("embed", 1)]
                    dve.wait_ge(ring_free[i], n + 2)
                    apart(dve)
                    group_moments(mag, lambda s: got_word[:, s, :], g, "emb_moments")
                elif slot == 15:
                    dve.wait_ge(mag.named("emb_moments"), g + 1)
                    dve.wait_ge(mag.named("emb_rstd"), g + 1)
                    for s in range(GROUP):
                        last = scale_tile(got_word[:, s, :], got_word[:, s, :], s, 0)
                    last.then_inc(mag.named("emb_scaled"), 1)
                elif slot in (16, 17):
                    i_row, op, src = ((0, ALU.mult, got_word[:, :, :]), (1, ALU.add, tiles))[slot - 16]
                    dve.wait_ge(mag.named("emb_affine0" if i_row else "emb_scaled"), g + 1 + i_row)
                    ve.tensor_tensor(tiles, src, row_c[:, i_row, :].unsqueeze(1).to_broadcast([128, GROUP, HID]),
                                     op).then_inc(mag.named(f"emb_affine{i_row}"), 1)
                elif slot == 18:
                    dve.wait_ge(mag.named("emb_affine1"), g + 1)
                    apart(dve)
                    group_moments(mag, lambda s: resid[:, GROUP * g + s, :], g, "x_moments")
                elif slot in (19, 20):
                    if slot == 19:
                        dve.wait_ge(mag.named("x_moments"), g + 1)
                        dve.wait_ge(mag.named("x_rstd"), g + 1)
                    for s in (2 * (slot - 19), 2 * (slot - 19) + 1):
                        t = GROUP * g + s
                        scale_tile(xn[:, s, 0:128], resid[:, t, 0:128], s, 1)
                        scale_tile(xn[:, s, 128:256].rearrange("p (c d) -> p c d", c=2),
                                   dup_view(resid[:, t, 128:HID]), s, 1).then_inc(mag.x_ready, 1)

            def causal_input_step(g, slot):
                if slot == 16:
                    if isinstance(g, int):
                        dve.wait_ge(mag.ctx_done, GROUP * (g + 1))
                    group_moments(cau, lambda s: resid[:, GROUP * g + s, :], g, "moments")
                elif slot == 18:
                    dve.wait_ge(cau.named("moments"), g + 1)
                    dve.wait_ge(cau.named("first_rstd"), g + 1)
                    k = cau.named("x_in")
                    for s in range(GROUP):
                        t = GROUP * g + s
                        last = scale_tile(xin[:, t, :], resid[:, t, :], s, 0)
                    last.then_inc(k, 1)
                    dve.wait_ge(k, g + 1)
                    tiles = bass.ds(GROUP * g, GROUP)
                    ve.tensor_tensor(resid[:, tiles, :], resid[:, tiles, :], xin[:, tiles, :], ALU.add)
                elif slot == 20:
                    dve.wait_ge(cau.named("second_rstd"), g + 1)
                    for s in range(GROUP):
                        t = GROUP * g + s
                        r = rstd[:, 1, s:s + 1]
                        ve.tensor_scalar(xn[:, s, 0:128], xin[:, t, 0:128], r, None, ALU.mult)
                        ve.tensor_scalar(xn[:, s, 128:256].rearrange("p (c d) -> p c d", c=2),
                                         dup_view(xin[:, t, 128:HID]), r, None, ALU.mult).then_inc(cau.x_ready, 1)

            def one_pass(turn, number):
                front, back, prep = turn.groups(number)
                by_slot, places = turn.schedule(number)
                for slot in range(PASS_SLOTS):
                    for p, g, fl in by_slot[slot]:
                        fill(p, g, fl, places[fl])
                    if back and back[0] is cau and slot >= 7 and (slot - 7) % 3 == 0 and (slot - 7) // 3 < GROUP:
                        normalise_z(*back, (slot - 7) // 3)
                    if front and slot >= JOBS:
                        maxima(*front, slot - JOBS)
                    if turn is mag_last and slot == 18:
                        split_weights_low(cau_w_loaded, cau_w_high, cau_w_split, 2)
                    if prep and prep[0] is mag:
                        embedding_step(prep[1], slot, places)
                    elif prep:
                        causal_input_step(prep[1], slot)

            count = [0]

            def step(ins):
                count[0] += 1
                ins.then_inc(route, 1)
                dve.wait_ge(route, count[0])

            def route_tokens():
                for i in range(RING):
                    dve.wait_ge(ring_free[i], (tail.end - i - 1) // RING + 1 + 1)
                for t in range(SEQS):
                    last = ve.max(best[:, t, :], logits[:, t, :])
                step(last)
                for t in range(SEQS):
                    last = ve.max_index(best_at[:, t, :], best[:, t, :], logits[:, t, :])
                step(last)
                ve.tensor_tensor(gap[:, 0, :], best[:, :, 1], best[:, :, 0], ALU.subtract).then_inc(gap_ready, 1)
                step(ve.tensor_copy(choice[:, :, :], best_at[:, :, 0:TOPK].rearrange("p t k -> p k t")))
                chosen = choice[:, :, :].rearrange("p k t -> p (k t)")
                pairs = TOPK * SEQS
                ve.tensor_tensor(hot[:, :, :], number_e[:, :].unsqueeze(1).to_broadcast([128, pairs, EXPERTS]),
                                 chosen.unsqueeze(2).to_broadcast([128, pairs, EXPERTS]),
                                 ALU.is_equal).then_inc(hot_ready, 1)
                dve.wait_ge(ranked, 1)
                dve.wait_ge(hot_ready, 1)
                total = ps_scores[:, 1, :].rearrange("p (t e) -> p t e", e=EXPERTS)
                for e in range(EXPERTS):
                    last = ve.tensor_tensor_scan(rank_e[:, :, e], one_f[:, :], total[:, :, e], 0.0,
                                                 ALU.mult, ALU.add)
                step(last)
                step(ve.tensor_tensor(rank_e[:, :, :], rank_e[:, :, :], total, ALU.subtract))
                step(ve.tensor_tensor(rank_e[:, :, :], rank_e[:, :, :],
                                      ps_scores[:, 0, :].rearrange("p (t e) -> p t e", e=EXPERTS), ALU.add))
                step(ve.tensor_tensor(rank_e[:, :, :], rank_e[:, :, :], hot[:, :, :], ALU.mult))
                ranks = rank[:, :, :].rearrange("p k t -> p (k t)")
                keeps = keep[:, :, :].rearrange("p k t -> p (k t)")
                step(ve.tensor_reduce(ranks, rank_e[:, :, :], AX.X, ALU.add))
                step(ve.tensor_scalar(keeps, ranks, float(CAP), None, ALU.is_lt))
                step(ve.tensor_scalar(slot_f[:, 0, :], keeps, -float(SLOTS), float(SLOTS), ALU.mult, ALU.add))
                step(ve.tensor_tensor(slot_f[:, 0, :], slot_f[:, 0, :], ranks, ALU.add))
                step(ve.scalar_tensor_tensor(out=slot_f[:, 0, :], in0=chosen, scalar=float(CAP),
                                             in1=slot_f[:, 0, :], op0=ALU.mult, op1=ALU.add))
                ve.tensor_copy(put_at[:, :], slot_f[:, 0, :]).then_inc(put_ready, 1)
                step(ve.tensor_scalar(slot_f[:, 1, :], ranks, float(CAP - 1), None, ALU.min))
                step(ve.scalar_tensor_tensor(out=slot_f[:, 2, :], in0=chosen, scalar=float(CAP),
                                             in1=slot_f[:, 1, :], op0=ALU.mult, op1=ALU.add))
                ve.tensor_copy(take_at[:, :], slot_f[:, 2, :]).then_inc(put_ready, 1)
                dve.wait_ge(gap_exp, 1)
                step(ve.tensor_scalar(gap[:, 2, :], gap[:, 1, :], 1.0, None, ALU.add))
                step(ve.reciprocal(weight[:, 0, :], gap[:, 2, :]))
                step(ve.tensor_tensor(weight[:, 1, :], gap[:, 1, :], weight[:, 0, :], ALU.mult))
                step(ve.tensor_tensor(weight[:, :, :], weight[:, :, :], keep[:, :, :], ALU.mult))

            def experts():
                dve.wait_ge(bias_loaded, 16 * (1 + EXPERTS))
                dve.sem_inc(raw_split, 1)

                def split_weights(e):
                    dve.wait_ge(raw_loaded, 48 * e + 48)
                    dve.wait_ge(fc_high, e + 1)
                    ve.tensor_tensor(w_lo[:, :, 0:2, :], raw_fc.rearrange("p c (m n) -> p c m n", m=2),
                                     f(w_hi[:, :, 0:2, :]), ALU.subtract).then_inc(raw_split, 1)

                def split_x(e, c):
                    t0, nt = CHUNKS[c]
                    hl = slice(REST, 128)
                    for t in range(t0, t0 + nt):
                        tok = slice(128 * (t - t0), 128 * (t - t0) + 128)
                        dve.wait_ge(ex_whole, e * CAP_TILES + t + 1)
                        ve.tensor_copy(x_hi[:, :, tok], x_full[:, :, 0:128]).then_inc(ex_high, 1)
                        dve.wait_ge(ex_high, e * CAP_TILES + t + 1)
                        ve.tensor_tensor(x_lo[:, tok], x_full[:, 0, 0:128], f(x_hi[:, 0, tok]), ALU.subtract)
                        ve.tensor_tensor(x_hi[hl, 1, tok], x_full[hl, 1, 0:128], f(x_hi[hl, 1, tok]),
                                         ALU.subtract).then_inc(ex_turn_free[t % 2], 1)

                def add_bias(e, c):
                    t0, nt = CHUNKS[c]
                    for t in range(t0, t0 + nt):
                        i, n = t % 2, e * (CAP_TILES // 2) + t // 2
                        dve.wait_ge(y_full[i], n + 1)
                        o = t % OUT_RING
                        if not (isinstance(e, int) and t < OUT_RING):
                            dve.wait_ge(y_stored[o], e * (16 * CAP_TILES // OUT_RING) + 16 * (t // OUT_RING))
                        ve.tensor_tensor(slot_y[:, o, :], ps_ring[:, i, 0:HID], pj_bias[:, e, :], ALU.add
                                         ).then_inc(y_free[i], 1)

                def expert(e):
                    split_weights(e)
                    split_x(e, 0)
                    split_x(e, 1)
                    add_bias(e, 0)
                    split_x(e, 2)
                    add_bias(e, 1)
                    add_bias(e, 2)

                expert(0)
                with dve.Fori(1, EXPERTS, 1) as e:
                    expert(e)

            def combine():
                for t in range(SEQS + 1):
                    if t < SEQS:
                        o = t % TAKE_RING
                        dve.wait_ge(rows_taken[o], 16 * TOPK * (t // TAKE_RING + 1))
                        ve.scalar_tensor_tensor(out=resid[:, t, :], in0=taken[:, o, 0, :],
                                                scalar=weight[:, 0, t:t + 1], in1=resid[:, t, :],
                                                op0=ALU.mult, op1=ALU.add).then_inc(first_added, 1)
                    if t > 0:
                        b = t - 1
                        dve.wait_ge(first_added, b + 1)
                        ve.scalar_tensor_tensor(out=resid[:, b, :], in0=taken[:, b % TAKE_RING, 1, :],
                                                scalar=weight[:, 1, b:b + 1], in1=resid[:, b, :],
                                                op0=ALU.mult, op1=ALU.add).then_inc(token_done, 1)

            dve.sem_inc(mag.max_done, 2)
            dve.sem_inc(mag.named("emb_affine0"), 1)
            dve.sem_inc(z_used, 2)
            dve.sem_inc(z_kept, 2)
            dve.wait_ge(ident_ready, 1)
            dve.wait_ge(const_loaded, CONST)
            split_weights_low(mag_w_loaded, mag_w_high, mag_w_split, 3)
            dve.wait_ge(mag_w_split, 2)
            negate_imaginary_keys()
            one_pass(lead, -1)
            one_pass(mag_first, 0)
            with dve.Fori(1, GROUPS - 1, 1) as g:
                one_pass(mag_loop, g)
            one_pass(mag_last, GROUPS - 1)
            one_pass(bridge, 0)
            dve.wait_ge(mag.ctx_done, SEQS)
            with dve.Fori(1, GROUPS - 1, 1) as g:
                one_pass(cau_loop, g)
            one_pass(cau_last, GROUPS - 1)
            one_pass(tail, GROUPS)
            route_tokens()
            experts()
            combine()

        return nc


def kernel(**inputs):
    import numpy as np
    import concourse.bacc as bacc
    from concourse.bass_utils import run_bass_kernel_spmd

    g = lambda name: np.asarray(inputs[name])
    tok, attn, ffn = "L0_tok_", "L0_attn_", "L0_ffn_"

    def by_head(a):
        return a.reshape(HID, HEADS, HEAD_DIM)

    wqr, wqi, wkr, wki, wv = (g(attn + n).T for n in ("Wqr", "Wqi", "Wkr", "Wki", "Wv"))
    pair = lambda a, b: np.concatenate([by_head(a), by_head(b)], axis=2).reshape(HID, 384)
    mag_qk = np.stack([pair(wqr, wqi), pair(wkr, wki), pair(wki, wkr)], axis=1)
    qkv_w, qkv_b = g(ffn + "attn_qkv_w"), g(ffn + "attn_qkv_b")
    twice = lambda a: np.concatenate(
        [a.reshape(-1, HEADS, HEAD_DIM)] * 2, axis=2).reshape(-1, 384)
    causal_qk = np.stack([twice(qkv_w[:, 0:HID]), twice(qkv_w[:, HID:2 * HID])], axis=1)
    causal_qk_b = np.concatenate([twice(qkv_b[0:HID]), twice(qkv_b[HID:2 * HID])]).reshape(6, 128).T
    low_rows = -(np.arange(128) % (2 * HEAD_DIM) // HEAD_DIM).astype(causal_qk_b.dtype)[:, None]
    causal_qk_b = np.concatenate([causal_qk_b, low_rows], axis=1)
    chunks = lambda a: np.stack([a[0:128], np.concatenate([a[128:], a[128:]])], axis=1)
    ln_cols = np.concatenate([chunks(g(ffn + n)) for n in ("ln1_w", "ln1_b", "ln2_w", "ln2_b")], axis=1)
    arrays = {
        "ids": np.stack([g("x"), g("itok_BS_0_4999"), g("pos_BS")]).transpose(2, 0, 1),
        "kinds": np.stack([g("mask_BS_i0_1").reshape(-1)] * 2),
        "word_table": g(tok + "word_table"),
        "domain_table": g(tok + "domain_table"),
        "pos_table": g(tok + "pos_table"),
        "kind_rows": np.concatenate([g(tok + "type_table"), g(tok + "proj_b")[None]]),
        "domain_w": g(tok + "proj_w").T,
        "mag_qk": mag_qk,
        "mag_v": wv,
        "causal_qk": causal_qk,
        "causal_qk_b": causal_qk_b,
        "causal_v": qkv_w[:, 2 * HID:],
        "ln_cols": ln_cols,
        "rows": np.stack([g(tok + "ln_gamma"), g(tok + "ln_beta"), qkv_b[2 * HID:], g(ffn + "attn_proj_b")]),
        "out_w": g(ffn + "attn_proj_w"),
        "gate_w": g(ffn + "w_g"),
        "fc_w": g(ffn + "exp_fc_w"),
        "fc_b": g(ffn + "exp_fc_b").reshape(EXPERTS, FF_CHUNKS, 128).transpose(2, 0, 1),
        "pj_w": g(ffn + "exp_proj_w"),
        "pj_b": g(ffn + "exp_proj_b").reshape(EXPERTS, HID),
    }
    arrays = {name: np.ascontiguousarray(a) for name, a in arrays.items()}
    nc = bacc.Bacc("TRN2", target_bir_lowering=False, num_devices=1)
    args = [nc.dram_tensor(name, list(a.shape), mybir.dt.from_np(a.dtype), kind="ExternalInput").ap()
            for name, a in arrays.items()]
    out = nc.dram_tensor("out", [SEQS, SEQ, HID], F32, kind="ExternalOutput").ap()
    tower_kernel(nc, *args, out)
    r = run_bass_kernel_spmd(nc, [arrays], core_ids=[0])
    return r.results[0]["out"]
```

```python
from contextlib import ExitStack

import concourse.bass as bass
from concourse import mybir

F32 = mybir.dt.float32
F32R = mybir.dt.float32r
BF16 = mybir.dt.bfloat16
I32 = mybir.dt.int32
U32 = mybir.dt.uint32
ALU = mybir.AluOpType
ACT = mybir.ActivationFunctionType
AX = mybir.AxisListType

SEQS, SEQ, HID = 32, 128, 192
REST = HID - 128
TOKENS = SEQS * SEQ
HEADS, HEAD_DIM = 12, 16
GROUP = 4
GROUPS = SEQS // GROUP
BLOCKS = 3
JOBS = GROUP * BLOCKS
EXPERTS, TOPK, FF = 8, 2, 768
FF_CHUNKS = FF // 128
CAP = (TOPK * 5 * TOKENS) // (4 * EXPERTS)
CAP += CAP % 2
SLOTS = EXPERTS * CAP
CAP_TILES = CAP // 128
CHUNKS = [(0, 4), (4, 4), (8, 2)]
MASKED = -1.0e30
WORD_EPS, LN_EPS = 1e-12, 1e-5


PASS_SLOTS = 24
RING = 3


def back_turns(slot):
    fills = [("probT", slot)] if slot < JOBS else []
    if slot >= 4 and (slot - 4) % 3 == 0 and (slot - 4) // 3 < GROUP:
        fills += [("ctx", (slot - 4) // 3)]
    return fills


def back_fills_causal(slot):
    fills = back_turns(slot)
    for s in range(GROUP):
        fills += [("ctxT", s)] if slot == 3 * s + 5 else []
        fills += [("out", s)] if slot == 3 * s + 6 else []
        fills += [("zT", s)] if slot == 3 * s + 9 else []
    fills += [("logits", 0)] if slot == 19 else []
    fills += [("logitsT", 0)] if slot == 20 else []
    return fills


def projections(slot, count):
    return [("proj", k) for k in range(count) if max(0, k - 2) == slot]


def front_fills_magnitude(slot):
    return projections(slot, 9) + ([("value", slot - 14)] if 14 <= slot <= 15 else [])


def front_fills_causal(slot):
    return projections(slot, 6) + ([("value", slot - 14)] if 14 <= slot <= 17 else [])


def prep_fills_embedding(slot):
    fills = [("domT", 0), ("domT", 1)] if slot == 12 else []
    fills += [("embed", 0), ("embed", 1)] if slot == 13 else []
    return fills + prep_fills(slot)


def prep_fills(slot):
    return [("xT", slot - 21)] if 21 <= slot <= 22 else []


class Phase:

    def __init__(self, sem, name, front, back, prep, values_per_fill):
        self.front, self.back, self.prep, self.values_per_fill = front, back, prep, values_per_fill
        self.high_done = sem(f"{name}_high_done")
        self.scores_full = sem(f"{name}_scores_full")
        self.scores_free = sem(f"{name}_scores_free")
        self.max_done = sem(f"{name}_max_done")
        self.neg_max_done = sem(f"{name}_neg_max_done")
        self.exp_done = sem(f"{name}_exp_done")
        self.pv_done = sem(f"{name}_pv_done")
        self.ctx_copied = sem(f"{name}_ctx_copied")
        self.recip_done = sem(f"{name}_recip_done")
        self.ctx_done = sem(f"{name}_ctx_done")
        self.x_ready = sem(f"{name}_x_ready")
        self.step = {}
        self.sem, self.name = sem, name

    def named(self, what):
        if what not in self.step:
            self.step[what] = self.sem(f"{self.name}_{what}")
        return self.step[what]


class Turn:

    def __init__(self, first, front=None, back=None, prep=None, loops=1):
        self.front, self.back, self.prep, self.first = front, back, prep, first
        self.by_slot = [[(role, f) for role, some in (("front", front), ("back", back), ("prep", prep)) if some
                         for f in {"front": some[0].front, "back": some[0].back,
                                   "prep": some[0].prep}[role](slot)]
                        for slot in range(PASS_SLOTS)]
        self.fills = sum(len(fills) for fills in self.by_slot)
        self.loops = loops
        assert loops == 1 or self.fills % RING == 0
        self.end = first + self.fills * loops

    def place(self, k, g):
        n = self.first + k
        return n % RING, n // RING + ((g - 1) * (self.fills // RING) if self.loops > 1 else 0)

    def groups(self, g):
        return [some and (some[0], g + some[1]) for some in (self.front, self.back, self.prep)]

    def schedule(self, g):
        shift = {"front": 0, "back": 1, "prep": -1}
        roles = {"front": self.front, "back": self.back, "prep": self.prep}
        by_slot = [[(roles[role][0], g + roles[role][1] + shift[role], f) for role, f in fills]
                   for fills in self.by_slot]
        flat = [f for fills in self.by_slot for _, f in fills]
        places = {f: self.place(k, g) for k, f in enumerate(flat)}
        places["input"] = self.place(-1, g)
        return by_slot, places


def tower_kernel(nc, ids, kinds, word_table, domain_table, pos_table, kind_rows, domain_w, mag_qk, mag_v,
                 causal_qk, causal_qk_b, causal_v, ln_cols, rows, out_w, gate_w, fc_w, fc_b, pj_w, pj_b, out):
    ctx = ExitStack()
    with ctx:
        def sb(name, shape, dt=F32):
            return ctx.enter_context(nc.sbuf_tensor(name, shape, dt))

        def pb(name, shape):
            return ctx.enter_context(nc.psum_tensor(name, shape, F32))

        def sem(name):
            return ctx.enter_context(nc.semaphore(name))

        token_in = nc.dram_tensor("token_in", [TOKENS, 256], F32, kind="Internal").ap()
        token_out = nc.dram_tensor("token_out", [TOPK * TOKENS, HID], F32, kind="Internal").ap()

        ps_scores = pb("ps_scores", [128, 4, 512])
        ps_ctx = pb("ps_ctx", [128, 512])
        ps_ring = pb("ps_ring", [128, RING, 512])

        resid = sb("resid", [128, SEQS, HID])
        xin = sb("xin", [128, SEQS, HID])
        logits = sb("logits", [128, SEQS, EXPERTS])
        ident = sb("ident", [128, 128])
        causal = sb("causal", [128, 128])
        zeros = sb("zeros", [128, HID])
        row_c = sb("row_c", [128, 4, HID])
        ln_c = sb("ln_c", [128, 8])
        half = sb("half", [128, GROUP])
        w_hi = sb("w_hi", [128, 2, 3, 384], F32R)
        w_lo = sb("w_lo", [128, 2, 3, 384], F32R)
        v_hi = sb("v_hi", [128, 2, HID], F32R)
        v_lo = sb("v_lo", [128, 2, HID], F32R)
        qk_b = sb("qk_b", [128, 6])
        xn = sb("xn", [128, GROUP, 256])
        x_hi = sb("x_hi", [128, 2, GROUP * 128], F32R)
        x_lo = sb("x_lo", [128, GROUP * 128], F32R)
        q_hi = sb("q_hi", [128, BLOCKS, GROUP, 128], F32R)
        q_lo = sb("q_lo", [128, BLOCKS, GROUP, 128], F32R)
        k_hi = sb("k_hi", [128, BLOCKS, GROUP, 2, 128], F32R)
        k_lo = sb("k_lo", [128, BLOCKS, GROUP, 2, 128], F32R)
        square = sb("square", [128, 2, 4, 2, 128])
        vals = sb("vals", [128, GROUP, HEADS, 32])
        probs = sb("probs", [128, JOBS, 4, 128])
        row_max = sb("row_max", [128, GROUP, HEADS])
        row_root = sb("row_root", [128, GROUP, HEADS])
        neg_max = sb("neg_max", [128, GROUP, HEADS])
        prob_t = sb("prob_t", [128, 2, 4, 128])
        ctx_t = sb("ctx_t", [128, BLOCKS, 128])
        recip = sb("recip", [128, HEADS])
        ctx_n = sb("ctx_n", [128, 256])
        id_all = sb("id_all", [128, 3, SEQS], I32)
        id_now = sb("id_now", [128, 3, GROUP], I32)
        work = sb("work", [128, 4096])
        kind_i = work[0:2, 0:TOKENS].bitcast(I32)
        kind_sc = sb("kind_sc", [2, 2])
        kind_w = sb("kind_w", [3, HID])
        dom_w = sb("dom_w", [128, HID])
        got = sb("got", [128, GROUP * (HID + 128 + HID)])
        got_word = got[:, 0:GROUP * HID].rearrange("p (s d) -> p s d", s=GROUP)
        got_pos = got[:, GROUP * HID:2 * GROUP * HID].rearrange("p (s d) -> p s d", s=GROUP)
        got_dom = got[:, 2 * GROUP * HID:].rearrange("p (s d) -> p s d", s=GROUP)
        cau_q = square[:, :, :, :, :].rearrange("p i h m k -> p (i h m k)")[:, 0:BLOCKS * GROUP * 128].rearrange(
            "p (b s k) -> p b s k", b=BLOCKS, s=GROUP)
        cau_k = got[:, 0:BLOCKS * GROUP * 128].rearrange("p (b s k) -> p b s k", b=BLOCKS, s=GROUP)
        stats = sb("stats", [128, GROUP, 6])
        moments = sb("moments", [128, GROUP, 2])
        rstd = sb("rstd", [128, 6, GROUP])
        o_w = sb("o_w", [128, 2, HID])
        g_w = sb("g_w", [128, 2, EXPERTS])
        z = sb("z", [128, 2, HID])
        z_t = sb("z_t", [128, 2, GROUP * 128])
        dom_t = z_t[:, 0, :].rearrange("p (s t) -> p s t", s=GROUP)
        kind_hot = z_t[0:3, 1, :]
        gate_t = work[0:EXPERTS, 1536:2048]
        ctxn_t = work[:, 2048:2304].rearrange("p (c t) -> p c t", c=2)
        out_b = work[:, 2304:2304 + HID]
        x_full = sb("x_full", [128, 2, 256])
        z_stats = sb("z_stats", [128, 6])
        z_moments = sb("z_moments", [128, 2])
        number = work[:, 3840:3968]
        below = sb("below", [128, 128], BF16)
        ones_b = sb("ones_b", [128, 128], BF16)
        one_f = sb("one_f", [128, TOPK * SEQS])
        token_no = work[:, 1472:1536]
        scratch = work[:, 0:1536].rearrange("p (a n) -> p a n", n=256)
        best = scratch[:, 0, :].rearrange("p (t e) -> p t e", e=8)
        best_at = scratch[:, 1, :].bitcast(U32).rearrange("p (t e) -> p t e", e=8)
        choice = sb("choice", [128, TOPK, SEQS])
        hot = scratch[:, 2, :].bitcast(BF16).rearrange("p (t e) -> p t e", e=EXPERTS)
        rank_e = work[:, 768:1280].rearrange("p (t e) -> p t e", e=EXPERTS)
        rank = sb("rank", [128, TOPK, SEQS])
        keep = sb("keep", [128, TOPK, SEQS])
        slot_f = work[:, 1280:1472].rearrange("p (a n) -> p a n", a=3)
        at_i = scratch[:, 0, :].bitcast(I32).rearrange("p (a n) -> p a n", a=4)
        at_f = scratch[:, 1, :].rearrange("p (a n) -> p a n", a=4)
        LOW, HIGH = 128, SLOTS // 128
        PAIRS_AT_ONCE, HOT_RING = 4, 3
        low_hot = q_hi[:, :, :, :].rearrange("p b s k -> p (b s k)").rearrange(
            "p (r c n) -> p r c n", r=HOT_RING, c=PAIRS_AT_ONCE)
        high_hot = q_lo[:, :, :, :].rearrange("p b s k -> p (b s k)")[:, 0:HOT_RING * PAIRS_AT_ONCE * HIGH].rearrange(
            "p (r c n) -> p r c n", r=HOT_RING, c=PAIRS_AT_ONCE)
        slots_now = sb("slots_now", [128, 2, 2, CAP_TILES], I32)
        high_one = xn[:, :, :].rearrange("p s d -> p (s d)")[:, 0:HOT_RING * PAIRS_AT_ONCE * HIGH].rearrange(
            "p (r c n) -> p r c n", r=HOT_RING, c=PAIRS_AT_ONCE)
        of_slot = scratch[:, 2, 0:240].rearrange("p (a n) -> p a n", a=3)
        slot_src = sb("slot_src", [128, HIGH], I32)
        slot_dst = sb("slot_dst", [128, HIGH], I32)
        weight = sb("weight", [128, TOPK, SEQS])
        gap = sb("gap", [128, 3, SEQS])
        fc_bias = sb("fc_bias", [128, EXPERTS, FF_CHUNKS])

        mag = Phase(sem, "mag", front_fills_magnitude, back_turns, prep_fills_embedding, 2)
        cau = Phase(sem, "cau", front_fills_causal, back_fills_causal, prep_fills, 1)
        ring_full = [sem(f"ring_full{i}") for i in range(RING)]
        ring_free = [sem(f"ring_free{i}") for i in range(RING)]
        last = GROUPS - 1
        lead = Turn(0, prep=(mag, 1))
        mag_first = Turn(lead.end, front=(mag, 0), prep=(mag, 1))
        mag_loop = Turn(mag_first.end, front=(mag, 0), back=(mag, -1), prep=(mag, 1), loops=GROUPS - 2)
        mag_last = Turn(mag_loop.end, front=(mag, 0), back=(mag, -1), prep=(cau, -last))
        bridge = Turn(mag_last.end, front=(cau, 0), back=(mag, last), prep=(cau, 1))
        cau_loop = Turn(bridge.end, front=(cau, 0), back=(cau, -1), prep=(cau, 1), loops=GROUPS - 2)
        cau_last = Turn(cau_loop.end, front=(cau, 0), back=(cau, -1))
        tail = Turn(cau_last.end, back=(cau, -1))

        const_loaded = sem("const_loaded")
        ids_loaded = sem("ids_loaded")
        const_made = sem("const_made")
        ident_ready = sem("ident_ready")
        wait_ended = sem("wait_ended")
        mag_w_loaded = sem("mag_w_loaded")
        mag_w_high = sem("mag_w_high")
        mag_w_split = sem("mag_w_split")
        cau_w_loaded = sem("cau_w_loaded")
        cau_w_high = sem("cau_w_high")
        cau_w_split = sem("cau_w_split")
        zero_filled = sem("zero_filled")
        id_copied = sem("id_copied")
        word_got = sem("word_got")
        dom_got = sem("dom_got")
        pos_got = sem("pos_got")
        z_ready = sem("z_ready")
        z_kept = sem("z_kept")
        z_used = sem("z_used")
        raw = probs[:, :, :, :].rearrange("p j h k -> p (j h k)")

        def raw_weights(m):
            place, n = (raw, 3 * 768) if m == 3 else (work, 2 * 768)
            return (place[:, 0:n].rearrange("p (c m n) -> p c m n", c=2, m=m),
                    place[:, n:n + 2 * HID].rearrange("p (c n) -> p c n", c=2))

        raw_fc = vals[:, :, :, :].rearrange("p s h d -> p (s h d)").rearrange("p (c n) -> p c n", c=2)
        fc_hi = k_hi[:, :, :, :, :].rearrange("p b s m k -> p (b s m k)").rearrange("p (u c n) -> p u c n", u=2, c=2)
        fc_lo = k_lo[:, :, :, :, :].rearrange("p b s m k -> p (b s m k)").rearrange("p (u c n) -> p u c n", u=2, c=2)
        pj_w_sb = work[:, 2 * FF:2 * FF + 2 * FF_CHUNKS * HID].rearrange("p (u c n) -> p u c n", u=2, c=FF_CHUNKS)
        pj_bias = got[:, 0:EXPERTS * HID].rearrange("p (e n) -> p e n", e=EXPERTS)
        slot_x = [square[:, i, :, :, :].rearrange("p h m k -> p h (m k)") for i in range(2)] + [xn[:, 0:2, :]]
        hidden = raw.rearrange("p (u f t) -> p u f t", u=2, f=FF_CHUNKS)
        OUT_RING = 5
        slot_y = z_t[:, :, :].rearrange("p c t -> p (c t)")[:, 0:OUT_RING * HID].rearrange(
            "p (t d) -> p t d", t=OUT_RING)
        TAKE_TILES, TAKE_RING = 4, 4
        taken = raw.rearrange("p (r k t d) -> p r k t d", r=TAKE_RING, k=TOPK, t=TAKE_TILES)

        ps_x = [ps_ring[:, 2, :], ps_ctx[:, :]]
        ps_y = [ps_ring[:, 0, :], ps_ring[:, 1, :], ps_scores[:, 3, :]]
        Y_RING = len(ps_y)
        Y_USES = [len(range(i, CAP_TILES, Y_RING)) for i in range(Y_RING)]

        def y_place(e, t):
            return t % Y_RING, e * Y_USES[t % Y_RING] + t // Y_RING

        TURNS = [len(range(i, CAP_TILES // 2, 2)) for i in range(2)]

        def turn_place(e, m):
            return m % 2, e * TURNS[m % 2] + m // 2


        route = sem("route")
        hot_ready = sem("hot_ready")
        ranked = sem("ranked")
        gap_ready = sem("gap_ready")
        gap_exp = sem("gap_exp")
        ones_made = sem("ones_made")
        hots_made = sem("hots_made")
        hots_used = sem("hots_used")
        map_ready = sem("map_ready")
        rows_stored = sem("rows_stored")
        number_made = sem("number_made")
        src_copied = sem("src_copied")
        dst_copied = sem("dst_copied")
        bias_loaded = sem("bias_loaded")
        raw_loaded = sem("raw_loaded")
        raw_split = sem("raw_split")
        fc_high = sem("fc_high")
        pj_loaded = [sem(f"pj_loaded{u}") for u in range(2)]
        pj_used = [sem(f"pj_used{u}") for u in range(2)]
        x_loaded = [sem(f"x_loaded{c}") for c in range(3)]
        ex_turn_full = [sem(f"ex_turn_full{i}") for i in range(2)]
        ex_turn_free = [sem(f"ex_turn_free{i}") for i in range(2)]
        ex_whole = sem("ex_whole")
        ex_high = sem("ex_high")
        FC_RING = 3
        fc_full = [sem(f"fc_full{i}") for i in range(FC_RING)]
        gelu_done = [sem(f"gelu_done{i}") for i in range(FC_RING)]
        y_full = [sem(f"y_full{i}") for i in range(Y_RING)]
        y_free = [sem(f"y_free{i}") for i in range(Y_RING)]
        y_stored = [sem(f"y_stored{i}") for i in range(OUT_RING)]
        rows_taken = [sem(f"rows_taken{i}") for i in range(TAKE_RING)]
        first_added = sem("first_added")
        token_done = sem("token_done")
        out_stored = sem("out_stored")
        CONST = 13 * 16
        ZERO_FILLS = TOPK * TOKENS // 1024
        WARM = {slot: 4 if slot >= 20 else 2 for slot in range(JOBS + 2, PASS_SLOTS)}
        blk = ctx.enter_context(nc.Block())

        def apart(eng):
            eng.sem_inc(wait_ended, 1)

        @blk.sync
        def _(sp):
            def load(dst, src, done=const_loaded):
                sp.dma_start(dst, src).then_inc(done, 16)

            load(id_all[:, :, :], ids, ids_loaded)
            load(kind_i, kinds)
            load(kind_w[:, :], kind_rows)
            load(dom_w[:, :], domain_w)
            load(ln_c[:, :], ln_cols)
            for i in range(4):
                load(row_c[:, i, :], rows[i:i + 1, :].to_broadcast([128, HID]))
            load(o_w[:, 0, :], out_w[0:128, :])
            load(o_w[0:REST, 1, :], out_w[128:HID, :])
            load(g_w[:, 0, :], gate_w[0:128, :])
            load(g_w[0:REST, 1, :], gate_w[128:HID, :])
            load(qk_b[:, :], causal_qk_b)
            for w_src, v_src, done, after in ((mag_qk, mag_v, mag_w_loaded, None),
                                              (causal_qk, causal_v, cau_w_loaded, mag)):
                m = w_src.shape[1]
                raw_qk, raw_v = raw_weights(m)
                if after is not None:
                    sp.wait_ge(const_made, 1)
                    sp.wait_ge(mag.named("kinds_done"), 2)
                    for t in range(ZERO_FILLS):
                        sp.dma_start(token_out[1024 * t:1024 * (t + 1), :].rearrange("(k p) d -> p k d", p=128),
                                     zeros[:, :].unsqueeze(1).to_broadcast([128, 8, HID])
                                     ).then_inc(zero_filled, 16)
                    sp.wait_ge(mag.named("kinds_done"), GROUPS)
                load(raw_qk[:, 0, :, :], w_src[0:128, :, :], done)
                load(raw_qk[0:REST, 1, :, :], w_src[128:HID, :, :], done)
                load(raw_qk[REST:128, 1, :, :], w_src[128:HID, :, :], done)
                load(raw_v[:, 0, :], v_src[0:128, :], done)
                load(raw_v[0:REST, 1, :], v_src[128:HID, :], done)
                load(raw_v[REST:128, 1, :], v_src[128:HID, :], done)
            sp.dma_start(fc_bias[:, :, :], fc_b).then_inc(bias_loaded, 16)
            with sp.Fori(0, GROUPS, 1) as g:
                sp.wait_ge(z_kept, GROUP * g + GROUP + 2)
                rows_ = token_in[bass.ds(GROUP * 128 * g, GROUP * 128), :].rearrange("(t p) d -> p t d", p=128)
                tiles = xin[:, bass.ds(GROUP * g, GROUP), :]
                sp.dma_start(rows_[:, :, 0:HID], tiles).then_inc(rows_stored, 16)
                sp.dma_start(rows_[:, :, HID:256], tiles[:, :, 128:HID]).then_inc(rows_stored, 16)
            sp.wait_ge(cau.pv_done, JOBS * GROUPS + 2)
            for e in range(EXPERTS):
                sp.dma_start(pj_bias[:, e, :], pj_b[e:e + 1, :].to_broadcast([128, HID])).then_inc(bias_loaded, 16)
            with sp.Fori(0, EXPERTS // 2, 1) as r:
                for u in range(2):
                    e = r * 2 + u
                    sp.wait_ge(raw_split, e + 1)
                    for dst, rows_ in ((raw_fc[:, 0, :], slice(0, 128)), (raw_fc[0:REST, 1, :], slice(128, HID)),
                                       (raw_fc[REST:128, 1, :], slice(128, HID))):
                        sp.dma_start(dst, fc_w[bass.ds(e, 1), rows_, :].rearrange("e p n -> p (e n)")
                                     ).then_inc(raw_loaded, 16)
                    sp.wait_ge(hot_ready, 1)
                    sp.wait_ge(pj_used[u], r + 1)
                    sp.dma_start(pj_w_sb[:, u, :, :], pj_w[bass.ds(e, 1), :, :].rearrange(
                        "e (c p) n -> p (e c) n", p=128)).then_inc(pj_loaded[u], 16)
            for i in range(OUT_RING):
                sp.wait_ge(y_stored[i], 16 * EXPERTS * CAP_TILES // OUT_RING)
            for q in range(SEQS // TAKE_TILES):
                o = q % TAKE_RING
                if q >= TAKE_RING:
                    sp.wait_ge(token_done, TAKE_TILES * (q - TAKE_RING + 1))
                for k in range(TOPK):
                    row = k * TOKENS + 128 * TAKE_TILES * q
                    sp.dma_start(taken[:, o, k, :, :], token_out[row:row + 128 * TAKE_TILES, :].rearrange(
                        "(t p) d -> p t d", p=128)).then_inc(rows_taken[o], 16)


        @blk.gpsimd
        def _(pool):
            gp = nc.gpsimd
            gp.memset(zeros[:, :], 0.0).then_inc(const_made, 1)
            gp.memset(half[:, :], -0.5)
            gp.memset(kind_hot[:, :], 1.0)
            gp.memset(ident[:, :], 0.0)
            gp.memset(causal[:, :], 0.0)
            gp.iota(kind_sc[:, 0:1], pattern=[[0, 1]], base=-1, channel_multiplier=2,
                    allow_small_or_imprecise_dtypes=True)
            gp.iota(kind_sc[:, 1:2], pattern=[[0, 1]], base=1, channel_multiplier=-1,
                    allow_small_or_imprecise_dtypes=True)
            gp.memset(below[:, :], 1.0)
            gp.memset(ones_b[:, :], 1.0)
            gp.memset(one_f[:, :], 1.0)
            gp.memset(vals[:, :, :, :], 0.0).then_inc(const_made, 1)
            pool.wait_ge(const_made, 2)
            gp.affine_select(out=ident[:, :], in_=ident[:, :], compare_op=ALU.not_equal, fill=1.0, base=0,
                             pattern=[[-1, 128]], channel_multiplier=1)
            gp.affine_select(out=below[:, :], in_=below[:, :], compare_op=ALU.is_gt, fill=0.0, base=0,
                             pattern=[[1, 128]], channel_multiplier=-1)
            gp.affine_select(out=causal[:, :], in_=causal[:, :], compare_op=ALU.is_ge, fill=MASKED, base=0,
                             pattern=[[-1, 128]], channel_multiplier=1)
            gp.memset(vals[:, :, :, HEAD_DIM:HEAD_DIM + 1], 1.0).then_inc(ident_ready, 1)
            pool.wait_ge(ids_loaded, 16)

            def power(n, src, dst, eps, p, name):
                k = p.named(name + "_eps")
                gp.tensor_scalar(dst, src, eps, None, ALU.add).then_inc(k, 1)
                pool.wait_ge(k, n + 1)
                gp.tensor_tensor(dst, dst, half[:, 0:dst.shape[1]], ALU.pow).then_inc(p.named(name), 1)

            def gathers(g):
                pool.wait_ge(mag.named("emb_affine0"), g + 1)
                gp.tensor_copy(id_now[:, :, :], id_all[:, :, bass.ds(GROUP * g, GROUP)]).then_inc(id_copied, 1)
                pool.wait_ge(id_copied, g + 1)
                apart(pool)
                for table, dst, done, i in ((domain_table, got_dom, dom_got, 1), (word_table, got_word, word_got, 0),
                                            (pos_table, got_pos, pos_got, 2)):
                    for s in range(GROUP):
                        gp.indirect_dma_start(dst[:, s, :], None, table[:, :],
                                              bass.IndirectOffsetOnAxis(id_now[:, i, s:s + 1], 0)
                                              ).then_inc(done, 16)

            def embedding_norms(g):
                pool.wait_ge(mag.named("emb_moments"), g + 1)
                apart(pool)
                power(g, moments[:, :, 1], rstd[:, 0, :], WORD_EPS, mag, "emb_rstd")
                pool.wait_ge(mag.named("x_moments"), g + 1)
                apart(pool)
                power(g, moments[:, :, 1], rstd[:, 1, :], LN_EPS, mag, "x_rstd")

            def negate_max_roots(g):
                for s in range(GROUP):
                    pool.wait_ge(mag.named("max_root_done"), GROUP * g + s + 1)
                    apart(pool)
                    gp.tensor_scalar(neg_max[:, s, :], row_root[:, s, :], -1.0, None,
                                     ALU.mult).then_inc(mag.neg_max_done, 1)

            def take_row(u, t):
                c, (t0, nt) = next((c, at) for c, at in enumerate(CHUNKS) if at[0] <= t < sum(at))
                gp.indirect_dma_start(slot_x[c][:, t - t0, :], None, token_in[:, :],
                                      bass.IndirectOffsetOnAxis(slots_now[:, u, 0, t:t + 1], 0)
                                      ).then_inc(x_loaded[c], 16)

            def put_row(e, u, t):
                i, n = y_place(e, t)
                pool.wait_ge(y_free[i], n + 2)
                apart(pool)
                gp.indirect_dma_start(token_out[:, :], bass.IndirectOffsetOnAxis(slots_now[:, u, 1, t:t + 1], 0),
                                      slot_y[:, t % OUT_RING, :], None, bounds_check=TOPK * TOKENS - 1,
                                      oob_is_err=False).then_inc(y_stored[t % OUT_RING], 16)

            def slots_at_hand(a, table, e, u, done):
                gp.tensor_copy(slots_now[:, u, a, :], table[:, bass.ds(e * CAP_TILES, CAP_TILES)]).then_inc(done, 1)
                pool.wait_ge(done, e + 1)
                apart(pool)

            def move_rows():
                pool.wait_ge(map_ready, 1)
                slots_at_hand(0, slot_src, 0, 0, src_copied)
                pool.wait_ge(rows_stored, 2 * 16 * GROUPS)
                for t in range(CAP_TILES):
                    take_row(0, t)
                pool.wait_ge(map_ready, 2)
                pool.wait_ge(zero_filled, 16 * ZERO_FILLS)

                def expert(e, u, more):
                    if more:
                        slots_at_hand(0, slot_src, e + 1, 1 - u, src_copied)
                    slots_at_hand(1, slot_dst, e, u, dst_copied)
                    for c, (t0, nt) in enumerate(CHUNKS):
                        for t in range(t0, t0 + nt):
                            put_row(e, u, t)
                        if more:
                            i, n = turn_place(e, (t0 + nt) // 2 - 1)
                            pool.wait_ge(ex_turn_full[i], n + 1)
                            apart(pool)
                            for t in range(t0, t0 + nt):
                                take_row(1 - u, t)

                with pool.Fori(0, EXPERTS // 2 - 1, 1) as r:
                    expert(r * 2, 0, True)
                    expert(r * 2 + 1, 1, True)
                expert(EXPERTS - 2, 0, True)
                expert(EXPERTS - 1, 1, False)

            def layer_norm_scales(g):
                n = g
                pool.wait_ge(cau.named("moments"), n + 1)
                apart(pool)
                power(n, moments[:, :, 1], rstd[:, 0, :], LN_EPS, cau, "first_rstd")
                k = cau.named("second_var")
                pool.wait_ge(cau.named("first_rstd"), n + 1)
                gp.tensor_tensor(rstd[:, 2, :], moments[:, :, 1], rstd[:, 0, :], ALU.mult).then_inc(k, 1)
                pool.wait_ge(k, 2 * n + 1)
                gp.tensor_tensor(rstd[:, 3, :], rstd[:, 2, :], rstd[:, 0, :], ALU.mult).then_inc(k, 1)
                pool.wait_ge(k, 2 * n + 2)
                apart(pool)
                power(n, rstd[:, 3, :], rstd[:, 1, :], LN_EPS, cau, "second_rstd")

            def z_scale(g, s):
                n = GROUP * g + s
                pool.wait_ge(cau.named("z_moments"), n + 1)
                apart(pool)
                power(n, z_moments[:, 1:2], rstd[:, 4, 0:1], LN_EPS, cau, "z_rstd")

            def keep_z(g, s):
                n = GROUP * g + s
                gp.tensor_tensor(resid[:, n, :], resid[:, n, :], xin[:, n, :], ALU.add
                                 ).then_inc(cau.named("resid_added"), 1)
                pool.wait_ge(cau.named("resid_added"), n + 1)
                pool.wait_ge(z_ready, n + 1)
                apart(pool)
                gp.tensor_copy(xin[:, n, :], z[:, s % 2, :]).then_inc(z_kept, 1)

            def one_pass(turn, number):
                front, back, prep = turn.groups(number)
                if back and back[0] is cau:
                    for s in range(GROUP):
                        z_scale(back[1], s)
                        keep_z(back[1], s)
                if prep and prep[0] is mag:
                    gathers(prep[1])
                    embedding_norms(prep[1])
                elif prep:
                    layer_norm_scales(prep[1])
                if front and front[0] is mag:
                    negate_max_roots(front[1])

            one_pass(lead, -1)
            one_pass(mag_first, 0)
            with pool.Fori(1, GROUPS - 1, 1) as g:
                one_pass(mag_loop, g)
            one_pass(mag_last, GROUPS - 1)
            one_pass(bridge, 0)
            with pool.Fori(1, GROUPS - 1, 1) as g:
                one_pass(cau_loop, g)
            one_pass(cau_last, GROUPS - 1)
            one_pass(tail, GROUPS)
            gp.iota(number, pattern=[[1, 128]], base=0, channel_multiplier=0,
                    allow_small_or_imprecise_dtypes=True)
            gp.iota(token_no, pattern=[[0, TOPK], [128, SEQS]], base=1, channel_multiplier=1,
                    allow_small_or_imprecise_dtypes=True).then_inc(number_made, 1)
            move_rows()

        @blk.tensor
        def _(pe):
            for i in range(RING):
                pe.sem_inc(ring_free[i], 1)
            for p in (mag, cau):
                pe.sem_inc(p.scores_free, 2)
                pe.sem_inc(p.pv_done, 2)
                pe.sem_inc(p.ctx_copied, 1)

            def transpose(dst, src, n=128):
                return pe.transpose(dst, src, ident[0:n, 0:n])

            def split_product(dst, x, w_cols, v, begun=None):
                pairs = ((x[0], w_cols[0]), (x[0], w_cols[1]), (x[1], w_cols[0]), (x[2], w_cols[2]),
                         (x[2], w_cols[3]))
                for k, (a, w) in enumerate(pairs):
                    lhs, rhs = (a, w) if v else (w, a)
                    last = pe.matmul(dst, lhs, rhs, start=(k == 0), stop=(k == 4))
                    if begun is not None and k == 0:
                        last.then_inc(begun, 1)
                return last

            def taken_out(p, d, f, own):
                i, n = d[f]
                if i != own:
                    pe.wait_ge(ring_free[i], n + 2)

            def fill(p, g, f, place, d):
                i, n = place
                kind, s = f
                pe.wait_ge(ring_free[i], n + 1)
                dst = ps_ring[:, i, :]
                if kind == "xT":
                    pe.wait_ge(p.x_ready, GROUP * (g + 1) + 2 * s + 2)
                    for t in range(2):
                        for c in range(2):
                            last = transpose(dst[:, 256 * t + 128 * c:256 * t + 128 * c + 128],
                                             xn[:, 2 * s + t, 128 * c:128 * c + 128])
                elif kind == "proj":
                    m, b = divmod(s, 3)
                    if s == 0:
                        taken_out(p, d, "input", i)
                    col = slice(128 * b, 128 * b + 128)
                    last = split_product(dst, (x_hi[:, 0, :], x_lo[:, :], x_hi[:, 1, :]),
                                         (w_hi[:, 0, m, col], w_lo[:, 0, m, col], w_hi[:, 1, m, col],
                                          w_lo[:, 1, m, col]), False)
                elif kind == "value":
                    for t in range(p.values_per_fill):
                        k = 128 * (p.values_per_fill * s + t)
                        tok = slice(k, k + 128)
                        last = split_product(dst[:, HID * t:HID * t + HID],
                                             (x_hi[:, 0, tok], x_lo[:, tok], x_hi[:, 1, tok]),
                                             (v_hi[:, 0, :], v_lo[:, 0, :], v_hi[:, 1, :], v_lo[:, 1, :]), True)
                elif kind == "domT":
                    pe.wait_ge(dom_got, 16 * GROUP * (g + 1) + 16 * GROUP)
                    for t in range(2):
                        last = transpose(dst[:, 128 * t:128 * t + 128], got_dom[:, 2 * s + t, :])
                elif kind == "embed":
                    taken_out(p, d, ("domT", s), i)
                    pe.wait_ge(p.named("kinds_done"), g + 2)
                    for t in (2 * s, 2 * s + 1):
                        o = HID * (t % 2)
                        pe.matmul(dst[:, o:o + HID], dom_t[:, t, :], dom_w[:, :], start=True, stop=False)
                        last = pe.matmul(dst[:, o:o + HID], kind_hot[:, 128 * t:128 * t + 128], kind_w[:, :],
                                         start=False, stop=True)
                elif kind == "ctxT":
                    pe.wait_ge(p.named("ctx_dup"), GROUP * (g - 1) + s + 1)
                    transpose(dst[:, 0:128], ctx_n[:, 0:128])
                    last = transpose(dst[:, 128:256], ctx_n[:, 128:256])
                elif kind == "out":
                    taken_out(p, d, ("ctxT", s), i)
                    pe.matmul(dst[:, 0:HID], ctxn_t[:, 0, :], o_w[:, 0, :], start=True, stop=False)
                    last = pe.matmul(dst[:, 0:HID], ctxn_t[0:REST, 1, :], o_w[0:REST, 1, :],
                                     start=False, stop=True)
                elif kind == "zT":
                    pe.wait_ge(z_ready, GROUP * (g - 1) + s + 1)
                    transpose(dst[:, 0:128], z[:, s % 2, 0:128])
                    last = transpose(dst[0:REST, 128:256], z[:, s % 2, 128:HID])
                elif kind == "logits":
                    taken_out(p, d, ("zT", GROUP - 1), i)
                    pe.matmul(dst[0:EXPERTS, :], g_w[:, 0, :], z_t[:, 0, :], start=True, stop=False)
                    last = pe.matmul(dst[0:EXPERTS, :], g_w[0:REST, 1, :], z_t[0:REST, 1, :],
                                     start=False, stop=True)
                elif kind == "logitsT":
                    taken_out(p, d, ("logits", s), i)
                    apart(pe)
                    for t in range(GROUP):
                        last = transpose(dst[:, 8 * t:8 * t + 8], gate_t[:, 128 * t:128 * t + 128], EXPERTS)
                elif kind == "probT":
                    pe.wait_ge(p.exp_done, JOBS * (g - 1) + s + 1)
                    for h in range(4):
                        last = transpose(dst[:, 128 * h:128 * h + 128], probs[:, s, h, :])
                elif kind == "ctx":
                    pe.wait_ge(p.ctx_copied, GROUP * (g - 1) + s + 2)
                    for b in range(BLOCKS):
                        last = transpose(dst[:, 128 * b:128 * b + 128], ctx_t[:, b, :])
                last.then_inc(ring_full[i], 1)

            def scores(p, g, j, d):
                s, b = divmod(j, 3)
                if j == 0:
                    taken_out(p, d, ("proj", 8 if p is mag else 5), None)
                for pair in range(2):
                    pe.wait_ge(p.scores_free, 2 * (JOBS * g + j) + pair + 1)
                    two = (2 * pair, 2 * pair + 1)
                    if p is mag:
                        for a, (q, k) in enumerate(((q_hi, k_hi), (q_lo, k_hi), (q_hi, k_lo))):
                            for h in two:
                                r = slice(32 * h, 32 * h + 32)
                                last = pe.matmul(ps_scores[:, h, 0:256], q[r, b, s, :],
                                                 k[r, b, s, :, :].rearrange("p m k -> p (m k)"),
                                                 start=(a == 0), stop=(a == 2))
                    else:
                        for h in two:
                            r = slice(32 * h, 32 * h + 32)
                            last = pe.matmul(ps_scores[:, h, 0:128], cau_q[r, b, s, :], cau_k[r, b, s, :],
                                             start=True, stop=True)
                    last.then_inc(p.scores_full, 1)

            def keep_clock(count):
                for _ in range(count):
                    pe.matmul(ps_ctx[:, :], w_hi[:, 0, 0, 0:128],
                              w_hi[:, 0, 0:2, :].rearrange("p m n -> p (m n)")[:, 0:512], start=True, stop=True)

            def values_product(p, gb, j, d):
                s, b = divmod(j, 3)
                i, n = d[("probT", j)]
                pe.wait_ge(ring_free[i], n + 2)
                if b == 0:
                    pe.wait_ge(p.ctx_copied, GROUP * gb + s + 1)
                for h in range(4):
                    last = pe.matmul(ps_ctx[32 * h:32 * h + 32, 128 * b:128 * b + 128],
                                     vals[:, s, 4 * b + h, :], prob_t[:, j % 2, h, :],
                                     start=True, stop=True, skip_group_check=True)
                last.then_inc(p.pv_done, 1)

            def one_pass(turn, number):
                front, back, prep = turn.groups(number)
                by_slot, places = turn.schedule(number)
                for slot in range(PASS_SLOTS):
                    if slot == 0 and back and back[0] is cau:
                        keep_clock(2)
                    for p, g, f in by_slot[slot]:
                        fill(p, g, f, places[f], places)
                    if back and 1 <= slot <= JOBS:
                        values_product(*back, slot - 1, places)
                    if front and slot >= JOBS:
                        if slot >= 14 and front[0] is cau:
                            keep_clock(WARM[slot])
                        scores(*front, slot - JOBS, places)


            pe.wait_ge(ident_ready, 1)
            pe.wait_ge(const_loaded, CONST)
            one_pass(lead, -1)
            pe.wait_ge(mag_w_split, 4)
            one_pass(mag_first, 0)
            with pe.Fori(1, GROUPS - 1, 1) as g:
                one_pass(mag_loop, g)
            one_pass(mag_last, GROUPS - 1)
            pe.wait_ge(cau_w_split, 2)
            one_pass(bridge, 0)
            with pe.Fori(1, GROUPS - 1, 1) as g:
                one_pass(cau_loop, g)
            one_pass(cau_last, GROUPS - 1)
            one_pass(tail, GROUPS)
            pe.wait_ge(hot_ready, 1)
            hots = hot[:, :, :].rearrange("p t e -> p (t e)")
            pe.matmul(ps_scores[:, 0, :], below[:, :], hots, start=True, stop=True)
            pe.matmul(ps_scores[:, 1, :], ones_b[:, :], hots, start=True, stop=True).then_inc(ranked, 1)

            chunks = TOPK * SEQS // PAIRS_AT_ONCE
            for q in range(chunks):
                pe.wait_ge(hots_made, q + 1)
                k, at = divmod(q, chunks // TOPK)
                for j in range(PAIRS_AT_ONCE):
                    last = pe.matmul(ps_scores[:, 2 + k, 0:HIGH], low_hot[:, q % HOT_RING, j, :],
                                     high_hot[:, q % HOT_RING, j, :], start=(at == 0 and j == 0),
                                     stop=(at == chunks // TOPK - 1 and j == PAIRS_AT_ONCE - 1))
                last.then_inc(hots_used, 1)

            for i in range(2):
                pe.sem_inc(ex_turn_free[i], 1)
            for i in range(Y_RING):
                pe.sem_inc(y_free[i], 1)
            pe.sem_inc(pj_used[0], 1)
            for i in range(FC_RING):
                pe.sem_inc(gelu_done[i], 1)

            def turn_x(e, c):
                t0, nt = CHUNKS[c]
                pe.wait_ge(x_loaded[c], e * (16 * nt) + 16 * nt)
                for m in range(t0 // 2, (t0 + nt) // 2):
                    i, n = turn_place(e, m)
                    pe.wait_ge(ex_turn_free[i], n + 1)
                    for t in (2 * m, 2 * m + 1):
                        for part in range(2):
                            at = 256 * (t % 2) + 128 * part
                            last = transpose(ps_x[i][:, at:at + 128],
                                             slot_x[c][:, t - t0, 128 * part:128 * part + 128])
                    last.then_inc(ex_turn_full[i], 1)

            def first_layer(u, e, c):
                t0, nt = CHUNKS[c]
                if c == 0:
                    pe.wait_ge(raw_split, e + 2)
                for m in range(t0 // 2, (t0 + nt) // 2):
                    i, n = turn_place(e, m)
                    pe.wait_ge(ex_turn_free[i], n + 2)
                tok = slice(0, 128 * nt)
                for f_ in range(FF_CHUNKS):
                    i = f_ % FC_RING
                    pe.wait_ge(gelu_done[i], e * 6 + 2 * c + f_ // FC_RING + 1)
                    col = slice(128 * f_, 128 * f_ + 128)
                    split_product(ps_scores[:, i, tok], (x_hi[:, 0, tok], x_lo[:, tok], x_hi[:, 1, tok]),
                                  (fc_hi[:, u, 0, col], fc_lo[:, u, 0, col], fc_hi[:, u, 1, col],
                                   fc_lo[:, u, 1, col]), False,
                                  begun=pj_used[1 - u] if c == 0 and f_ == 0 else None).then_inc(fc_full[i], 1)

            def second_layer(r, u, e, c):
                t0, nt = CHUNKS[c]
                if c == 0:
                    pe.wait_ge(pj_loaded[u], 16 * r + 16)
                for i in range(FC_RING):
                    pe.wait_ge(gelu_done[i], e * 6 + 2 * c + 3)
                for t in range(t0, t0 + nt):
                    i, n = y_place(e, t)
                    pe.wait_ge(y_free[i], n + 1)
                    tok = slice(128 * (t - t0), 128 * (t - t0) + 128)
                    for f_ in range(FF_CHUNKS):
                        last = pe.matmul(ps_y[i][:, 0:HID], hidden[:, c % 2, f_, tok], pj_w_sb[:, u, f_, :],
                                         start=(f_ == 0), stop=(f_ == FF_CHUNKS - 1))
                    last.then_inc(y_full[i], 1)

            def expert(r, u, more):
                e = r * 2 + u
                first_layer(u, e, 0)
                turn_x(e, 1)
                second_layer(r, u, e, 0)
                first_layer(u, e, 1)
                turn_x(e, 2)
                second_layer(r, u, e, 1)
                first_layer(u, e, 2)
                if more:
                    turn_x(e + 1, 0)
                second_layer(r, u, e, 2)

            turn_x(0, 0)
            with pe.Fori(0, EXPERTS // 2 - 1, 1) as r:
                expert(r, 0, True)
                expert(r, 1, True)
            expert(EXPERTS // 2 - 1, 0, True)
            expert(EXPERTS // 2 - 1, 1, False)

        @blk.scalar
        def _(act):
            sc = nc.scalar

            def split_weights_high(loaded, done, m):
                act.wait_ge(loaded, 6 * 16)
                raw_qk, raw_v = raw_weights(m)
                sc.activation(w_hi[:, :, 0:m, :], raw_qk, ACT.Copy).then_inc(done, 1)
                sc.activation(v_hi[:, :, :], raw_v, ACT.Copy).then_inc(done, 1)

            def fill(p, f, place, d):
                i, n = place
                kind, s = f
                src = ps_ring[:, i, :]
                if kind in ("embed", "out", "logitsT", "probT", "ctx"):
                    return
                act.wait_ge(ring_full[i], n + 1)
                tok = slice(128 * s, 128 * s + 128)
                if kind == "xT":
                    two = slice(256 * s, 256 * s + 256)
                    by_chunk = src.rearrange("p (s c t) -> p c s t", s=2, c=2)
                    if p is mag:
                        sc.activation(x_hi[:, :, two].rearrange("p c (s t) -> p c s t", s=2), by_chunk,
                                      ACT.Copy).then_inc(p.high_done, 1)
                    else:
                        if s > 0:
                            fi, fn = d[("xT", s - 1)]
                            act.wait_ge(ring_free[fi], fn + 2)
                        for c in range(2):
                            last = sc.activation(x_full[:, c, :].rearrange("p (s t) -> p s t", s=2),
                                                 by_chunk[:, c, :, :], ACT.Identity, bias=ln_c[:, 2 + c:3 + c],
                                                 scale=ln_c[:, c:c + 1])
                        last.then_inc(p.high_done, 1)
                elif kind == "proj":
                    m, b = divmod(s, 3)
                    dst = q_hi[:, b, :, :] if m == 0 else k_hi[:, b, :, m - 1, :]
                    view = src.rearrange("p (s k) -> p s k", s=GROUP)
                    if p is mag:
                        sc.activation(dst, view, ACT.Copy).then_inc(p.high_done, 1)
                    else:
                        sc.activation((cau_q, cau_k)[m][:, b, :, :], view, ACT.Identity,
                                      bias=qk_b[:, s:s + 1]).then_inc(ring_free[i], 1)
                elif kind == "value":
                    if p is mag:
                        sc.activation(vals[:, 2 * s:2 * s + 2, :, 0:HEAD_DIM],
                                      src[:, 0:2 * HID].rearrange("p (s h d) -> p s h d", s=2, h=HEADS),
                                      ACT.Copy).then_inc(ring_free[i], 1)
                elif kind == "domT":
                    sc.activation(dom_t[:, 2 * s:2 * s + 2, :], src[:, 0:256].rearrange("p (s t) -> p s t", s=2),
                                  ACT.Copy).then_inc(ring_free[i], 1)
                elif kind == "ctxT":
                    sc.activation(ctxn_t, src[:, 0:256].rearrange("p (c t) -> p c t", c=2),
                                  ACT.Copy).then_inc(ring_free[i], 1)
                elif kind == "zT":
                    sc.activation(z_t[:, 0, tok], src[:, 0:128], ACT.Identity, bias=ln_c[:, 6:7],
                                  scale=ln_c[:, 4:5]).then_inc(z_used, 1)
                    sc.activation(z_t[0:REST, 1, tok], src[0:REST, 128:256], ACT.Identity,
                                  bias=ln_c[0:REST, 7:8], scale=ln_c[0:REST, 5:6]).then_inc(ring_free[i], 1)
                elif kind == "logits":
                    sc.activation(gate_t, src[0:EXPERTS, :],
                                  ACT.Copy).then_inc(ring_free[i], 1)

            def exps(p, gb, j):
                s, b = divmod(j, 3)
                if b == 0:
                    if p is cau:
                        act.wait_ge(cau.scores_free, 2 * (JOBS * gb + 3 * s + 3) + 2)
                    else:
                        act.wait_ge(mag.neg_max_done, GROUP * gb + s + 1)
                        act.wait_ge(mag.named("root_done"), JOBS * gb + 3 * s + 3)
                for h in range(4):
                    last = sc.activation(probs[:, j, h, :], probs[:, j, h, :], ACT.Exp,
                                         bias=neg_max[:, s, 4 * b + h:4 * b + h + 1],
                                         scale=1.0 if p is mag else -1.0)
                last.then_inc(p.exp_done, 1)

            early = {"mag": 0, "cau": 6}

            def squares(g, j):
                act.wait_ge(mag.max_done, JOBS * g + j + 1)
                for pair in range(2):
                    act.wait_ge(mag.scores_full, 2 * (JOBS * g + j) + pair + 1)
                    h = slice(2 * pair, 2 * pair + 2)
                    sc.activation(square[:, j % 2, h, :, :].rearrange("p h m k -> p h (m k)"),
                                  ps_scores[:, h, 0:256], ACT.Square).then_inc(mag.scores_free, 1)

            def roots(g, j):
                s, b = divmod(j, 3)
                act.wait_ge(mag.max_done, JOBS * g + j + 1 + 2)
                if b == 2:
                    sc.activation(row_root[:, s, :], row_max[:, s, :], ACT.Sqrt, scale=1.0 / HEAD_DIM
                                  ).then_inc(mag.named("max_root_done"), 1)
                sc.activation(probs[:, j, :, :], probs[:, j, :, :], ACT.Sqrt, scale=1.0 / HEAD_DIM
                              ).then_inc(mag.named("root_done"), 1)

            def copy_ctx(p, gb, s):
                act.wait_ge(p.pv_done, JOBS * gb + 3 * s + 3 + 2)
                sc.activation(ctx_t[:, :, :], ps_ctx[:, 0:384].rearrange("p (b q) -> p b q", b=3),
                              ACT.Copy).then_inc(p.ctx_copied, 1)

            def one_pass(turn, number):
                front, back, prep = turn.groups(number)
                by_slot, places = turn.schedule(number)
                for slot in range(PASS_SLOTS):
                    fills = list(by_slot[slot])
                    for turn_of in range(2):
                        if slot == 0 and back and front:
                            p, _, f = fills.pop(0)
                            fill(p, f, places[f], places)
                        j = slot + turn_of
                        if back and j < JOBS and j >= early[back[0].name] and (turn_of or slot == 0):
                            exps(*back, j)
                    for p, _, f in fills:
                        fill(p, f, places[f], places)
                    if back and slot >= 3 and slot % 3 == 0 and slot // 3 <= GROUP:
                        copy_ctx(*back, slot // 3 - 1)
                    if front and front[0] is cau and 17 <= slot < 17 + early["cau"]:
                        exps(*front, slot - 17)
                    if front and front[0] is mag and slot >= JOBS:
                        j = slot - JOBS
                        squares(front[1], j)
                        if j >= 2:
                            roots(front[1], j - 2)
                    if turn is mag_last and slot == 18:
                        split_weights_high(cau_w_loaded, cau_w_high, 2)
                if front and front[0] is mag:
                    roots(front[1], JOBS - 2)
                    roots(front[1], JOBS - 1)

            act.wait_ge(const_loaded, CONST)
            split_weights_high(mag_w_loaded, mag_w_high, 3)
            one_pass(lead, -1)
            one_pass(mag_first, 0)
            with act.Fori(1, GROUPS - 1, 1) as g:
                one_pass(mag_loop, g)
            one_pass(mag_last, GROUPS - 1)
            one_pass(bridge, 0)
            with act.Fori(1, GROUPS - 1, 1) as g:
                one_pass(cau_loop, g)
            one_pass(cau_last, GROUPS - 1)
            one_pass(tail, GROUPS)
            act.wait_ge(gap_ready, 1)
            sc.activation(gap[:, 1, :], gap[:, 0, :], ACT.Exp).then_inc(gap_exp, 1)

            for q in range(TOPK * SEQS // PAIRS_AT_ONCE):
                act.wait_ge(ones_made, q + 1)
                for j in range(PAIRS_AT_ONCE):
                    c = PAIRS_AT_ONCE * q + j
                    last = sc.activation(high_hot[:, q % HOT_RING, j, :], high_one[:, q % HOT_RING, j, :], ACT.Copy,
                                         scale=token_no[:, c:c + 1])
                last.then_inc(hots_made, 1)

            def expert_weights_high(e, u):
                act.wait_ge(raw_loaded, 48 * e + 48)
                apart(act)
                sc.activation(fc_hi[:, u, :, :], raw_fc, ACT.Copy).then_inc(fc_high, 1)

            def whole_x(e, c):
                t0, nt = CHUNKS[c]
                for m in range(t0 // 2, (t0 + nt) // 2):
                    i, n = turn_place(e, m)
                    act.wait_ge(ex_turn_full[i], n + 1)
                    if m == 0:
                        act.wait_ge(ex_turn_free[0], e * TURNS[0] + 1)
                    else:
                        before, n = turn_place(e, m - 1)
                        act.wait_ge(ex_turn_free[before], n + 2)
                    by_part = ps_x[i].rearrange("p (t c k) -> p c t k", t=2, c=2)
                    for part in range(2):
                        last = sc.activation(x_full[:, part, :].rearrange("p (t k) -> p t k", t=2),
                                             by_part[:, part, :, :], ACT.Identity,
                                             bias=ln_c[:, 6 + part:7 + part], scale=ln_c[:, 4 + part:5 + part])
                    last.then_inc(ex_whole, 1)

            def gelus(e, c):
                nt = CHUNKS[c][1]
                for f_ in range(FF_CHUNKS):
                    i = f_ % FC_RING
                    act.wait_ge(fc_full[i], e * 6 + 2 * c + f_ // FC_RING + 1)
                    apart(act)
                    sc.activation(hidden[:, c % 2, f_, 0:128 * nt], ps_scores[:, i, 0:128 * nt], ACT.Gelu,
                                  bias=fc_bias[:, e, f_:f_ + 1]).then_inc(gelu_done[i], 1)

            def expert(e, u, more):
                gelus(e, 0)
                whole_x(e, 1)
                if more:
                    expert_weights_high(e + 1, 1 - u)
                gelus(e, 1)
                whole_x(e, 2)
                gelus(e, 2)
                if more:
                    whole_x(e + 1, 0)

            act.wait_ge(bias_loaded, 16 * (1 + EXPERTS))
            expert_weights_high(0, 0)
            whole_x(0, 0)
            with act.Fori(0, EXPERTS // 2 - 1, 1) as r:
                expert(r * 2, 0, True)
                expert(r * 2 + 1, 1, True)
            expert(EXPERTS - 2, 0, True)
            expert(EXPERTS - 1, 1, False)
            for t in range(0, SEQS, 4):
                act.wait_ge(token_done, t + 4)
                act.dma_start(out[t:t + 4].rearrange("t p d -> p t d"), resid[:, t:t + 4, :]).then_inc(out_stored, 16)
            act.wait_ge(out_stored, 16 * (SEQS // 4))

        @blk.vector
        def _(dve):
            ve = nc.vector
            f = lambda a: a.bitcast(F32)

            def split_weights_low(loaded, high, done, m):
                dve.wait_ge(loaded, 6 * 16)
                dve.wait_ge(high, 2)
                raw_qk, raw_v = raw_weights(m)
                ve.tensor_tensor(w_lo[:, :, 0:m, :], raw_qk, f(w_hi[:, :, 0:m, :]),
                                 ALU.subtract).then_inc(done, 1)
                ve.tensor_tensor(v_lo[:, :, :], raw_v, f(v_hi[:, :, :]), ALU.subtract).then_inc(done, 1)

            def negate_imaginary_keys():
                for w in (w_hi, w_lo):
                    v = w[:, :, 2, :].rearrange("p c (h x) -> p c h x", x=32)[:, :, :, 0:HEAD_DIM]
                    ve.tensor_scalar(v, f(v), -1.0, None, ALU.mult).then_inc(mag_w_split, 1)

            def fill(p, g, fl, place):
                i, n = place
                kind, s = fl
                src = ps_ring[:, i, :]
                free = ring_free[i]
                two = slice(256 * s, 256 * s + 256)
                hl = slice(REST, 128)
                if kind == "xT":
                    dve.wait_ge(p.high_done, high_count(p, g + 1 if kind == "xT" else g, fl))
                    if p is mag:
                        by_chunk = src.rearrange("p (s c t) -> p c s t", s=2, c=2)
                        halves = lambda a: a.rearrange("p (s t) -> p s t", s=2)
                        ve.tensor_tensor(halves(x_lo[:, two]), by_chunk[:, 0, :, :], halves(f(x_hi[:, 0, two])),
                                         ALU.subtract)
                        ve.tensor_tensor(halves(x_hi[hl, 1, two]), by_chunk[hl, 1, :, :],
                                         halves(f(x_hi[hl, 1, two])), ALU.subtract).then_inc(free, 1)
                    else:
                        ve.tensor_copy(x_hi[:, :, two], x_full[:, :, :]).then_inc(p.named("x_high"), 1)
                        dve.wait_ge(p.named("x_high"), 2 * (g + 1) + s + 1)
                        ve.tensor_tensor(x_lo[:, two], x_full[:, 0, :], f(x_hi[:, 0, two]), ALU.subtract)
                        ve.tensor_tensor(x_hi[hl, 1, two], x_full[hl, 1, :], f(x_hi[hl, 1, two]),
                                         ALU.subtract).then_inc(free, 1)
                elif kind == "proj" and p is mag:
                    dve.wait_ge(p.high_done, high_count(p, g + 1 if kind == "xT" else g, fl))
                    m, b = divmod(s, 3)
                    if m == 0:
                        lo, hi = q_lo[:, b, :, :], q_hi[:, b, :, :]
                    else:
                        lo, hi = k_lo[:, b, :, m - 1, :], k_hi[:, b, :, m - 1, :]
                    view = src.rearrange("p (s k) -> p s k", s=GROUP)
                    ve.tensor_tensor(lo, view, f(hi), ALU.subtract).then_inc(free, 1)
                elif kind == "value" and p is cau:
                    dve.wait_ge(ring_full[i], n + 1)
                    ve.tensor_tensor(vals[:, s, :, 0:HEAD_DIM],
                                     src[:, 0:HID].rearrange("p (h d) -> p h d", h=HEADS),
                                     row_c[:, 2, :].rearrange("p (h d) -> p h d", h=HEADS),
                                     ALU.add).then_inc(free, 1)
                elif kind == "embed":
                    dve.wait_ge(ring_full[i], n + 1)
                    pair = got_word[:, 2 * s:2 * s + 2, :]
                    ve.tensor_tensor(pair, src[:, 0:2 * HID].rearrange("p (s d) -> p s d", s=2), pair,
                                     ALU.add).then_inc(free, 1)
                elif kind == "probT":
                    dve.wait_ge(ring_full[i], n + 1)
                    dve.wait_ge(p.pv_done, JOBS * (g - 1) + s + 1)
                    ve.tensor_copy(prob_t[:, s % 2, :, :], src.rearrange("p (h q) -> p h q", h=4)
                                   ).then_inc(free, 1)
                elif kind == "ctx":
                    t = GROUP * (g - 1) + s
                    dve.wait_ge(ring_full[i], n + 1)
                    v = src[:, 0:384].rearrange("p (h x) -> p h x", x=32)
                    ve.reciprocal(recip[:, :], v[:, :, HEAD_DIM]).then_inc(p.recip_done, 1)
                    dve.wait_ge(p.recip_done, t + 1)
                    ve.tensor_tensor(ctx_n[:, 0:HID].rearrange("p (h d) -> p h d", h=HEADS), v[:, :, 0:HEAD_DIM],
                                     recip[:, :].unsqueeze(2).to_broadcast([128, HEADS, HEAD_DIM]),
                                     ALU.mult).then_inc(free, 1)
                    dve.wait_ge(free, n + 2)
                    if p is mag:
                        ve.tensor_tensor(resid[:, t, :], resid[:, t, :], ctx_n[:, 0:HID], ALU.add
                                         ).then_inc(p.ctx_done, 1)
                    else:
                        ve.tensor_copy(ctx_n[:, HID:256], ctx_n[:, 128:HID]).then_inc(p.named("ctx_dup"), 1)
                elif kind == "out":
                    t = GROUP * (g - 1) + s
                    dve.wait_ge(ring_full[i], n + 1)
                    ve.tensor_tensor(out_b, src[:, 0:HID], row_c[:, 3, :], ALU.add).then_inc(free, 1)
                    dve.wait_ge(free, n + 2)
                    ve.tensor_tensor(xin[:, t, :], xin[:, t, :], out_b, ALU.add
                                     ).then_inc(p.named("layer_sum"), 1)
                    dve.wait_ge(p.named("layer_sum"), t + 1)
                    apart(dve)
                    ve.bn_stats(z_stats[:, :], xin[:, t, :]).then_inc(p.named("z_stats"), 1)
                    dve.wait_ge(p.named("z_stats"), t + 1)
                    apart(dve)
                    ve.bn_aggr(z_moments[:, :], z_stats[:, :]).then_inc(p.named("z_moments"), 1)
                elif kind == "logitsT":
                    dve.wait_ge(ring_full[i], n + 1)
                    ve.tensor_copy(logits[:, bass.ds(GROUP * (g - 1), GROUP), :],
                                   src[:, 0:GROUP * EXPERTS].rearrange("p (t e) -> p t e", t=GROUP)
                                   ).then_inc(free, 1)

            def high_count(p, g, fl):
                kind, s = fl
                per = 2 + (9 if p is mag else 0)
                return per * g + (s if kind == "xT" else 2 + s) + 1

            def normalise_z(p, gb, s):
                t = GROUP * gb + s
                dve.wait_ge(p.named("z_rstd"), t + 1)
                dve.wait_ge(p.named("z_moments"), t + 1)
                dve.wait_ge(z_used, t + 1)
                dve.wait_ge(z_kept, t + 1)
                ve.tensor_scalar(z[:, s % 2, :], xin[:, t, :], z_moments[:, 0:1], rstd[:, 4, 0:1],
                                 ALU.subtract, ALU.mult).then_inc(z_ready, 1)

            def maxima(p, g, j):
                s, b = divmod(j, 3)
                for pair in range(2):
                    if p is mag:
                        dve.wait_ge(mag.scores_free, 2 * (JOBS * g + j) + pair + 1 + 2)
                    else:
                        dve.wait_ge(cau.scores_full, 2 * (JOBS * g + j) + pair + 1)
                    apart(dve)
                    for h in (2 * pair, 2 * pair + 1):
                        if p is mag:
                            a, c = square[:, j % 2, h, 0, :], square[:, j % 2, h, 1, :]
                        else:
                            a, c = ps_scores[:, h, 0:128], causal[:, :]
                        if p is mag:
                            last = ve.tensor_tensor_reduce(out=probs[:, j, h, :], in0=a, in1=c, scale=1.0,
                                                           scalar=-3.0e38, op0=ALU.add, op1=ALU.max,
                                                           accum_out=row_max[:, s, 4 * b + h:4 * b + h + 1])
                        else:
                            last = ve.tensor_tensor_reduce(out=probs[:, j, h, :], in0=a, in1=c,
                                                           scale=-(HEAD_DIM ** -0.5), scalar=3.0e38,
                                                           op0=ALU.add, op1=ALU.min,
                                                           accum_out=neg_max[:, s, 4 * b + h:4 * b + h + 1])
                    if p is cau:
                        last.then_inc(cau.scores_free, 1)
                if p is mag:
                    last.then_inc(p.max_done, 1)

            def lay_kinds(g):
                ve.tensor_scalar(kind_hot[0:2, :], kind_i[:, bass.ds(512 * g, 512)], kind_sc[:, 0:1],
                                 kind_sc[:, 1:2], ALU.mult, ALU.add).then_inc(mag.named("kinds_done"), 1)

            def add_positions(g):
                dve.wait_ge(word_got, 16 * GROUP * (g + 1))
                dve.wait_ge(pos_got, 16 * GROUP * (g + 1))
                ve.tensor_tensor(got_word[:, :, :], got_word[:, :, :], got_pos[:, :, :], ALU.add
                                 ).then_inc(mag.named("pos_added"), 1)
                dve.wait_ge(mag.named("pos_added"), g + 1)

            def group_moments(p, src, g, name):
                for s in range(GROUP):
                    last = ve.bn_stats(stats[:, s, :], src(s))
                last.then_inc(p.named(name + "_stats"), 1)
                dve.wait_ge(p.named(name + "_stats"), g + 1)
                apart(dve)
                for s in range(GROUP):
                    last = ve.bn_aggr(moments[:, s, :], stats[:, s, :])
                last.then_inc(p.named(name), 1)

            def scale_tile(dst, src, s, r):
                return ve.tensor_scalar(dst, src, moments[:, s, 0:1], rstd[:, r, s:s + 1], ALU.subtract, ALU.mult)

            def dup_view(a):
                return a.unsqueeze(1).to_broadcast([128, 2, REST])

            def embedding_step(g, slot, places):
                tiles = resid[:, bass.ds(GROUP * g, GROUP), :]
                if slot == 11:
                    lay_kinds(g)
                elif slot == 12:
                    add_positions(g)
                elif slot == 14:
                    i, n = places[("embed", 1)]
                    dve.wait_ge(ring_free[i], n + 2)
                    apart(dve)
                    group_moments(mag, lambda s: got_word[:, s, :], g, "emb_moments")
                elif slot == 15:
                    dve.wait_ge(mag.named("emb_moments"), g + 1)
                    dve.wait_ge(mag.named("emb_rstd"), g + 1)
                    for s in range(GROUP):
                        last = scale_tile(got_word[:, s, :], got_word[:, s, :], s, 0)
                    last.then_inc(mag.named("emb_scaled"), 1)
                elif slot in (16, 17):
                    i_row, op, src = ((0, ALU.mult, got_word[:, :, :]), (1, ALU.add, tiles))[slot - 16]
                    dve.wait_ge(mag.named("emb_affine0" if i_row else "emb_scaled"), g + 1 + i_row)
                    ve.tensor_tensor(tiles, src, row_c[:, i_row, :].unsqueeze(1).to_broadcast([128, GROUP, HID]),
                                     op).then_inc(mag.named(f"emb_affine{i_row}"), 1)
                elif slot == 18:
                    dve.wait_ge(mag.named("emb_affine1"), g + 1)
                    apart(dve)
                    group_moments(mag, lambda s: resid[:, GROUP * g + s, :], g, "x_moments")
                elif slot in (19, 20):
                    if slot == 19:
                        dve.wait_ge(mag.named("x_moments"), g + 1)
                        dve.wait_ge(mag.named("x_rstd"), g + 1)
                    for s in (2 * (slot - 19), 2 * (slot - 19) + 1):
                        t = GROUP * g + s
                        scale_tile(xn[:, s, 0:128], resid[:, t, 0:128], s, 1)
                        scale_tile(xn[:, s, 128:256].rearrange("p (c d) -> p c d", c=2),
                                   dup_view(resid[:, t, 128:HID]), s, 1).then_inc(mag.x_ready, 1)

            def causal_input_step(g, slot):
                stats_done, in_done = cau.named("moments_stats"), cau.named("x_in")
                if slot in (14, 15):
                    if isinstance(g, int) and slot == 14:
                        dve.wait_ge(mag.ctx_done, GROUP * (g + 1))
                    for s in (2 * (slot - 14), 2 * (slot - 14) + 1):
                        last = ve.bn_stats(stats[:, s, :], resid[:, GROUP * g + s, :])
                    last.then_inc(stats_done, 1)
                elif slot == 16:
                    dve.wait_ge(stats_done, 2 * g + 2)
                    apart(dve)
                    for s in range(GROUP):
                        last = ve.bn_aggr(moments[:, s, :], stats[:, s, :])
                    last.then_inc(cau.named("moments"), 1)
                elif slot in (17, 18):
                    if slot == 17:
                        dve.wait_ge(cau.named("moments"), g + 1)
                        dve.wait_ge(cau.named("first_rstd"), g + 1)
                    for s in (2 * (slot - 17), 2 * (slot - 17) + 1):
                        last = scale_tile(xin[:, GROUP * g + s, :], resid[:, GROUP * g + s, :], s, 0)
                    last.then_inc(in_done, 1)
                elif slot in (19, 20):
                    if slot == 19:
                        dve.wait_ge(in_done, 2 * g + 2)
                        dve.wait_ge(cau.named("second_rstd"), g + 1)
                    for s in (2 * (slot - 19), 2 * (slot - 19) + 1):
                        t = GROUP * g + s
                        r = rstd[:, 1, s:s + 1]
                        ve.tensor_scalar(xn[:, s, 0:128], xin[:, t, 0:128], r, None, ALU.mult)
                        ve.tensor_scalar(xn[:, s, 128:256].rearrange("p (c d) -> p c d", c=2),
                                         dup_view(xin[:, t, 128:HID]), r, None, ALU.mult).then_inc(cau.x_ready, 1)

            count = [0]

            def step(ins):
                count[0] += 1
                ins.then_inc(route, 1)
                dve.wait_ge(route, count[0])

            def order_experts(first, end):
                for t in range(first, end):
                    last = ve.max(best[:, t, :], logits[:, t, :])
                step(last)
                for t in range(first, end):
                    last = ve.max_index(best_at[:, t, :], best[:, t, :], logits[:, t, :])
                step(last)

            def one_pass(turn, number):
                front, back, prep = turn.groups(number)
                by_slot, places = turn.schedule(number)
                for slot in range(PASS_SLOTS):
                    if turn is tail and slot == 19:
                        i, n = cau_last.schedule(number - 1)[1][("logitsT", 0)]
                        dve.wait_ge(ring_free[i], n + 2)
                        order_experts(0, SEQS - GROUP)
                    for p, g, fl in by_slot[slot]:
                        fill(p, g, fl, places[fl])
                    if back and back[0] is cau and slot >= 7 and (slot - 7) % 3 == 0 and (slot - 7) // 3 < GROUP:
                        normalise_z(*back, (slot - 7) // 3)
                    if front and slot >= JOBS:
                        maxima(*front, slot - JOBS)
                    if turn is mag_last and slot == 18:
                        split_weights_low(cau_w_loaded, cau_w_high, cau_w_split, 2)
                    if prep and prep[0] is mag:
                        embedding_step(prep[1], slot, places)
                    elif prep:
                        causal_input_step(prep[1], slot)

            def route_tokens():
                for i in range(RING):
                    dve.wait_ge(ring_free[i], (tail.end - i - 1) // RING + 1 + 1)
                order_experts(SEQS - GROUP, SEQS)
                ve.tensor_tensor(gap[:, 0, :], best[:, :, 1], best[:, :, 0], ALU.subtract).then_inc(gap_ready, 1)
                step(ve.tensor_copy(choice[:, :, :], best_at[:, :, 0:TOPK].rearrange("p t k -> p k t")))
                chosen = choice[:, :, :].rearrange("p k t -> p (k t)")
                pairs = TOPK * SEQS
                dve.wait_ge(number_made, 1)
                ve.tensor_tensor(hot[:, :, :], number[:, 0:EXPERTS].unsqueeze(1).to_broadcast([128, pairs, EXPERTS]),
                                 chosen.unsqueeze(2).to_broadcast([128, pairs, EXPERTS]),
                                 ALU.is_equal).then_inc(hot_ready, 1)
                dve.wait_ge(ranked, 1)
                dve.wait_ge(hot_ready, 1)
                total = ps_scores[:, 1, :].rearrange("p (t e) -> p t e", e=EXPERTS)
                for e in range(EXPERTS):
                    last = ve.tensor_tensor_scan(rank_e[:, :, e], one_f[:, :], total[:, :, e], 0.0,
                                                 ALU.mult, ALU.add)
                step(last)
                step(ve.tensor_tensor(rank_e[:, :, :], rank_e[:, :, :], total, ALU.subtract))
                step(ve.tensor_tensor(rank_e[:, :, :], rank_e[:, :, :],
                                      ps_scores[:, 0, :].rearrange("p (t e) -> p t e", e=EXPERTS), ALU.add))
                step(ve.tensor_tensor(rank_e[:, :, :], rank_e[:, :, :], hot[:, :, :], ALU.mult))
                ranks = rank[:, :, :].rearrange("p k t -> p (k t)")
                keeps = keep[:, :, :].rearrange("p k t -> p (k t)")
                step(ve.tensor_reduce(ranks, rank_e[:, :, :], AX.X, ALU.add))
                step(ve.tensor_scalar(keeps, ranks, float(CAP), None, ALU.is_lt))
                step(ve.tensor_scalar(slot_f[:, 0, :], keeps, -float(SLOTS), float(SLOTS), ALU.mult, ALU.add))
                step(ve.tensor_tensor(slot_f[:, 0, :], slot_f[:, 0, :], ranks, ALU.add))
                step(ve.scalar_tensor_tensor(out=slot_f[:, 0, :], in0=chosen, scalar=float(CAP),
                                             in1=slot_f[:, 0, :], op0=ALU.mult, op1=ALU.add))
                low_i, high_i, low, high = at_i[:, 0, :], at_i[:, 1, :], at_f[:, 0, :], at_f[:, 1, :]
                step(ve.tensor_copy(at_i[:, 2, :], slot_f[:, 0, :]))
                step(ve.tensor_scalar(low_i, at_i[:, 2, :], LOW - 1, None, ALU.bitwise_and))
                step(ve.tensor_scalar(high_i, at_i[:, 2, :], LOW.bit_length() - 1, None, ALU.logical_shift_right))
                step(ve.tensor_copy(low, low_i))
                step(ve.tensor_copy(high, high_i))
                for q in range(pairs // PAIRS_AT_ONCE):
                    if q >= HOT_RING:
                        dve.wait_ge(hots_used, q - HOT_RING + 1)
                    some = slice(PAIRS_AT_ONCE * q, PAIRS_AT_ONCE * (q + 1))
                    ve.tensor_tensor(low_hot[:, q % HOT_RING, :, :],
                                     number.unsqueeze(1).to_broadcast([128, PAIRS_AT_ONCE, LOW]),
                                     low[:, some].unsqueeze(2).to_broadcast([128, PAIRS_AT_ONCE, LOW]), ALU.is_equal)
                    ve.tensor_tensor(high_one[:, q % HOT_RING, :, :],
                                     number[:, 0:HIGH].unsqueeze(1).to_broadcast([128, PAIRS_AT_ONCE, HIGH]),
                                     high[:, some].unsqueeze(2).to_broadcast([128, PAIRS_AT_ONCE, HIGH]),
                                     ALU.is_equal).then_inc(ones_made, 1)
                dve.wait_ge(hots_used, pairs // PAIRS_AT_ONCE)
                second, token, empty = (of_slot[:, i, :] for i in range(3))
                step(ve.tensor_copy(second, ps_scores[:, 3, 0:HIGH]))
                step(ve.tensor_tensor(token, second, ps_scores[:, 2, 0:HIGH], ALU.add))
                ve.tensor_scalar(slot_src[:, :], token, -1.0, 0.0, ALU.add, ALU.max).then_inc(map_ready, 1)
                step(ve.tensor_scalar(second, second, 0.0, float(TOKENS), ALU.is_gt, ALU.mult))
                step(ve.tensor_scalar(empty, token, 0.0, float(4 * TOKENS), ALU.is_equal, ALU.mult))
                step(ve.tensor_tensor(token, token, second, ALU.add))
                step(ve.tensor_tensor(token, token, empty, ALU.add))
                ve.tensor_scalar(slot_dst[:, :], token, -1.0, None, ALU.add).then_inc(map_ready, 1)
                dve.wait_ge(gap_exp, 1)
                step(ve.tensor_scalar(gap[:, 2, :], gap[:, 1, :], 1.0, None, ALU.add))
                step(ve.reciprocal(weight[:, 0, :], gap[:, 2, :]))
                step(ve.tensor_tensor(weight[:, 1, :], gap[:, 1, :], weight[:, 0, :], ALU.mult))
                step(ve.tensor_tensor(weight[:, :, :], weight[:, :, :], keep[:, :, :], ALU.mult))

            def experts():
                dve.wait_ge(bias_loaded, 16 * (1 + EXPERTS))

                def split_weights(e, u):
                    dve.wait_ge(raw_loaded, 48 * e + 48)
                    dve.wait_ge(fc_high, e + 1)
                    ve.tensor_tensor(fc_lo[:, u, :, :], raw_fc, f(fc_hi[:, u, :, :]), ALU.subtract
                                     ).then_inc(raw_split, 1)

                def split_x(e, c):
                    t0, nt = CHUNKS[c]
                    hl = slice(REST, 128)
                    for m in range(t0 // 2, (t0 + nt) // 2):
                        tok = slice(128 * (2 * m - t0), 128 * (2 * m - t0) + 256)
                        dve.wait_ge(ex_whole, e * (CAP_TILES // 2) + m + 1)
                        ve.tensor_copy(x_hi[:, :, tok], x_full[:, :, :]).then_inc(ex_high, 1)
                        dve.wait_ge(ex_high, e * (CAP_TILES // 2) + m + 1)
                        ve.tensor_tensor(x_lo[:, tok], x_full[:, 0, :], f(x_hi[:, 0, tok]), ALU.subtract)
                        ve.tensor_tensor(x_hi[hl, 1, tok], x_full[hl, 1, :], f(x_hi[hl, 1, tok]),
                                         ALU.subtract).then_inc(ex_turn_free[m % 2], 1)

                def add_bias(e, c):
                    t0, nt = CHUNKS[c]
                    for t in range(t0, t0 + nt):
                        i, n = y_place(e, t)
                        dve.wait_ge(y_full[i], n + 1)
                        o = t % OUT_RING
                        if not (isinstance(e, int) and e == 0 and t < OUT_RING):
                            dve.wait_ge(y_stored[o], e * (16 * CAP_TILES // OUT_RING) + 16 * (t // OUT_RING))
                        ve.tensor_tensor(slot_y[:, o, :], ps_y[i][:, 0:HID], pj_bias[:, e, :], ALU.add
                                         ).then_inc(y_free[i], 1)

                def expert(e, u, more):
                    split_x(e, 1)
                    add_bias(e, 0)
                    if more:
                        split_weights(e + 1, 1 - u)
                    split_x(e, 2)
                    add_bias(e, 1)
                    if more:
                        split_x(e + 1, 0)
                    add_bias(e, 2)

                split_weights(0, 0)
                split_x(0, 0)
                expert(0, 0, True)
                expert(1, 1, True)
                with dve.Fori(1, EXPERTS // 2 - 1, 1) as r:
                    expert(r * 2, 0, True)
                    expert(r * 2 + 1, 1, True)
                expert(EXPERTS - 2, 0, True)
                expert(EXPERTS - 1, 1, False)

            def combine():
                for t in range(SEQS + 1):
                    if t < SEQS:
                        q, at = divmod(t, TAKE_TILES)
                        dve.wait_ge(rows_taken[q % TAKE_RING], 16 * TOPK * (q // TAKE_RING + 1))
                        ve.scalar_tensor_tensor(out=resid[:, t, :], in0=taken[:, q % TAKE_RING, 0, at, :],
                                                scalar=weight[:, 0, t:t + 1], in1=resid[:, t, :],
                                                op0=ALU.mult, op1=ALU.add).then_inc(first_added, 1)
                    if t > 0:
                        b = t - 1
                        q, at = divmod(b, TAKE_TILES)
                        dve.wait_ge(first_added, b + 1)
                        ve.scalar_tensor_tensor(out=resid[:, b, :], in0=taken[:, q % TAKE_RING, 1, at, :],
                                                scalar=weight[:, 1, b:b + 1], in1=resid[:, b, :],
                                                op0=ALU.mult, op1=ALU.add).then_inc(token_done, 1)

            dve.sem_inc(raw_split, 1)
            dve.sem_inc(mag.max_done, 2)
            dve.sem_inc(mag.named("emb_affine0"), 1)
            dve.sem_inc(z_used, 2)
            dve.sem_inc(z_kept, 2)
            dve.wait_ge(ident_ready, 1)
            dve.wait_ge(const_loaded, CONST)
            split_weights_low(mag_w_loaded, mag_w_high, mag_w_split, 3)
            dve.wait_ge(mag_w_split, 2)
            negate_imaginary_keys()
            one_pass(lead, -1)
            one_pass(mag_first, 0)
            with dve.Fori(1, GROUPS - 1, 1) as g:
                one_pass(mag_loop, g)
            one_pass(mag_last, GROUPS - 1)
            one_pass(bridge, 0)
            dve.wait_ge(mag.ctx_done, SEQS)
            with dve.Fori(1, GROUPS - 1, 1) as g:
                one_pass(cau_loop, g)
            one_pass(cau_last, GROUPS - 1)
            one_pass(tail, GROUPS)
            route_tokens()
            experts()
            combine()

        return nc


def kernel(**inputs):
    import numpy as np
    import concourse.bacc as bacc
    from concourse.bass_utils import run_bass_kernel_spmd

    g = lambda name: np.asarray(inputs[name])
    tok, attn, ffn = "L0_tok_", "L0_attn_", "L0_ffn_"

    def by_head(a):
        return a.reshape(HID, HEADS, HEAD_DIM)

    wqr, wqi, wkr, wki, wv = (g(attn + n).T for n in ("Wqr", "Wqi", "Wkr", "Wki", "Wv"))
    pair = lambda a, b: np.concatenate([by_head(a), by_head(b)], axis=2).reshape(HID, 384)
    mag_qk = np.stack([pair(wqr, wqi), pair(wkr, wki), pair(wki, wkr)], axis=1)
    qkv_w, qkv_b = g(ffn + "attn_qkv_w"), g(ffn + "attn_qkv_b")
    pad = lambda a: np.concatenate(
        [a.reshape(-1, HEADS, HEAD_DIM), np.zeros((a.size // HID, HEADS, HEAD_DIM), a.dtype)], axis=2).reshape(-1, 384)
    causal_qk = np.stack([pad(qkv_w[:, 0:HID]), pad(qkv_w[:, HID:2 * HID])], axis=1)
    causal_qk_b = np.concatenate([pad(qkv_b[0:HID]), pad(qkv_b[HID:2 * HID])]).reshape(6, 128).T
    chunks = lambda a: np.stack([a[0:128], np.concatenate([a[128:], a[128:]])], axis=1)
    ln_cols = np.concatenate([chunks(g(ffn + n)) for n in ("ln1_w", "ln1_b", "ln2_w", "ln2_b")], axis=1)
    arrays = {
        "ids": np.stack([g("x"), g("itok_BS_0_4999"), g("pos_BS")]).transpose(2, 0, 1),
        "kinds": np.stack([g("mask_BS_i0_1").reshape(-1)] * 2),
        "word_table": g(tok + "word_table"),
        "domain_table": g(tok + "domain_table"),
        "pos_table": g(tok + "pos_table"),
        "kind_rows": np.concatenate([g(tok + "type_table"), g(tok + "proj_b")[None]]),
        "domain_w": g(tok + "proj_w").T,
        "mag_qk": mag_qk,
        "mag_v": wv,
        "causal_qk": causal_qk,
        "causal_qk_b": causal_qk_b,
        "causal_v": qkv_w[:, 2 * HID:],
        "ln_cols": ln_cols,
        "rows": np.stack([g(tok + "ln_gamma"), g(tok + "ln_beta"), qkv_b[2 * HID:], g(ffn + "attn_proj_b")]),
        "out_w": g(ffn + "attn_proj_w"),
        "gate_w": g(ffn + "w_g"),
        "fc_w": g(ffn + "exp_fc_w"),
        "fc_b": g(ffn + "exp_fc_b").reshape(EXPERTS, FF_CHUNKS, 128).transpose(2, 0, 1),
        "pj_w": g(ffn + "exp_proj_w"),
        "pj_b": g(ffn + "exp_proj_b").reshape(EXPERTS, HID),
    }
    arrays = {name: np.ascontiguousarray(a) for name, a in arrays.items()}
    nc = bacc.Bacc("TRN2", target_bir_lowering=False, num_devices=1)
    args = [nc.dram_tensor(name, list(a.shape), mybir.dt.from_np(a.dtype), kind="ExternalInput").ap()
            for name, a in arrays.items()]
    out = nc.dram_tensor("out", [SEQS, SEQ, HID], F32, kind="ExternalOutput").ap()
    tower_kernel(nc, *args, out)
    r = run_bass_kernel_spmd(nc, [arrays], core_ids=[0])
    return r.results[0]["out"]
```
